# Optimizing a Trainium2 kernel written in Bass

```python
import numpy as np
import jax
import jax.numpy as jnp

def _softmax(x, axis=-1):
    return jax.nn.softmax(x, axis=axis)

def _gelu(x):
    return jax.nn.gelu(x, approximate=True)

def _silu(x):
    return jax.nn.silu(x)

def _sigmoid(x):
    return jax.nn.sigmoid(x)

def _layernorm(x, axis=-1, eps=1e-05):
    m = jnp.mean(x, axis=axis, keepdims=True)
    v = jnp.var(x, axis=axis, keepdims=True)
    return (x - m) / jnp.sqrt(v + eps)

def _scatter_add(tgt, idx, src, axis=0):
    return tgt.at[idx].add(src)

def _segment_sum(src, seg, n):
    return jax.ops.segment_sum(src, seg, n)
kernel_name = 'mk_audio_tower_d2_tok_audfeat1024_r4_d8234e'

def setup_inputs(seed: int=0):
    np.random.seed(seed)
    _w = jnp.asarray

    def _rec_inputs():
        import jax
        import jax.numpy as jnp
        _rk = jax.random.key(seed)
        x = -0.000494162 + 1.00033 * jax.random.normal(jax.random.fold_in(_rk, 1), (64, 1, 750), jnp.float32)
        return x
    x = _rec_inputs()

    def _L0_tok_setup():
        import jax, jax.numpy as jnp
        import numpy as np
        from jax import lax
        B, C_IN, L = (8, 1, 120000)
        DIMS, HEAD = (256, 16)
        HEAD_DIM = DIMS // HEAD
        GROUPS = DIMS // 8

        def _conv1d(x, w, b, stride, pad, groups=1):
            y = lax.conv_general_dilated(x, w, window_strides=(stride,), padding=[(pad, pad)], dimension_numbers=('NCH', 'OIH', 'NCH'), feature_group_count=groups)
            return y + b[None, :, None]

        def _gelu(v):
            return jax.nn.gelu(v, approximate=False)
        key = jax.random.key(seed)
        ks = jax.random.split(key, 12)
        s = 0.02
        inp = {'x': jax.random.normal(ks[0], (B, C_IN, L), dtype=jnp.float32), 'w1': jax.random.normal(ks[1], (DIMS // 8, C_IN, 15), dtype=jnp.float32) * s, 'b1': jnp.zeros((DIMS // 8,), dtype=jnp.float32), 'w2': jax.random.normal(ks[2], (DIMS // 4, DIMS // 8, 7), dtype=jnp.float32) * s, 'b2': jnp.zeros((DIMS // 4,), dtype=jnp.float32), 'w3': jax.random.normal(ks[3], (DIMS, DIMS // 4, 9), dtype=jnp.float32) * s, 'b3': jnp.zeros((DIMS,), dtype=jnp.float32), 'w4': jax.random.normal(ks[4], (DIMS, DIMS // GROUPS, 3), dtype=jnp.float32) * s, 'b4': jnp.zeros((DIMS,), dtype=jnp.float32), 'w5': jax.random.normal(ks[5], (DIMS, DIMS, 1), dtype=jnp.float32) * s, 'b5': jnp.zeros((DIMS,), dtype=jnp.float32), 'rope_freqs': 1.0 / 50.0 ** (jnp.arange(0, HEAD_DIM, 2, dtype=jnp.float32) / HEAD_DIM), 'norm_w': jnp.ones((DIMS,), dtype=jnp.float32)}
        return inp
    _L0_tok_all = _L0_tok_setup()
    _L0_tok_in = {k: v for k, v in _L0_tok_all.items() if k in ('w1', 'b1', 'w2', 'b2', 'w3', 'b3', 'w4', 'b4', 'w5', 'b5', 'rope_freqs', 'norm_w')}
    del _L0_tok_all

    def _L0_attn_setup():
        import math
        import jax, jax.numpy as jnp
        import numpy as np
        N_EMBD = 256
        N_HEAD = 16
        N_QUERY_SETS = 4
        B, T = (8, 256)
        key = jax.random.key(seed)
        kx, kw1, kw2 = jax.random.split(key, 3)
        C = N_EMBD
        x = jax.random.normal(kx, (B, T, C), dtype=jnp.float32)
        W_attn = jax.random.normal(kw1, ((N_QUERY_SETS + 2) * C, C), dtype=jnp.float32) * (1.0 / math.sqrt(C))
        W_proj = jax.random.normal(kw2, (C, N_QUERY_SETS * C), dtype=jnp.float32) * (1.0 / math.sqrt(N_QUERY_SETS * C))
        return {'x': x, 'W_attn': W_attn, 'W_proj': W_proj}
    _L0_attn_all = _L0_attn_setup()
    _L0_attn_in = {k: v for k, v in _L0_attn_all.items() if k in ('W_attn', 'W_proj')}
    del _L0_attn_all

    def _L0_ffn_setup():
        import jax, jax.numpy as jnp
        import numpy as np
        import math
        D_MODEL = 256
        N_EXPERTS = 16
        D_FF = 1024
        CAP_FACTOR = 1.25
        MIN_CAPACITY = 4

        def _capacity(num_tokens, num_experts):
            cap = math.floor(CAP_FACTOR * num_tokens / num_experts)
            cap += cap % 2
            return max(cap, MIN_CAPACITY)

        def _top1_router(gate_logits, capacity):
            s, e = gate_logits.shape
            probs = jax.nn.softmax(gate_logits, axis=-1)
            top1 = jnp.argmax(gate_logits, axis=-1)
            mask = jax.nn.one_hot(top1, e, dtype=jnp.int32)
            ranks = jnp.cumsum(mask, axis=0) - 1
            mask = mask * (ranks < capacity).astype(jnp.int32)
            rank1 = jnp.sum(mask * ranks, axis=-1)
            ranks_oh = jax.nn.one_hot(rank1, capacity, dtype=probs.dtype)
            weight = mask.astype(probs.dtype) * probs
            combine_weights = weight[:, :, None] * ranks_oh[:, None, :]
            sec_mask = combine_weights > 0
            return (combine_weights, sec_mask)
        key = jax.random.key(seed)
        k1, k2, k3, k4 = jax.random.split(key, 4)
        x = jax.random.normal(k1, (4, 512, D_MODEL), dtype=jnp.float32)
        gate_w = jax.random.normal(k2, (N_EXPERTS, D_MODEL), dtype=jnp.float32) * math.sqrt(0.1 / D_MODEL)
        w1 = jax.random.normal(k3, (N_EXPERTS, D_MODEL, D_FF), dtype=jnp.float32) * (1.0 / math.sqrt(D_MODEL))
        w2 = jax.random.normal(k4, (N_EXPERTS, D_FF, D_MODEL), dtype=jnp.float32) * (1.0 / math.sqrt(D_FF))
        return {'x': x, 'gate_w': gate_w, 'w1': w1, 'w2': w2}
    _L0_ffn_all = _L0_ffn_setup()
    _L0_ffn_in = {k: v for k, v in _L0_ffn_all.items() if k in ('gate_w', 'w1', 'w2')}
    del _L0_ffn_all

    def _L1_attn_setup():
        import jax, jax.numpy as jnp
        import numpy as np
        import math
        N_HEAD = 16
        HEAD_QKV = 256
        WM_DECAY_LENGTH = 512
        WM_DECAY_RATE = 1.0
        WM_ECHOIC = 16

        def decay_weight_matrix(n):
            dl = WM_DECAY_LENGTH - WM_ECHOIC + 1
            nums = jnp.linspace(0.0, 1.0, dl)
            decay_values = 1.0 - jnp.power(nums, 1.0 / (np.e * WM_DECAY_RATE))
            decay_values = jnp.concatenate([jnp.ones(WM_ECHOIC - 1), decay_values])
            decay_values = decay_values[:n]
            idx = jnp.arange(n)[:, None] - jnp.arange(n)[None, :]
            mat = decay_values[jnp.clip(idx, 0, n - 1)]
            return jnp.tril(mat).astype(jnp.float32)
        key = jax.random.key(seed)
        k1, k2, k3 = jax.random.split(key, 3)
        B, T, C = (2, 512, 256)
        x = jax.random.normal(k1, (B, T, C), dtype=jnp.float32)
        W_attn = jax.random.normal(k2, (C, 3 * HEAD_QKV), dtype=jnp.float32) * (1.0 / math.sqrt(C))
        W_proj = jax.random.normal(k3, (HEAD_QKV, C), dtype=jnp.float32) * (1.0 / math.sqrt(HEAD_QKV))
        return {'x': x, 'W_attn': W_attn, 'W_proj': W_proj}
    _L1_attn_all = _L1_attn_setup()
    _L1_attn_in = {k: v for k, v in _L1_attn_all.items() if k in ('W_attn', 'W_proj')}
    del _L1_attn_all

    def _L1_ffn_setup():
        import jax, jax.numpy as jnp
        import numpy as np
        N_EXPERTS = 8
        N_GROUP = 4
        TOPK_GROUP = 2
        TOP_K = 2
        HIDDEN = 256
        INTER = 512
        B, S = (1, 256)

        def _grouped_topk(scores):
            T, E = scores.shape
            per_group = E // N_GROUP
            group_scores = scores.reshape(T, N_GROUP, per_group).max(-1)
            _, gidx = jax.lax.top_k(group_scores, TOPK_GROUP)
            gmask = jnp.zeros((T, N_GROUP), scores.dtype).at[jnp.arange(T)[:, None], gidx].set(1.0)
            smask = jnp.repeat(gmask, per_group, axis=1)
            masked = jnp.where(smask > 0, scores, 0.0)
            topk_w, topk_ids = jax.lax.top_k(masked, TOP_K)
            topk_w = topk_w / topk_w.sum(-1, keepdims=True)
            return (topk_ids, topk_w)
        key = jax.random.key(seed)
        k1, k2, k3, k4 = jax.random.split(key, 4)
        return {'hidden_states': jax.random.normal(k1, (B, S, HIDDEN), jnp.float32), 'gate_w': jax.random.normal(k2, (N_EXPERTS, HIDDEN), jnp.float32) * 0.02, 'w13_weight': jax.random.normal(k3, (N_EXPERTS, 2 * INTER, HIDDEN), jnp.float32) * 0.02, 'w2_weight': jax.random.normal(k4, (N_EXPERTS, HIDDEN, INTER), jnp.float32) * 0.02}
    _L1_ffn_all = _L1_ffn_setup()
    _L1_ffn_in = {k: v for k, v in _L1_ffn_all.items() if k in ('gate_w', 'w13_weight', 'w2_weight')}
    del _L1_ffn_all
    return {'x': x, 'L0_tok_w1': _L0_tok_in['w1'], 'L0_tok_b1': _L0_tok_in['b1'], 'L0_tok_w2': _L0_tok_in['w2'], 'L0_tok_b2': _L0_tok_in['b2'], 'L0_tok_w3': _L0_tok_in['w3'], 'L0_tok_b3': _L0_tok_in['b3'], 'L0_tok_w4': _L0_tok_in['w4'], 'L0_tok_b4': _L0_tok_in['b4'], 'L0_tok_w5': _L0_tok_in['w5'], 'L0_tok_b5': _L0_tok_in['b5'], 'L0_tok_rope_freqs': _L0_tok_in['rope_freqs'], 'L0_tok_norm_w': _L0_tok_in['norm_w'], 'L0_attn_W_attn': _L0_attn_in['W_attn'], 'L0_attn_W_proj': _L0_attn_in['W_proj'], 'L0_ffn_gate_w': _L0_ffn_in['gate_w'], 'L0_ffn_w1': _L0_ffn_in['w1'], 'L0_ffn_w2': _L0_ffn_in['w2'], 'L1_attn_W_attn': _L1_attn_in['W_attn'], 'L1_attn_W_proj': _L1_attn_in['W_proj'], 'L1_ffn_gate_w': _L1_ffn_in['gate_w'], 'L1_ffn_w13_weight': _L1_ffn_in['w13_weight'], 'L1_ffn_w2_weight': _L1_ffn_in['w2_weight']}

def reference(x, L0_tok_w1, L0_tok_b1, L0_tok_w2, L0_tok_b2, L0_tok_w3, L0_tok_b3, L0_tok_w4, L0_tok_b4, L0_tok_w5, L0_tok_b5, L0_tok_rope_freqs, L0_tok_norm_w, L0_attn_W_attn, L0_attn_W_proj, L0_ffn_gate_w, L0_ffn_w1, L0_ffn_w2, L1_attn_W_attn, L1_attn_W_proj, L1_ffn_gate_w, L1_ffn_w13_weight, L1_ffn_w2_weight):
    import jax
    import jax.numpy as jnp

    def _L0_tok_ref(x, w1, b1, w2, b2, w3, b3, w4, b4, w5, b5, rope_freqs, norm_w):
        import jax, jax.numpy as jnp
        import numpy as np
        from jax import lax
        B, C_IN, L = (8, 1, 120000)
        DIMS, HEAD = (256, 16)
        HEAD_DIM = DIMS // HEAD
        GROUPS = DIMS // 8

        def _conv1d(x, w, b, stride, pad, groups=1):
            y = lax.conv_general_dilated(x, w, window_strides=(stride,), padding=[(pad, pad)], dimension_numbers=('NCH', 'OIH', 'NCH'), feature_group_count=groups)
            return y + b[None, :, None]

        def _gelu(v):
            return jax.nn.gelu(v, approximate=False)
        h = _gelu(_conv1d(x, w1, b1, stride=8, pad=7))
        h = _gelu(_conv1d(h, w2, b2, stride=4, pad=3))
        h = _gelu(_conv1d(h, w3, b3, stride=5, pad=4))
        h = _gelu(_conv1d(h, w4, b4, stride=1, pad=1, groups=GROUPS))
        h = _gelu(_conv1d(h, w5, b5, stride=1, pad=0))
        h = jnp.transpose(h, (0, 2, 1))
        Bb, T, D = h.shape
        xh = h.reshape(Bb, T, HEAD, HEAD_DIM).transpose(0, 2, 1, 3)
        t = jnp.arange(T, dtype=jnp.float32)
        ang = t[:, None] * rope_freqs[None, :]
        cos, sin = (jnp.cos(ang), jnp.sin(ang))
        xp = xh.reshape(Bb, HEAD, T, HEAD_DIM // 2, 2)
        xr, xi = (xp[..., 0], xp[..., 1])
        out_r = xr * cos - xi * sin
        out_i = xr * sin + xi * cos
        xh = jnp.stack([out_r, out_i], axis=-1).reshape(Bb, HEAD, T, HEAD_DIM)
        h = xh.transpose(0, 2, 1, 3).reshape(Bb, T, D)
        ms = jnp.mean(h * h, axis=-1, keepdims=True)
        return h * jax.lax.rsqrt(ms + 1e-08) * norm_w

    def _L0_attn_ref(x, W_attn, W_proj):
        import math
        import jax, jax.numpy as jnp
        import numpy as np
        N_EMBD = 256
        N_HEAD = 16
        N_QUERY_SETS = 4
        B, T = (8, 256)
        Bz, Tz, C = x.shape
        hd = C // N_HEAD
        scale = 1.0 / math.sqrt(hd)
        qkv = x @ W_attn.T
        parts = jnp.split(qkv, N_QUERY_SETS + 2, axis=-1)
        k = parts[-2].reshape(Bz, Tz, N_HEAD, hd).transpose(0, 2, 1, 3)
        v = parts[-1].reshape(Bz, Tz, N_HEAD, hd).transpose(0, 2, 1, 3)
        causal = jnp.tril(jnp.ones((Tz, Tz), dtype=bool))
        outs = []
        for g in range(N_QUERY_SETS):
            q = parts[g].reshape(Bz, Tz, N_HEAD, hd).transpose(0, 2, 1, 3)
            att = jnp.einsum('bhqd,bhkd->bhqk', q, k) * scale
            att = jnp.where(causal, att, -jnp.inf)
            att = jax.nn.softmax(att, axis=-1)
            y = jnp.einsum('bhqk,bhkd->bhqd', att, v)
            outs.append(y.transpose(0, 2, 1, 3).reshape(Bz, Tz, C))
        combined = jnp.concatenate(outs, axis=-1)
        return combined @ W_proj.T

    def _L0_ffn_ref(x, gate_w, w1, w2):
        import jax, jax.numpy as jnp
        import numpy as np
        import math
        D_MODEL = 256
        N_EXPERTS = 16
        D_FF = 1024
        CAP_FACTOR = 1.25
        MIN_CAPACITY = 4

        def _capacity(num_tokens, num_experts):
            cap = math.floor(CAP_FACTOR * num_tokens / num_experts)
            cap += cap % 2
            return max(cap, MIN_CAPACITY)

        def _top1_router(gate_logits, capacity):
            s, e = gate_logits.shape
            probs = jax.nn.softmax(gate_logits, axis=-1)
            top1 = jnp.argmax(gate_logits, axis=-1)
            mask = jax.nn.one_hot(top1, e, dtype=jnp.int32)
            ranks = jnp.cumsum(mask, axis=0) - 1
            mask = mask * (ranks < capacity).astype(jnp.int32)
            rank1 = jnp.sum(mask * ranks, axis=-1)
            ranks_oh = jax.nn.one_hot(rank1, capacity, dtype=probs.dtype)
            weight = mask.astype(probs.dtype) * probs
            combine_weights = weight[:, :, None] * ranks_oh[:, None, :]
            sec_mask = combine_weights > 0
            return (combine_weights, sec_mask)
        tokens = x.reshape(-1, D_MODEL)
        s = tokens.shape[0]
        capacity = _capacity(s, N_EXPERTS)
        gate_logits = tokens.astype(jnp.float32) @ gate_w.T
        combine_weights, sec_mask = _top1_router(gate_logits, capacity)
        dispatch = jnp.einsum('sec,sd->ecd', sec_mask.astype(tokens.dtype), tokens)
        h = jax.nn.gelu(jnp.einsum('ecd,edf->ecf', dispatch, w1))
        expert_out = jnp.einsum('ecf,efd->ecd', h, w2)
        out = jnp.einsum('sec,ecd->sd', combine_weights.astype(tokens.dtype), expert_out)
        return out.reshape(x.shape)

    def _L1_attn_ref(x, W_attn, W_proj):
        import jax, jax.numpy as jnp
        import numpy as np
        import math
        N_HEAD = 16
        HEAD_QKV = 256
        WM_DECAY_LENGTH = 512
        WM_DECAY_RATE = 1.0
        WM_ECHOIC = 16

        def decay_weight_matrix(n):
            dl = WM_DECAY_LENGTH - WM_ECHOIC + 1
            nums = jnp.linspace(0.0, 1.0, dl)
            decay_values = 1.0 - jnp.power(nums, 1.0 / (np.e * WM_DECAY_RATE))
            decay_values = jnp.concatenate([jnp.ones(WM_ECHOIC - 1), decay_values])
            decay_values = decay_values[:n]
            idx = jnp.arange(n)[:, None] - jnp.arange(n)[None, :]
            mat = decay_values[jnp.clip(idx, 0, n - 1)]
            return jnp.tril(mat).astype(jnp.float32)
        B, T, C = x.shape
        hd = HEAD_QKV // N_HEAD
        qkv = x @ W_attn
        q, k, v = jnp.split(qkv, 3, axis=-1)
        q = q.reshape(B, T, N_HEAD, hd).transpose(0, 2, 1, 3)
        k = k.reshape(B, T, N_HEAD, hd).transpose(0, 2, 1, 3)
        v = v.reshape(B, T, N_HEAD, hd).transpose(0, 2, 1, 3)
        att = jnp.einsum('bhqd,bhkd->bhqk', q, k) * (1.0 / math.sqrt(hd))
        causal = jnp.tril(jnp.ones((T, T), dtype=bool))
        att = jnp.where(causal, att, -jnp.inf)
        att = jax.nn.softmax(att, axis=-1)
        att = att * decay_weight_matrix(T)
        y = jnp.einsum('bhqk,bhkd->bhqd', att, v)
        y = y.transpose(0, 2, 1, 3).reshape(B, T, HEAD_QKV)
        return y @ W_proj

    def _L1_ffn_ref(hidden_states, gate_w, w13_weight, w2_weight):
        import jax, jax.numpy as jnp
        import numpy as np
        N_EXPERTS = 8
        N_GROUP = 4
        TOPK_GROUP = 2
        TOP_K = 2
        HIDDEN = 256
        INTER = 512
        B, S = (1, 256)

        def _grouped_topk(scores):
            T, E = scores.shape
            per_group = E // N_GROUP
            group_scores = scores.reshape(T, N_GROUP, per_group).max(-1)
            _, gidx = jax.lax.top_k(group_scores, TOPK_GROUP)
            gmask = jnp.zeros((T, N_GROUP), scores.dtype).at[jnp.arange(T)[:, None], gidx].set(1.0)
            smask = jnp.repeat(gmask, per_group, axis=1)
            masked = jnp.where(smask > 0, scores, 0.0)
            topk_w, topk_ids = jax.lax.top_k(masked, TOP_K)
            topk_w = topk_w / topk_w.sum(-1, keepdims=True)
            return (topk_ids, topk_w)
        Bm, Sm, H = hidden_states.shape
        x = hidden_states.reshape(-1, H)
        T = x.shape[0]
        scores = jax.nn.softmax(x @ gate_w.T, axis=-1)
        topk_ids, topk_w = _grouped_topk(scores)
        combine = jnp.zeros((T, N_EXPERTS), x.dtype).at[jnp.arange(T)[:, None], topk_ids].add(topk_w)
        gu = jnp.einsum('th,eih->tei', x, w13_weight)
        gate, up = (gu[..., :INTER], gu[..., INTER:])
        act = jax.nn.silu(gate) * up
        act = act * combine[:, :, None]
        out = jnp.einsum('tei,ehi->th', act, w2_weight)
        return out.reshape(Bm, Sm, H)
    h = _L0_tok_ref(x, L0_tok_w1, L0_tok_b1, L0_tok_w2, L0_tok_b2, L0_tok_w3, L0_tok_b3, L0_tok_w4, L0_tok_b4, L0_tok_w5, L0_tok_b5, L0_tok_rope_freqs, L0_tok_norm_w)
    h = h + _L0_attn_ref(_layernorm(h, axis=-1), L0_attn_W_attn, L0_attn_W_proj)
    h = h + _L0_ffn_ref(_layernorm(h, axis=-1), L0_ffn_gate_w, L0_ffn_w1, L0_ffn_w2)
    h = h + _L1_attn_ref(_layernorm(h, axis=-1), L1_attn_W_attn, L1_attn_W_proj)
    h = h + _L1_ffn_ref(_layernorm(h, axis=-1), L1_ffn_gate_w, L1_ffn_w13_weight, L1_ffn_w2_weight)
    return h

_drawn_inputs = setup_inputs


def setup_inputs(seed=0):
    import zlib

    import numpy as np

    out = dict(_drawn_inputs(seed))
    spreads = {'L0_tok_b1': (0.0, 0.8),
     'L0_tok_b2': (0.0, 0.8),
     'L0_tok_b3': (0.0, 0.8),
     'L0_tok_b4': (0.0, 0.1),
     'L0_tok_b5': (0.0, 0.1),
     'L0_tok_norm_w': (1.0, 0.2)}
    factors = {'x': 8.0,
     'L0_tok_w1': 8.0,
     'L0_tok_w2': 8.0,
     'L0_tok_w3': 8.0,
     'L0_tok_w4': 6.607,
     'L1_ffn_gate_w': 4.695,
     'L1_ffn_w13_weight': 5.173,
     'L1_ffn_w2_weight': 4.998}
    for name, (base, spread) in spreads.items():
        noise = np.random.default_rng([zlib.crc32(name.encode()), seed]).standard_normal(out[name].shape)
        drawn = base * np.exp(spread * noise) if base else spread * noise
        out[name] = jnp.asarray(drawn.astype(out[name].dtype))
    for name, factor in factors.items():
        out[name] = (out[name] * factor).astype(out[name].dtype)
    return out
```

```python
import math
from contextlib import ExitStack

import numpy as np

import concourse.bass as bass
from concourse import mybir

P = 128
B, T = 64, 5
N = B * T
NP = 384
NT = NP // P
D = 256
C1, C2 = 32, 64
G1 = 24
TAPS = 39
POS1 = 94
M2 = 12
HEADS, HD = 16, 16
SETS = 4
E0, F0, CAP = 16, 1024, 26
SLOT = 32
E1, F1 = 8, 512
PAIRS = T * (T + 1) // 2
OFF = [sum(T - i for i in range(d)) for d in range(T)]
LN_EPS, RMS_EPS = 1e-5, 1e-8
SCALE = 1.0 / math.sqrt(HD)
TWO_PI_HI, TWO_PI_LO = 6.28125, 2 * math.pi - 6.28125
ROUND = 1.5 * 2.0 ** 23
FAR = 4096.0

W0_COLS = 2 * F0 + (F0 // P) * D
W1_COLS = 2 * 2 * F1 + (F1 // P) * D
RING = 8

CB1, CB2, CB3, CB4, CB5, CNW, CFR, NVEC = 0, 1, 2, 4, 6, 8, 10, 11
K_ID, K_IND, K_REV16, K_E32, K_REV8, K_REV4, K_SLOT, K_KEY, K_T = 0, 128, 256, 272, 288, 296, 300, 304, 307
NCONST = 312


def audio_tower(nc: bass.Bass, a: dict, out: bass.AP):
    f32, bf16 = mybir.dt.float32, mybir.dt.bfloat16
    ALU, ACT, AX = mybir.AluOpType, mybir.ActivationFunctionType, mybir.AxisListType

    with ExitStack() as ctx:
        def sb(name, cols, dt=f32):
            return ctx.enter_context(nc.sbuf_tensor(name, [P, cols], dt))

        def sem(name):
            return ctx.enter_context(nc.semaphore(name))

        bank = [ctx.enter_context(nc.psum_tensor(f"bank{i}", [P, 512], f32)) for i in range(8)]

        ring = sb("ring", RING * W0_COLS)
        vec = sb("vec", NVEC)
        const = sb("const", NCONST)
        w_conv12 = sb("w_conv12", P + 3 * P)
        w_qkv0 = sb("w_qkv0", 2 * 12 * P)
        w_proj0 = sb("w_proj0", 2 * SETS * D)
        w_qkv1 = sb("w_qkv1", 2 * 6 * P)
        w_proj1 = sb("w_proj1", 2 * D)
        w_gates = sb("w_gates", 2 * (E0 + E1))
        mean_w = sb("mean_w", P)
        slot_id = sb("slot_id", E0 * SLOT)
        key_row = sb("key_row", NP)
        before = sb("before", NT * NP, bf16)
        resid = sb("resid", 2 * NP)
        normed = sb("normed", 2 * NP)
        squares = sb("squares", 2 * NP)
        small = sb("small", 512)
        arena = sb("arena", 7936)

        def carve(t, at, *dims):
            n = 1
            for d in dims:
                n *= d
            v = t[:, at:at + n]
            if len(dims) == 1:
                return v
            names = [f"a{i}" for i in range(len(dims))]
            return v.rearrange(f"p ({' '.join(names)}) -> p {' '.join(names)}",
                               **{n: d for n, d in zip(names[1:], dims[1:])})

        resid_v, squares_v, normed_v = (carve(x, 0, 2, NP) for x in (resid, squares, normed))
        ident = const[:, K_ID:K_ID + P]
        lane_of = carve(const, K_IND, 2, 2, 32)

        borrowed6, borrowed7 = 6 * W0_COLS, 7 * W0_COLS
        w_conv3 = carve(ring, borrowed6, 10, D)
        w_conv4 = carve(ring, borrowed6 + 10 * D, 3, 2, P)
        w_conv5 = carve(ring, borrowed6 + 10 * D + 6 * P, 2, D)
        windows = arena[0:TAPS, 0:G1 * B]
        h1 = carve(arena, 1536, G1, B)
        h2 = carve(arena, 3072, M2, B)
        h3 = carve(arena, 3840, 2, N)
        h4 = carve(arena, 4480, 2, N)
        h5 = carve(arena, 5120, 2, N)
        turned = carve(arena, 5760, 2, N)
        crossed = carve(arena, 6400, 2, N)
        rope_sin = carve(arena, 7040, T)
        rope_cos = carve(arena, 7048, T)
        rope_a = carve(arena, 7056, T)
        rope_b = carve(arena, 7064, T)

        q = carve(arena, 0, 2, SETS, N)
        k = carve(arena, 2560, 2, N)
        values = carve(arena, 3840, 2, N)
        vx = carve(arena, 4480, 2, PAIRS, B)
        score = carve(arena, 6400, 480)
        prob = carve(arena, 6880, 480)
        peak = carve(arena, 7360, 160)
        total = carve(arena, 7520, 160)
        inv = carve(arena, 7680, 160)
        PRODS = 3
        prods = [carve(ring, borrowed7 + i * SETS * N, SETS, N) for i in range(PRODS)]
        lane_to = w_qkv0[:, 0:P * HD]
        weighted = [ring[:, borrowed7:borrowed7 + 3840], arena[:, 0:3840]]

        x_tok = carve(arena, 6720, NT, D)
        place = carve(w_proj0, 0, NT, E0 * SLOT)
        x_slot = carve(arena, 0, 2, E0 * SLOT)
        inner = [carve(arena, 1024 + i * F0, F0) for i in range(2)]
        inner_t = carve(arena, 3072, F0 // P, P)
        y_slot = carve(arena, 4096, 4, D)
        back = carve(arena, 5120, 4, N)
        weight_row = carve(arena, 6400, N)

        share = carve(arena, 0, E1, N)
        NG = 4
        gate_out = [carve(arena, 2560 + i * N, N) for i in range(NG)]
        up_gate = [carve(arena, 3840 + i * N, N) for i in range(NG)]
        act_in = [carve(arena, 5120 + i * N, N) for i in range(NG)]
        final_tok = carve(w_proj0, 0, NT, P, 2)

        ld_first, ld_const, ld_conv, ld_qkv0, ld_proj0, ld_gates, ld_qkv1, ld_proj1 = (
            sem(n) for n in ("ld_first", "ld_const", "ld_conv", "ld_qkv0", "ld_proj0", "ld_gates", "ld_qkv1", "ld_proj1"))
        ld_slot = [sem(f"ld_slot{i}") for i in range(RING)]
        stored = sem("stored")
        pads_set, iotas, lane_ready = sem("pads_set"), sem("iotas"), sem("lane_ready")
        conv_mm, conv_out = sem("conv_mm"), sem("conv_out")
        angle_ready, sincos_ready, rope_done = sem("angle_ready"), sem("sincos_ready"), sem("rope_done")
        resid_ready = sem("resid_ready")
        mean_mm, centred_ready, squares_ready, sums_mm = (sem(n) for n in ("mean_mm", "centred_ready", "squares_ready", "sums_mm"))
        var_ready, std_ready, rstd_ready, rstd_mm, normed_ready = (
            sem(n) for n in ("var_ready", "std_ready", "rstd_ready", "rstd_mm", "normed_ready"))
        qkv_mm = [sem(f"qkv_mm{l}") for l in range(2)]
        qkv_act = [sem(f"qkv_act{l}") for l in range(2)]
        qkv_dve = [sem(f"qkv_dve{l}") for l in range(2)]
        prod_ready = [sem(f"prod_ready{l}") for l in range(2)]
        score_mm = [sem(f"score_mm{l}") for l in range(2)]
        shifted_ready = [sem(f"shifted_ready{l}") for l in range(2)]
        exp_ready = [sem(f"exp_ready{l}") for l in range(2)]
        prob_ready = [sem(f"prob_ready{l}") for l in range(2)]
        vx_ready = [sem(f"vx_ready{l}") for l in range(2)]
        spread_mm = [sem(f"spread_mm{l}") for l in range(2)]
        weighted_ready = [sem(f"weighted_ready{l}") for l in range(2)]
        mixed_pool = [sem(f"mixed_pool{l}") for l in range(2)]
        mixed_dve = [sem(f"mixed_dve{l}") for l in range(2)]
        proj_mm = [sem(f"proj_mm{l}") for l in range(2)]
        logit_mm = [sem(f"logit_mm{l}") for l in range(2)]
        lsub_ready = [sem(f"lsub_ready{l}") for l in range(2)]
        lexp_ready = [sem(f"lexp_ready{l}") for l in range(2)]
        xtok_mm, xtok_ready, onehot_ready, rank_mm, pos_ready, gatew_ready = (
            sem(n) for n in ("xtok_mm", "xtok_ready", "onehot_ready", "rank_mm", "pos_ready", "gatew_ready"))
        place_ready, xslot_mm, xslot_ready, row_mm, wrow_ready, back_ready = (
            sem(n) for n in ("place_ready", "xslot_mm", "xslot_ready", "row_mm", "wrow_ready", "back_ready"))
        ff1_mm, inner_ready, innert_mm, innert_ready, ff2_mm, yslot_ready, combine_mm = (
            sem(n) for n in ("ff1_mm", "inner_ready", "innert_mm", "innert_ready", "ff2_mm", "yslot_ready", "combine_mm"))
        comb_ready, share_mm, share_ready, gate_mm, silu_ready, upgate_ready, act_ready, down_mm = (
            sem(n) for n in ("comb_ready", "share_mm", "share_ready", "gate_mm", "silu_ready", "upgate_ready", "act_ready", "down_mm"))
        final_ready, final_mm, tok_ready = sem("final_ready"), sem("final_mm"), sem("tok_ready")
        dve_step, pool_step = sem("dve_step"), sem("pool_step")

        QKV_TILES = [12, 6]
        QKV_BY_DVE = [{1, 3}, {1}]

        def taken(l, i):
            by_dve = QKV_BY_DVE[l]
            if i in by_dve:
                return qkv_dve[l], len([x for x in by_dve if x <= i])
            return qkv_act[l], len([x for x in range(i + 1) if x not in by_dve])

        def qkv_dst(l, i):
            per = 1 + (SETS if l == 0 else 1)
            if i >= 2 * per:
                return values[:, i - 2 * per, :]
            r, j = divmod(i, per)
            return k[:, r, :] if j == 0 else q[:, r, j - 1, :]

        block = ctx.enter_context(nc.Block())

        @block.sync
        def _(sp):
            sp.dma_start(vec[:, :], a["vec"]).then_inc(ld_first, 16)
            sp.dma_start(w_conv12[:, :], a["w_conv12"]).then_inc(ld_first, 16)
            sp.dma_start(windows, a["windows"]).then_inc(ld_first, 16)
            sp.dma_start(const[:, :], a["const"]).then_inc(ld_const, 16)
            sp.dma_start(ring[:, borrowed6:borrowed6 + 10 * D + 6 * P + 2 * D], a["w_conv345"]).then_inc(ld_conv, 16)
            sp.dma_start(w_qkv0[:, :], a["w_qkv0"]).then_inc(ld_qkv0, 16)
            sp.dma_start(w_proj0[:, :], a["w_proj0"]).then_inc(ld_proj0, 16)
            sp.dma_start(w_gates[:, :], a["w_gates"]).then_inc(ld_gates, 16)
            for e in range(E0):
                if e == 6:
                    sp.wait_ge(conv_mm, 11)
                if e == 7:
                    sp.wait_ge(proj_mm[0], 2)
                if e >= RING:
                    sp.wait_ge(ff2_mm, (e - RING) // 4 + 1)
                s = e % RING
                sp.dma_start(ring[:, s * W0_COLS:(s + 1) * W0_COLS], a["w_exp0"][e]).then_inc(ld_slot[s], 16)
                if e == RING - 1:
                    sp.dma_start(w_qkv1[:, :], a["w_qkv1"]).then_inc(ld_qkv1, 16)
                    sp.dma_start(w_proj1[:, :], a["w_proj1"]).then_inc(ld_proj1, 16)
            for e in range(E1):
                sp.wait_ge(ff2_mm, (e + RING) // 4 + 1)
                if e == 7:
                    sp.wait_ge(proj_mm[1], 2)
                sp.dma_start(ring[:, e * W0_COLS:e * W0_COLS + W1_COLS], a["w_exp1"][e]).then_inc(ld_slot[e], 16)
            for t in range(T):
                sp.wait_ge(tok_ready, t // 2 + 1)
                rows = slice(B * (t % 2), B * (t % 2) + B)
                sp.dma_start(out[:, t, :], final_tok[rows, t // 2, :, :].rearrange("b p r -> b (p r)")).then_inc(stored, 16)
            sp.wait_ge(stored, 16 * T)

        @block.gpsimd
        def _(pool):
            g = nc.gpsimd
            g.memset(mean_w[:, :], 1.0 / D).then_inc(pads_set, 1)
            g.memset(h1[:, G1 - 1, :], 0.0).then_inc(pads_set, 1)
            for v in (resid_v, squares_v, normed_v):
                g.memset(v[:, :, N:NP], 0.0).then_inc(pads_set, 1)
            g.iota(slot_id[:, :], [[1, E0 * SLOT]], base=1, channel_multiplier=0,
                   allow_small_or_imprecise_dtypes=True).then_inc(iotas, 1)
            g.iota(key_row[:, 0:N].rearrange("p (t b) -> p t b", b=B), [[1, T], [T, B]], base=0, channel_multiplier=0,
                   allow_small_or_imprecise_dtypes=True).then_inc(iotas, 1)
            g.memset(key_row[:, N:NP], FAR).then_inc(iotas, 1)

            pool.wait_ge(ld_const, 16)
            pool.wait_ge(qkv_mm[0], QKV_TILES[0])
            g.tensor_copy(lane_to.rearrange("p (l d) -> p l d", d=HD), ident.unsqueeze(2).to_broadcast([P, P, HD]))\
                .then_inc(lane_ready, 1)

            def attention(l, width):
                pool.wait_ge(qkv_act[l], QKV_TILES[l] - len(QKV_BY_DVE[l]))
                for d in range(T):
                    n = (T - d) * B
                    g.tensor_copy(vx[:, :, OFF[d]:OFF[d] + T - d, :].rearrange("p r s b -> p r (s b)"),
                                  values[:, :, 0:n]).then_inc(vx_ready[l], 1)
                pool.wait_ge(weighted_ready[l], 8 if l == 0 else 2)
                w = weighted[0].rearrange("p (c s) -> p c s", c=8)[:, :, :] if l == 0 else \
                    weighted[0][:, 0:960].rearrange("p (c s) -> p c s", c=8)
                for d in range(1, T):
                    dst = w[:, :, d * width:T * width]
                    g.tensor_tensor(dst, dst, w[:, :, OFF[d] * width:(OFF[d] + T - d) * width], ALU.add)\
                        .then_inc(mixed_pool[l], 1)
                    pool.wait_ge(mixed_pool[l], d)
            attention(0, 32)
            attention(1, 8)

        @block.scalar
        def _(act):
            s = nc.scalar
            act.wait_ge(ld_first, 48)
            act.wait_ge(angle_ready, 1)
            s.activation(rope_sin, rope_a, ACT.Sin).then_inc(sincos_ready, 1)
            s.activation(rope_cos, rope_b, ACT.Sin).then_inc(sincos_ready, 1)
            act.wait_ge(pads_set, 2)
            for c in range(3):
                act.wait_ge(conv_mm, c + 1)
                if c < 2:
                    s.activation(h1[:, 8 * c:8 * c + 8, :].rearrange("p g b -> p (g b)"), bank[c][:, :], ACT.Gelu,
                                 bias=vec[:, CB1:CB1 + 1]).then_inc(conv_out, 1)
                else:
                    s.activation(h1[:, 16:23, :].rearrange("p g b -> p (g b)"), bank[2][:, 0:7 * B], ACT.Gelu,
                                 bias=vec[:, CB1:CB1 + 1]).then_inc(conv_out, 1)
                    last = (POS1 - 4 * (G1 - 1)) * C1
                    s.activation(h1[0:last, 23, :], bank[2][0:last, 7 * B:8 * B], ACT.Gelu,
                                 bias=vec[0:last, CB1:CB1 + 1]).then_inc(conv_out, 1)
            for c in range(2):
                act.wait_ge(conv_mm, 4 + c)
                s.activation(h2[:, 6 * c:6 * c + 6, :].rearrange("p m b -> p (m b)"), bank[3 + c][:, 0:6 * B], ACT.Gelu,
                             bias=vec[:, CB2:CB2 + 1]).then_inc(conv_out, 1)
            for n, (dst, cb, banks) in enumerate(((h3, CB3, (5, 6)), (h4, CB4, (7, 0)), (h5, CB5, (1, 2)))):
                for r in range(2):
                    act.wait_ge(conv_mm, 6 + 2 * n + r)
                    s.activation(dst[:, r, :], bank[banks[r]][:, 0:N], ACT.Gelu,
                                 bias=vec[:, cb + r:cb + r + 1]).then_inc(conv_out, 1)

            def norm(i, src):
                if i == 0:
                    act.wait_ge(conv_out, 12)
                    act.wait_ge(pads_set, 5)
                else:
                    act.wait_ge(centred_ready, i)
                    act.wait_ge(rstd_mm, i)
                s.activation(squares_v[:, :, 0:N], src, ACT.Square).then_inc(squares_ready, 1)
                act.wait_ge(var_ready, i + 1)
                s.activation(small[:, 4:7], small[:, 0:3], ACT.Sqrt).then_inc(std_ready, 1)

            def attention(l):
                for i in range(QKV_TILES[l]):
                    if i in QKV_BY_DVE[l]:
                        continue
                    act.wait_ge(qkv_mm[l], i + 1)
                    s.activation(qkv_dst(l, i), bank[i % 8][:, 0:N], ACT.Copy).then_inc(qkv_act[l], 1)
                act.wait_ge(shifted_ready[l], T)
                n = 480 if l == 0 else 120
                s.activation(prob[:, 0:n], score[:, 0:n], ACT.Exp, scale=SCALE).then_inc(exp_ready[l], 1)

            def router(l, n):
                act.wait_ge(lsub_ready[l], 1)
                s.activation(small[:, 100:100 + NT * n], small[:, 40:40 + NT * n], ACT.Exp).then_inc(lexp_ready[l], 1)

            norm(0, h5)
            norm(1, normed_v[:, :, 0:N])
            attention(0)
            norm(2, normed_v[:, :, 0:N])
            act.wait_ge(xtok_mm, 1)
            s.activation(x_tok[:, 0:2, :].rearrange("p k f -> p (k f)"), bank[1][:, :], ACT.Copy).then_inc(xtok_ready, 1)
            s.activation(x_tok[:, 2, :], bank[2][:, 0:D], ACT.Copy).then_inc(xtok_ready, 1)
            router(0, E0)
            act.wait_ge(xslot_mm, 1)
            s.activation(x_slot[:, 0, :], bank[4][:, :], ACT.Copy).then_inc(xslot_ready, 1)
            act.wait_ge(row_mm, 2)
            s.activation(weight_row, bank[7][:, 0:N], ACT.Copy).then_inc(wrow_ready, 1)
            for e4 in range(E0 // 4):
                if e4 >= 2:
                    act.wait_ge(innert_mm, 2 * (e4 - 1))
                for c in range(2):
                    act.wait_ge(ff1_mm, 2 * e4 + c + 1)
                    s.activation(inner[e4 % 2][:, 512 * c:512 * c + 512], bank[2 * (e4 % 2) + c][:, :],
                                 ACT.Gelu_apprx_tanh).then_inc(inner_ready, 1)
                if e4 >= 1:
                    act.wait_ge(ff2_mm, e4)
                    s.activation(y_slot[:, e4 - 1, :], bank[6 + (e4 - 1) % 2][:, 0:D], ACT.Copy).then_inc(yslot_ready, 1)
            act.wait_ge(ff2_mm, 4)
            s.activation(y_slot[:, 3, :], bank[7][:, 0:D], ACT.Copy).then_inc(yslot_ready, 1)
            norm(3, normed_v[:, :, 0:N])
            attention(1)
            norm(4, normed_v[:, :, 0:N])
            router(1, E1)

            def silu(n):
                act.wait_ge(gate_mm, n + 1)
                if n >= NG:
                    act.wait_ge(upgate_ready, n - NG + 1)
                s.activation(gate_out[n % NG], bank[1 + 2 * (n % 2)][:, 0:N], ACT.Silu).then_inc(silu_ready, 1)
            silu(0)
            silu(1)
            for e in range(E1):
                act.wait_ge(share_mm, e + 1)
                s.activation(share[:, e, :], bank[5 * (e % 2)][:, 0:N], ACT.Copy).then_inc(share_ready, 1)
            for n in range(2, 4 * E1):
                silu(n)

        @block.vector
        def _(dve):
            v = nc.vector
            steps = [0]

            def then(ins):
                steps[0] += 1
                ins.then_inc(dve_step, 1)
                dve.wait_ge(dve_step, steps[0])

            dve.wait_ge(ld_first, 48)
            dve.wait_ge(ld_const, 16)
            angle, turns, low, over = (carve(small, 8 * i, T) for i in range(2, 6))
            PI = 3.1415925
            then(v.tensor_scalar(angle, const[:, K_T:K_T + T], vec[:, CFR:CFR + 1], None, ALU.mult))
            then(v.tensor_scalar(turns, angle, 1 / (2 * math.pi), ROUND, ALU.mult, ALU.add))
            then(v.tensor_scalar(turns, turns, -ROUND, None, ALU.add))
            then(v.scalar_tensor_tensor(out=low, in0=turns, scalar=-TWO_PI_HI, in1=angle, op0=ALU.mult, op1=ALU.add))
            then(v.scalar_tensor_tensor(out=low, in0=turns, scalar=-TWO_PI_LO, in1=low, op0=ALU.mult, op1=ALU.add))
            then(v.tensor_scalar(rope_a, low, PI, -PI, ALU.min, ALU.max))
            then(v.tensor_scalar(low, low, math.pi / 2, None, ALU.add))
            then(v.tensor_scalar(over, low, math.pi, -2 * math.pi, ALU.is_gt, ALU.mult))
            then(v.tensor_tensor(low, low, over, ALU.add))
            v.tensor_scalar(rope_b, low, PI, -PI, ALU.min, ALU.max).then_inc(angle_ready, 1)
            dve.wait_ge(iotas, 3)
            for j in range(NT):
                then(v.tensor_scalar(before[:, j * NP:(j + 1) * NP], key_row[:, :], const[:, K_KEY + j:K_KEY + j + 1], None,
                                     ALU.is_ge))

            dve.wait_ge(sincos_ready, 2)
            dve.wait_ge(conv_out, 12)

            def by_time(x):
                return x.unsqueeze(2).to_broadcast([P, T, B])
            h5t = h5.rearrange("p r (t b) -> p r t b", b=B)
            tt = turned.rearrange("p r (t b) -> p r t b", b=B)
            ct = crossed.rearrange("p r (t b) -> p r t b", b=B)
            for r in range(2):
                v.tensor_tensor(tt[:, r], h5t[:, r], by_time(rope_cos), ALU.mult)
                last = v.tensor_tensor(ct[:, r], h5t[:, 1 - r], by_time(rope_sin), ALU.mult)
            then(last)
            v.tensor_tensor(turned[:, 0, :], turned[:, 0, :], crossed[:, 0, :], ALU.subtract)
            then(v.tensor_tensor(turned[:, 1, :], turned[:, 1, :], crossed[:, 1, :], ALU.add))

            def stats(i, eps):
                dve.wait_ge(sums_mm, i + 1)
                v.tensor_scalar(small[:, 0:3], bank[6][:, 0:3], eps, None, ALU.add).then_inc(var_ready, 1)
                dve.wait_ge(std_ready, i + 1)
                v.reciprocal(small[:, 8:11], small[:, 4:7]).then_inc(rstd_ready, 1)
                dve.wait_ge(rstd_mm, i + 1)

            def centre(i):
                dve.wait_ge(mean_mm, i)
                if i > 1:
                    dve.wait_ge(squares_ready, i)
                mean = bank[5][:, 0:N].unsqueeze(1).to_broadcast([P, 2, N])
                v.tensor_tensor(normed_v[:, :, 0:N], resid_v[:, :, 0:N], mean, ALU.subtract).then_inc(centred_ready, 1)
                stats(i, LN_EPS)
                rstd = bank[7][:, 0:N].unsqueeze(1).to_broadcast([P, 2, N])
                v.tensor_tensor(normed_v[:, :, 0:N], normed_v[:, :, 0:N], rstd, ALU.mult).then_inc(normed_ready, 1)

            stats(0, RMS_EPS)
            for r in range(2):
                v.scalar_tensor_tensor(out=resid_v[:, r, 0:N], in0=turned[:, r, :], scalar=vec[:, CNW + r:CNW + r + 1],
                                       in1=bank[7][:, 0:N], op0=ALU.mult, op1=ALU.mult).then_inc(resid_ready, 1)
            centre(1)

            def attention(l):
                sets = SETS if l == 0 else 1
                w = 32 if l == 0 else 8
                n = PAIRS * w
                for i in sorted(QKV_BY_DVE[l]):
                    dve.wait_ge(qkv_mm[l], i + 1)
                    v.tensor_copy(qkv_dst(l, i), bank[i % 8][:, 0:N]).then_inc(qkv_dve[l], 1)
                m = 0
                for r in range(2):
                    for i in range(r * (1 + sets), (r + 1) * (1 + sets)):
                        dve.wait_ge(*taken(l, i))
                    for d in range(T):
                        cols = (T - d) * B
                        if m >= PRODS:
                            dve.wait_ge(score_mm[l], m - PRODS + 1)
                        v.tensor_tensor(prods[m % PRODS][:, 0:sets, 0:cols], q[:, r, 0:sets, d * B:N],
                                        k[:, r, 0:cols].unsqueeze(1).to_broadcast([P, sets, cols]), ALU.mult)\
                            .then_inc(prod_ready[l], 1)
                        m += 1
                dve.wait_ge(score_mm[l], 2 * T)
                s_ps = bank[4 if l == 0 else 6]
                blk = [slice(OFF[d] * w, (OFF[d] + T - d) * w) for d in range(T)]
                late = [slice(d * w, T * w) for d in range(T)]
                then(v.tensor_copy(peak[:, late[0]], s_ps[:, blk[0]]))
                for d in range(1, T):
                    then(v.tensor_tensor(peak[:, late[d]], s_ps[:, blk[d]], peak[:, late[d]], ALU.max))
                for d in range(T):
                    v.tensor_tensor(score[:, blk[d]], s_ps[:, blk[d]], peak[:, late[d]], ALU.subtract)\
                        .then_inc(shifted_ready[l], 1)
                dve.wait_ge(exp_ready[l], 1)
                then(v.tensor_copy(total[:, late[0]], prob[:, blk[0]]))
                for d in range(1, T):
                    then(v.tensor_tensor(total[:, late[d]], total[:, late[d]], prob[:, blk[d]], ALU.add))
                then(v.reciprocal(inv[:, 0:T * w], total[:, 0:T * w]))
                for d in range(T):
                    v.tensor_tensor(prob[:, blk[d]], prob[:, blk[d]], inv[:, late[d]], ALU.mult).then_inc(prob_ready[l], 1)
                dve.wait_ge(vx_ready[l], T)
                dve.wait_ge(score_mm[l], 2 * T)
                for c in range(16 if l == 0 else 4):
                    dve.wait_ge(spread_mm[l], c + 1)
                    if l == 0:
                        r, (st, half_b) = c // 8, divmod(c % 8, 2)
                        dst = weighted[r][:, (c % 8) * n:(c % 8 + 1) * n].rearrange("p (s b) -> p s b", b=w)
                        src = bank[c % 4][:, 0:n].rearrange("p (s b) -> p s b", b=w)
                        val = vx[:, r, :, half_b * w:(half_b + 1) * w]
                    else:
                        r, quad = divmod(c, 2)
                        dst = weighted[r][:, quad * 4 * n:(quad + 1) * 4 * n].rearrange("p (o s b) -> p o s b", o=4, b=w)
                        src = bank[c % 4][:, 0:4 * n].rearrange("p (o s b) -> p o s b", o=4, b=w)
                        val = vx[:, r, :, quad * 32:(quad + 1) * 32].rearrange("p s (o b) -> p o s b", b=w)
                    v.tensor_tensor(dst, src, val, ALU.mult).then_inc(weighted_ready[l], 1)
                dve.wait_ge(weighted_ready[l], 16 if l == 0 else 4)
                wt = weighted[1][:, 0:8 * n].rearrange("p (c s) -> p c s", c=8)
                for d in range(1, T):
                    v.tensor_tensor(wt[:, :, late[d]], wt[:, :, late[d]], wt[:, :, blk[d]], ALU.add).then_inc(mixed_dve[l], 1)
                    dve.wait_ge(mixed_dve[l], d)
                for r in range(2):
                    dve.wait_ge(proj_mm[l], r + 1)
                    v.tensor_tensor(resid_v[:, r, 0:N], bank[r + (5 if l == 0 else 0)][:, 0:N], resid_v[:, r, 0:N], ALU.add)\
                        .then_inc(resid_ready, 1)

            attention(0)
            centre(2)

            def over_experts(x, n):
                return x.unsqueeze(2).to_broadcast([P, NT, n])

            def first_max(src, top, hit, which, rev, n):
                then(v.tensor_reduce(out=top, in_=src, axis=AX.X, op=ALU.max))
                then(v.tensor_tensor(hit, src, over_experts(top, n), ALU.is_ge))
                then(v.tensor_tensor(hit, hit, rev.unsqueeze(1).to_broadcast([P, NT, n]), ALU.mult))
                then(v.tensor_reduce(out=which, in_=hit, axis=AX.X, op=ALU.max))
                then(v.tensor_tensor(hit, hit, over_experts(which, n), ALU.is_equal))

            top, which = carve(small, 12, NT), carve(small, 16, NT)
            lsub, hit, lexp = carve(small, 40, NT, E0), carve(small, 160, NT, E0), carve(small, 100, NT, E0)
            slotval, kept = carve(small, 220, NT, E0), carve(small, 280, NT, E0)
            hit16 = carve(small, 340, NT, E0)
            pos, gate_w, expsum = carve(small, 20, NT), carve(small, 24, NT), carve(small, 28, NT)
            onehot = hit16.bitcast(bf16)[:, :, 0:E0]
            logits = bank[0][:, 0:NT * E0].rearrange("p (k e) -> p k e", e=E0)
            dve.wait_ge(logit_mm[0], 1)
            then(v.tensor_reduce(out=top, in_=logits, axis=AX.X, op=ALU.max))
            v.tensor_tensor(lsub, logits, over_experts(top, E0), ALU.subtract).then_inc(lsub_ready[0], 1)
            dve.wait_ge(lsub_ready[0], 1)
            then(v.tensor_scalar(hit, lsub, 0.0, None, ALU.is_ge))
            then(v.tensor_tensor(hit, hit, const[:, K_REV16:K_REV16 + E0].unsqueeze(1).to_broadcast([P, NT, E0]), ALU.mult))
            then(v.tensor_reduce(out=which, in_=hit, axis=AX.X, op=ALU.max))
            then(v.tensor_tensor(hit, hit, over_experts(which, E0), ALU.is_equal))
            v.tensor_copy(onehot, hit).then_inc(onehot_ready, 1)
            rank = bank[3][:, 0:NT * E0].rearrange("p (k e) -> p k e", e=E0)
            dve.wait_ge(rank_mm, 1)
            then(v.scalar_tensor_tensor(out=kept, in0=rank, scalar=float(CAP), in1=hit, op0=ALU.is_le, op1=ALU.mult))
            then(v.tensor_tensor(slotval, rank, const[:, K_E32:K_E32 + E0].unsqueeze(1).to_broadcast([P, NT, E0]), ALU.add))
            then(v.tensor_tensor(slotval, slotval, kept, ALU.mult))
            v.tensor_reduce(out=pos, in_=slotval, axis=AX.X, op=ALU.add).then_inc(pos_ready, 1)
            dve.wait_ge(pos_ready, 1)
            for j in range(NT):
                v.tensor_scalar(place[:, j, :], slot_id[:, :], pos[:, j:j + 1], None, ALU.is_equal).then_inc(place_ready, 1)
            dve.wait_ge(lexp_ready[0], 1)
            then(v.tensor_reduce(out=expsum, in_=lexp, axis=AX.X, op=ALU.add))
            v.reciprocal(gate_w, expsum).then_inc(gatew_ready, 1)
            dve.wait_ge(xslot_mm, 2)
            v.tensor_copy(x_slot[:, 1, :], bank[5][:, :]).then_inc(xslot_ready, 1)
            dve.wait_ge(wrow_ready, 1)
            for j in range(4):
                v.scalar_tensor_tensor(out=back[:, j, :], in0=bank[6][:, 0:N], scalar=const[:, K_SLOT + j:K_SLOT + j + 1],
                                       in1=weight_row, op0=ALU.is_equal, op1=ALU.mult).then_inc(back_ready, 1)
            for e4 in range(E0 // 4):
                for c in range(2):
                    dve.wait_ge(innert_mm, 2 * e4 + c + 1)
                    if e4 >= 1:
                        dve.wait_ge(ff2_mm, e4)
                    v.tensor_copy(inner_t[:, 4 * c:4 * c + 4, :].rearrange("p k s -> p (k s)"), bank[4 + c][:, :])\
                        .then_inc(innert_ready, 1)
            for r in range(2):
                dve.wait_ge(combine_mm, r + 1)
                v.tensor_tensor(resid_v[:, r, 0:N], bank[r][:, 0:N], resid_v[:, r, 0:N], ALU.add).then_inc(resid_ready, 1)
            centre(3)
            attention(1)
            centre(4)

            lsub, lexp = carve(small, 40, NT, E1), carve(small, 100, NT, E1)
            probs, masked, masked2 = carve(small, 160, NT, E1), carve(small, 200, NT, E1), carve(small, 240, NT, E1)
            hit_a, hit_b = carve(small, 280, NT, E1), carve(small, 320, NT, E1)
            gscore, gscore2 = carve(small, 360, NT, 4), carve(small, 380, NT, 4)
            ghit_a, ghit_b = carve(small, 400, NT, 4), carve(small, 420, NT, 4)
            top2, comb = carve(small, 32, NT), carve(small, 440, NT, E1)
            rev8, rev4 = const[:, K_REV8:K_REV8 + E1], const[:, K_REV4:K_REV4 + 4]
            logits = bank[0][:, 0:NT * E1].rearrange("p (k e) -> p k e", e=E1)
            dve.wait_ge(logit_mm[1], 1)
            then(v.tensor_reduce(out=top, in_=logits, axis=AX.X, op=ALU.max))
            v.tensor_tensor(lsub, logits, over_experts(top, E1), ALU.subtract).then_inc(lsub_ready[1], 1)
            dve.wait_ge(lexp_ready[1], 1)
            then(v.tensor_reduce(out=expsum, in_=lexp, axis=AX.X, op=ALU.add))
            then(v.reciprocal(gate_w, expsum))
            then(v.tensor_tensor(probs, lexp, over_experts(gate_w, E1), ALU.mult))
            pair = probs.rearrange("p k (g j) -> p k g j", j=2)
            then(v.tensor_tensor(gscore, pair[:, :, :, 0], pair[:, :, :, 1], ALU.max))
            first_max(gscore, top, ghit_a, which, rev4, 4)
            then(v.scalar_tensor_tensor(out=gscore2, in0=ghit_a, scalar=-2.0, in1=gscore, op0=ALU.mult, op1=ALU.add))
            first_max(gscore2, top, ghit_b, which, rev4, 4)
            then(v.tensor_tensor(ghit_a, ghit_a, ghit_b, ALU.add))
            mp = masked.rearrange("p k (g j) -> p k g j", j=2)
            v.tensor_tensor(mp[:, :, :, 0], pair[:, :, :, 0], ghit_a, ALU.mult)
            then(v.tensor_tensor(mp[:, :, :, 1], pair[:, :, :, 1], ghit_a, ALU.mult))
            first_max(masked, top, hit_a, which, rev8, E1)
            then(v.scalar_tensor_tensor(out=masked2, in0=hit_a, scalar=-2.0, in1=masked, op0=ALU.mult, op1=ALU.add))
            first_max(masked2, top2, hit_b, which, rev8, E1)
            v.tensor_tensor(top, top, top2, ALU.add)
            then(v.tensor_tensor(hit_a, hit_a, hit_b, ALU.add))
            v.reciprocal(gate_w, top)
            then(v.tensor_tensor(masked, masked, hit_a, ALU.mult))
            v.tensor_tensor(comb, masked, over_experts(gate_w, E1), ALU.mult).then_inc(comb_ready, 1)
            for n in range(4 * E1):
                if n % 4 == 0:
                    dve.wait_ge(share_ready, n // 4 + 1)
                dve.wait_ge(silu_ready, n + 1)
                v.tensor_tensor(up_gate[n % NG], bank[2 + 2 * (n % 2)][:, 0:N], gate_out[n % NG], ALU.mult).then_inc(upgate_ready, 1)
                dve.wait_ge(upgate_ready, n + 1)
                if n >= NG:
                    dve.wait_ge(down_mm, n - NG + 1)
                v.tensor_tensor(act_in[n % NG], up_gate[n % NG], share[:, n // 4, :], ALU.mult).then_inc(act_ready, 1)
            dve.wait_ge(down_mm, 4 * E1)
            for r in range(2):
                v.tensor_tensor(normed_v[:, r, 0:N], bank[6 + r][:, 0:N], resid_v[:, r, 0:N], ALU.add).then_inc(final_ready, 1)
            for j in range(NT):
                dve.wait_ge(final_mm, j + 1)
                v.tensor_copy(final_tok[:, j, :, :].rearrange("t p r -> t r p"),
                              bank[j][:, 0:D].rearrange("t (r p) -> t r p", r=2)).then_inc(tok_ready, 1)

        @block.tensor
        def _(pe):
            def mm(o, w, x, start, stop, **kw):
                return nc.tensor.matmul(o, w, x, start=start, stop=stop, **kw)

            pe.wait_ge(ld_first, 48)
            for c in range(3):
                mm(bank[c][:, :], w_conv12[0:TAPS, 0:P], windows[:, 512 * c:512 * c + 512], True, True).then_inc(conv_mm, 1)
            pe.wait_ge(pads_set, 2)
            w2 = carve(w_conv12, P, 3, P)
            odd = h1.rearrange("p (m j) b -> p m j b", j=2)
            for c in range(2):
                pe.wait_ge(conv_out, 2 + 2 * c)
                o = bank[3 + c][:, 0:6 * B].rearrange("p (m b) -> p m b", b=B)
                m0 = 6 * c
                mm(o, w2[:, 1, :], odd[:, m0:m0 + 6, 0, :], True, False)
                if c == 0:
                    mm(o[:, 1:6, :], w2[:, 0, :], odd[:, 0:5, 1, :], False, False)
                else:
                    mm(o, w2[:, 0, :], odd[:, m0 - 1:m0 + 5, 1, :], False, False)
                mm(o, w2[:, 2, :], odd[:, m0:m0 + 6, 1, :], False, True).then_inc(conv_mm, 1)
            pe.wait_ge(ld_conv, 16)
            pe.wait_ge(conv_out, 6)
            for r in range(2):
                o = bank[5 + r][:, 0:N].rearrange("p (t b) -> p t b", b=B)
                jobs = []
                for odd_t in range(2):
                    for dd in (2, 3, 0, 1, 4) if not odd_t else range(5):
                        ts = [t for t in range(odd_t, T, 2) if 0 <= first_pair(t) + dd < M2]
                        jobs.append((odd_t, dd, ts))
                for n, (odd_t, dd, ts) in enumerate(jobs):
                    m0 = first_pair(ts[0]) + dd
                    last = m0 + T * (len(ts) - 1)
                    x = h2[:, m0:last + 1:T, :]
                    i = mm(o[:, ts[0]:ts[-1] + 1:2, :], w_conv3[:, 5 * odd_t + dd, r * P:(r + 1) * P], x,
                           n == 0, n == len(jobs) - 1, skip_group_check=True)
                i.then_inc(conv_mm, 1)
            pe.wait_ge(conv_out, 8)
            for r in range(2):
                o = bank[(7, 0)[r]]
                mm(o[:, 0:N], w_conv4[:, 1, r, :], h3[:, r, :], True, False)
                mm(o[:, B:N], w_conv4[:, 0, r, :], h3[:, r, 0:N - B], False, False)
                mm(o[:, 0:N - B], w_conv4[:, 2, r, :], h3[:, r, B:N], False, True).then_inc(conv_mm, 1)
            pe.wait_ge(conv_out, 10)
            for r in range(2):
                for kk in range(2):
                    i = mm(bank[1 + r][:, 0:N], w_conv5[:, kk, r * P:(r + 1) * P], h4[:, kk, :], kk == 0, kk == 1)
                i.then_inc(conv_mm, 1)

            def norm(i):
                if i > 0:
                    pe.wait_ge(resid_ready, 2 * i)
                    for kk in range(2):
                        x = mm(bank[5][:, 0:N], mean_w[:, :], resid_v[:, kk, 0:N], kk == 0, kk == 1)
                    x.then_inc(mean_mm, 1)
                else:
                    pe.wait_ge(pads_set, 5)
                    pe.wait_ge(ld_const, 16)
                pe.wait_ge(squares_ready, i + 1)
                for j in range(NT):
                    for kk in range(2):
                        x = mm(bank[6][:, j:j + 1], squares_v[:, kk, j * P:(j + 1) * P], mean_w[:, 0:1], kk == 0, kk == 1)
                x.then_inc(sums_mm, 1)
                pe.wait_ge(rstd_ready, i + 1)
                spread_rows(bank[7], small[:, 8:11]).then_inc(rstd_mm, 1)

            def spread_rows(dst, cols):
                for j in range(NT):
                    n = min(P, N - j * P)
                    x = mm(dst[:, j * P:j * P + n], cols[:, j:j + 1].to_broadcast([P, P]), ident[:, 0:n], True, True)
                return x

            def attention(l, w_qkv, ld_qkv, w_proj, ld_proj):
                sets = SETS if l == 0 else 1
                tiles = QKV_TILES[l]
                pe.wait_ge(normed_ready, 1 if l == 0 else 3)
                pe.wait_ge(ld_qkv, 16)
                for i in range(tiles):
                    if i >= 8:
                        pe.wait_ge(*taken(l, i - 8))
                    for kk in range(2):
                        x = mm(bank[i % 8][:, 0:N], w_qkv[:, kk, i, :], normed_v[:, kk, 0:N], kk == 0, kk == 1)
                    x.then_inc(qkv_mm[l], 1)
                s_bank = bank[4 if l == 0 else 6]
                w = 32 if l == 0 else 8
                if l == 0:
                    pe.wait_ge(*taken(l, 4))
                m = 0
                for r in range(2):
                    for d in range(T):
                        pe.wait_ge(prod_ready[l], m + 1)
                        p = prods[m % PRODS].rearrange("p s (t b) -> p s t b", b=B)
                        for kap in range(2):
                            for gg in range(4):
                                if l == 0:
                                    src = p[:, 2 * (gg // 2) + kap, 0:T - d, (gg % 2) * 32:(gg % 2) * 32 + 32]
                                else:
                                    src = p[:, 0, 0:T - d, (2 * gg + kap) * 8:(2 * gg + kap) * 8 + 8]
                                o = s_bank[32 * gg:32 * gg + 32, OFF[d] * w:(OFF[d] + T - d) * w]
                                x = mm(o.rearrange("p (s b) -> p s b", b=w), lane_of[:, r, kap, :], src,
                                       m == 0 and kap == 0, r == 1 and kap == 1, skip_group_check=True,
                                       tile_position=(0, 32 * gg))
                        x.then_inc(score_mm[l], 1)
                        m += 1
                pe.wait_ge(prob_ready[l], T)
                pe.wait_ge(lane_ready, 1)
                n = PAIRS * w
                if l == 0:
                    pe.wait_ge(*taken(l, 11))
                for c in range(16 if l == 0 else 4):
                    if c >= 4:
                        pe.wait_ge(weighted_ready[l], c - 3)
                    for o8 in range(1 if l == 0 else 4):
                        if l == 0:
                            r, (st, half_b) = c // 8, divmod(c % 8, 2)
                            gg, kap = 2 * (st // 2) + half_b, st % 2
                        else:
                            r, quad = divmod(c, 2)
                            gg, kap = divmod(4 * quad + o8, 2)
                        base = 32 * gg + 16 * kap + 8 * r
                        x = mm(bank[c % 4][:, o8 * n:(o8 + 1) * n], lane_to[:, HD * base:HD * base + P],
                               prob[:, 0:n], True, True)
                    x.then_inc(spread_mm[l], 1)
                pe.wait_ge(ld_proj, 16)
                pe.wait_ge(mixed_pool[l], T - 1)
                pe.wait_ge(mixed_dve[l], T - 1)
                for mo in range(2):
                    dst = bank[mo + (5 if l == 0 else 0)]
                    for r in range(2):
                        for st in range(sets):
                            if l == 0:
                                y = weighted[r].rearrange("p (s h c) -> p s h c", s=SETS, h=2)[:, st, :, 0:T * w]
                                y = y.rearrange("p h (t b) -> p t h b", b=w)
                                o = dst[:, 0:N].rearrange("p (t h b) -> p t h b", h=2, b=w)
                            else:
                                y = weighted[r][:, 0:8 * n].rearrange("p (h c) -> p h c", h=8)[:, :, 0:T * w]
                                y = y.rearrange("p h (t b) -> p t h b", b=w)
                                o = dst[:, 0:N].rearrange("p (t h b) -> p t h b", h=8, b=w)
                            x = mm(o, w_proj[:, r, st, mo * P:(mo + 1) * P], y, r == 0 and st == 0, r == 1 and st == sets - 1)
                    x.then_inc(proj_mm[l], 1)

            def logits(l, n, w):
                for j in range(NT):
                    for kk in range(2):
                        x = mm(bank[0][:, j * n:(j + 1) * n], normed_v[:, kk, j * P:(j + 1) * P], w[:, kk, :], kk == 0, kk == 1)
                x.then_inc(logit_mm[l], 1)

            norm(0)
            norm(1)
            attention(0, carve(w_qkv0, 0, 2, 12, P), ld_qkv0, carve(w_proj0, 0, 2, SETS, D), ld_proj0)
            norm(2)
            pe.wait_ge(normed_ready, 2)
            pe.wait_ge(ld_gates, 16)
            logits(0, E0, carve(w_gates, 0, 2, E0))
            for j in range(NT):
                for r in range(2):
                    x = nc.tensor.transpose(bank[1 + j // 2][:, (j % 2) * D + r * P:(j % 2) * D + (r + 1) * P],
                                            normed_v[:, r, j * P:(j + 1) * P], ident)
            x.then_inc(xtok_mm, 1)
            pe.wait_ge(onehot_ready, 1)
            onehot = carve(small, 340, NT, E0).bitcast(bf16)[:, :, 0:E0]
            for j in range(NT):
                for jj in range(NT):
                    x = mm(bank[3][:, j * E0:(j + 1) * E0], before[:, jj * NP + j * P:jj * NP + (j + 1) * P], onehot[:, jj, :],
                           jj == 0, jj == NT - 1)
            x.then_inc(rank_mm, 1)
            pe.wait_ge(xtok_ready, 2)
            pe.wait_ge(place_ready, NT)
            for r in range(2):
                for j in range(NT):
                    x = mm(bank[4 + r][:, :], x_tok[:, j, r * P:(r + 1) * P], place[:, j, :], j == 0, j == NT - 1)
                x.then_inc(xslot_mm, 1)
            pe.wait_ge(gatew_ready, 1)
            spread_rows(bank[6], small[:, 20:23]).then_inc(row_mm, 1)
            spread_rows(bank[7], small[:, 24:27]).then_inc(row_mm, 1)
            pe.wait_ge(xslot_ready, 2)

            def expert(e):
                s = (e % RING) * W0_COLS
                return carve(ring, s, 2, F0), carve(ring, s + 2 * F0, F0 // P, D)

            def up(e4):
                for j in range(4):
                    e = 4 * e4 + j
                    pe.wait_ge(ld_slot[e % RING], 16 * (e // RING + 1))
                if e4 >= 2:
                    pe.wait_ge(inner_ready, 2 * (e4 - 1))
                for c in range(2):
                    for kk in range(2):
                        for j in range(4):
                            e = 4 * e4 + j
                            x = mm(bank[2 * (e4 % 2) + c][32 * j:32 * j + 32, :], x_slot[:, kk, SLOT * e:SLOT * e + SLOT],
                                   expert(e)[0][:, kk, 512 * c:512 * c + 512], kk == 0, kk == 1, tile_position=(0, 32 * j))
                    x.then_inc(ff1_mm, 1)

            def down(e4):
                if e4 == 0:
                    pe.wait_ge(back_ready, 4)
                for c in range(2):
                    pe.wait_ge(inner_ready, 2 * e4 + c + 1)
                    if e4 >= 1:
                        pe.wait_ge(innert_ready, 2 * (e4 - 1) + c + 1)
                    for kk in range(4):
                        at = 512 * c + P * kk
                        x = nc.tensor.transpose(bank[4 + c][:, P * kk:P * kk + P], inner[e4 % 2][:, at:at + P], ident)
                    x.then_inc(innert_mm, 1)
                if e4 >= 2:
                    pe.wait_ge(yslot_ready, e4 - 1)
                for kk in range(F0 // P):
                    if kk % 4 == 0:
                        pe.wait_ge(innert_ready, 2 * e4 + kk // 4 + 1)
                    for j in range(4):
                        x = mm(bank[6 + e4 % 2][32 * j:32 * j + 32, 0:D], inner_t[:, kk, 32 * j:32 * j + 32],
                               expert(4 * e4 + j)[1][:, kk, :], kk == 0, kk == F0 // P - 1, tile_position=(0, 32 * j))
                x.then_inc(ff2_mm, 1)

            up(0)
            for e4 in range(E0 // 4):
                if e4 < E0 // 4 - 1:
                    up(e4 + 1)
                down(e4)
            pe.wait_ge(yslot_ready, 4)
            for r in range(2):
                for j in range(4):
                    x = mm(bank[r][:, 0:N], y_slot[:, j, r * P:(r + 1) * P], back[:, j, :], j == 0, j == 3)
                x.then_inc(combine_mm, 1)
            norm(3)
            attention(1, carve(w_qkv1, 0, 2, 6, P), ld_qkv1, carve(w_proj1, 0, 2, 1, D), ld_proj1)
            norm(4)
            pe.wait_ge(normed_ready, 4)
            logits(1, E1, carve(w_gates, 2 * E0, 2, E1))

            def gate_up(n):
                e, it = divmod(n, 4)
                if it == 0:
                    pe.wait_ge(ld_slot[e], 48)
                if n >= 2:
                    pe.wait_ge(upgate_ready, n - 1)
                w = carve(ring, e * W0_COLS, 2, 2 * (F1 // P), P)
                for kind in range(2):
                    for kk in range(2):
                        x = mm(bank[1 + 2 * (n % 2) + kind][:, 0:N], w[:, kk, kind * (F1 // P) + it, :], normed_v[:, kk, 0:N],
                               kk == 0, kk == 1)
                x.then_inc(gate_mm, 1)

            def down1(n):
                e, it = divmod(n, 4)
                w = carve(ring, e * W0_COLS + 4 * F1, F1 // P, D)
                pe.wait_ge(act_ready, n + 1)
                for r in range(2):
                    x = mm(bank[6 + r][:, 0:N], w[:, it, r * P:(r + 1) * P], act_in[n % NG], n == 0, n == 4 * E1 - 1)
                x.then_inc(down_mm, 1)

            gate_up(0)
            gate_up(1)
            pe.wait_ge(comb_ready, 1)
            comb = carve(small, 440, NT, E1)
            for e in range(E1):
                if e >= 2:
                    pe.wait_ge(share_ready, e - 1)
                for j in range(NT):
                    n = min(P, N - j * P)
                    x = mm(bank[5 * (e % 2)][:, j * P:j * P + n], comb[:, j, e:e + 1].to_broadcast([P, P]), ident[:, 0:n], True, True)
                x.then_inc(share_mm, 1)
            for n in range(4 * E1):
                if n + 2 < 4 * E1 and n >= 0:
                    pass
                if n >= 1 and n + 1 < 4 * E1:
                    gate_up(n + 1)
                down1(n)
            pe.wait_ge(final_ready, 2)
            for j in range(NT):
                for r in range(2):
                    x = nc.tensor.transpose(bank[j][:, r * P:(r + 1) * P], normed_v[:, r, j * P:(j + 1) * P], ident)
                x.then_inc(final_mm, 1)


def first_pair(t):
    return (5 * t - 4) // 2


def layouts(x, w1, b1, w2, b2, w3, b3, w4, b4, w5, b5, freqs, norm_w, attn0, proj0, gate0, up0, down0, attn1, proj1, gate1, w13, down1):
    f = np.float32
    perm = np.arange(D).reshape(P, 2).T
    arr = {}
    vec = np.zeros((P, NVEC), f)
    vec[:, CB1] = np.tile(b1, 4)
    vec[:, CB2] = np.tile(b2, 2)
    vec[:, CB3:CB3 + 2] = b3.reshape(2, P).T
    vec[:, CB4:CB4 + 2] = b4.reshape(2, P).T
    vec[:, CB5:CB5 + 2] = b5[perm].T
    vec[:, CNW:CNW + 2] = norm_w[perm].T
    vec[:, CFR] = np.tile(freqs, P // (HD // 2))
    arr["vec"] = vec
    pad = np.zeros((B, 32 * (G1 - 1) + TAPS), f)
    pad[:, 7:7 + x.shape[2]] = x[:, 0, :]
    arr["windows"] = np.stack([pad[:, i:i + 32 * (G1 - 1) + 1:32].T for i in range(TAPS)]).reshape(TAPS, G1 * B)
    c12 = np.zeros((P, 4 * P), f)
    for j in range(4):
        c12[8 * j:8 * j + 15, 32 * j:32 * j + 32] = w1[:, 0, :].T
    c2 = c12[:, P:].reshape(4, C1, 3, 2, C2)
    for j in range(4):
        if j >= 1:
            c2[j, :, 0, 0, :] = w2[:, :, j - 1].T
            c2[j, :, 1, 1, :] = w2[:, :, j - 1].T
        c2[j, :, 1, 0, :] = w2[:, :, j + 3].T
        c2[j, :, 2, 1, :] = w2[:, :, j + 3].T
    arr["w_conv12"] = c12
    c3 = np.zeros((2, C2, 2, 5, D), f)
    for par in range(2):
        for d in range(5):
            if 2 * d + par <= 8:
                c3[par, :, 0, d, :] = w3[:, :, 2 * d + par].T
            if 2 * d + par >= 1:
                c3[par, :, 1, d, :] = w3[:, :, 2 * d + par - 1].T
    c4 = np.zeros((P, 3, 2, P), f)
    for o in range(D):
        r, oc = divmod(o, P)
        c4[oc // 8 * 8:oc // 8 * 8 + 8, :, r, oc] = w4[o]
    c5 = w5[:, :, 0][perm].transpose(2, 0, 1).reshape(2, P, D).transpose(1, 0, 2)
    arr["w_conv345"] = np.concatenate([c3.reshape(P, -1), c4.reshape(P, -1), c5.reshape(P, -1)], axis=1)
    a0 = attn0.reshape(SETS + 2, 2, P, D)
    tiles = [a0[j, r] for r in range(2) for j in [SETS] + list(range(SETS))] + [a0[SETS + 1, r] for r in range(2)]
    arr["w_qkv0"] = np.stack(tiles)[:, :, perm].transpose(3, 2, 0, 1).reshape(P, -1)
    arr["w_proj0"] = proj0[perm].reshape(2, P, SETS, 2, P).transpose(4, 3, 2, 0, 1).reshape(P, -1)
    a1 = attn1.T.reshape(3, 2, P, D)
    tiles = [a1[j, r] for r in range(2) for j in (1, 0)] + [a1[2, r] for r in range(2)]
    arr["w_qkv1"] = np.stack(tiles)[:, :, perm].transpose(3, 2, 0, 1).reshape(P, -1)
    arr["w_proj1"] = proj1[:, perm].reshape(2, P, 2, P).transpose(1, 0, 2, 3).reshape(P, -1)
    arr["w_gates"] = np.concatenate([gate0[:, perm].transpose(2, 1, 0).reshape(P, -1), gate1[:, perm].transpose(2, 1, 0).reshape(P, -1)], axis=1)
    ups = up0[:, perm, :].transpose(0, 2, 1, 3).reshape(E0, P, -1)
    downs = down0[:, :, perm].reshape(E0, F0 // P, P, D).transpose(0, 2, 1, 3).reshape(E0, P, -1)
    arr["w_exp0"] = np.concatenate([ups, downs], axis=2)
    ups = w13[:, :, perm].transpose(0, 3, 2, 1).reshape(E1, P, -1)
    downs = down1[:, perm, :].transpose(0, 3, 1, 2).reshape(E1, F1 // P, P, D).transpose(0, 2, 1, 3).reshape(E1, P, -1)
    arr["w_exp1"] = np.concatenate([ups, downs], axis=2)
    const = np.zeros((P, NCONST), f)
    const[:, K_ID:K_ID + P] = np.eye(P)
    lanes = const[:, K_IND:K_IND + P].reshape(P, 2, 2, 32)
    for p in range(P):
        for r in range(2):
            for kap in range(2):
                lanes[p, r, kap, 16 * kap + 8 * r + p // HD] = 1
    const[:, K_REV16:K_REV16 + E0] = E0 - np.arange(E0)
    const[:, K_E32:K_E32 + E0] = SLOT * np.arange(E0)
    const[:, K_REV8:K_REV8 + E1] = E1 - np.arange(E1)
    const[:, K_REV4:K_REV4 + 4] = 4 - np.arange(4)
    const[:, K_SLOT:K_SLOT + 4] = 1 + np.arange(4 * P).reshape(4, P).T
    key = np.full(NP, 2 * FAR)
    key[:N] = (np.arange(B)[None, :] * T + np.arange(T)[:, None]).ravel()
    const[:, K_KEY:K_KEY + NT] = key.reshape(NT, P).T
    const[:, K_T:K_T + T] = np.arange(T)
    arr["const"] = const
    return {n: np.ascontiguousarray(v, dtype=f) for n, v in arr.items()}


def kernel(x, L0_tok_w1, L0_tok_b1, L0_tok_w2, L0_tok_b2, L0_tok_w3, L0_tok_b3, L0_tok_w4, L0_tok_b4, L0_tok_w5, L0_tok_b5,
           L0_tok_rope_freqs, L0_tok_norm_w, L0_attn_W_attn, L0_attn_W_proj, L0_ffn_gate_w, L0_ffn_w1, L0_ffn_w2,
           L1_attn_W_attn, L1_attn_W_proj, L1_ffn_gate_w, L1_ffn_w13_weight, L1_ffn_w2_weight):
    import concourse.bacc as bacc
    from concourse.bass_utils import run_bass_kernel_spmd

    arrays = layouts(*(np.asarray(v) for v in (
        x, L0_tok_w1, L0_tok_b1, L0_tok_w2, L0_tok_b2, L0_tok_w3, L0_tok_b3, L0_tok_w4, L0_tok_b4, L0_tok_w5, L0_tok_b5,
        L0_tok_rope_freqs, L0_tok_norm_w, L0_attn_W_attn, L0_attn_W_proj, L0_ffn_gate_w, L0_ffn_w1, L0_ffn_w2,
        L1_attn_W_attn, L1_attn_W_proj, L1_ffn_gate_w, L1_ffn_w13_weight, L1_ffn_w2_weight)))
    nc = bacc.Bacc("TRN2", target_bir_lowering=False, num_devices=1)
    aps = {n: nc.dram_tensor(f"in_{n}", v.shape, mybir.dt.from_np(v.dtype), kind="ExternalInput").ap() for n, v in arrays.items()}
    out = nc.dram_tensor("tokens_out", (B, T, D), mybir.dt.float32, kind="ExternalOutput").ap()
    audio_tower(nc, aps, out)
    r = run_bass_kernel_spmd(nc, [{f"in_{n}": v for n, v in arrays.items()}], core_ids=[0])
    return r.results[0]["tokens_out"]
```

```python
import math
from contextlib import ExitStack

import numpy as np

import concourse.bass as bass
from concourse import mybir

P = 128
B, T = 64, 5
N = B * T
NP = 384
NT = NP // P
D = 256
C1, C2 = 32, 64
G1 = 24
TAPS = 39
POS1 = 94
M2 = 12
HEADS, HD = 16, 16
SETS = 4
E0, F0, CAP = 16, 1024, 26
SLOT = 32
E1, F1 = 8, 512
PAIRS = T * (T + 1) // 2
OFF = [sum(T - i for i in range(d)) for d in range(T)]
LN_EPS, RMS_EPS = 1e-5, 1e-8
SCALE = 1.0 / math.sqrt(HD)
TWO_PI_HI, TWO_PI_LO = 6.28125, 2 * math.pi - 6.28125
ROUND = 1.5 * 2.0 ** 23
FAR = 4096.0

W0_COLS = 2 * F0 + (F0 // P) * D
W1_COLS = 2 * 2 * F1 + (F1 // P) * D
RING = 8
WARM = [9, 6, 4, 13, 5, 30, 18, 3, 5, 10, 2, 3, 5, 3, 5]

CB1, CB2, CB3, CB4, CB5, CNW, CFR, NVEC = 0, 1, 2, 4, 6, 8, 10, 11
K_ID, K_IND, K_REV16, K_E32, K_REV8, K_REV4, K_SLOT, K_KEY, K_T = 0, 128, 256, 272, 288, 296, 300, 304, 307
NCONST = 312


def audio_tower(nc: bass.Bass, a: dict, out: bass.AP):
    f32, bf16 = mybir.dt.float32, mybir.dt.bfloat16
    ALU, ACT, AX = mybir.AluOpType, mybir.ActivationFunctionType, mybir.AxisListType

    with ExitStack() as ctx:
        def sb(name, cols, dt=f32):
            return ctx.enter_context(nc.sbuf_tensor(name, [P, cols], dt))

        def sem(name):
            return ctx.enter_context(nc.semaphore(name))

        bank = [ctx.enter_context(nc.psum_tensor(f"bank{i}", [P, 512], f32)) for i in range(8)]

        ring = sb("ring", RING * W0_COLS)
        vec = sb("vec", NVEC)
        const = sb("const", NCONST)
        w_conv12 = sb("w_conv12", P + 3 * P)
        w_qkv0 = sb("w_qkv0", 2 * 12 * P)
        w_proj0 = sb("w_proj0", 2 * SETS * D)
        w_qkv1 = sb("w_qkv1", 2 * 6 * P)
        w_proj1 = sb("w_proj1", 2 * D)
        w_gates = sb("w_gates", 2 * (E0 + E1))
        mean_w = sb("mean_w", P)
        slot_id = sb("slot_id", E0 * SLOT)
        key_row = sb("key_row", NP)
        before = sb("before", NT * NP, bf16)
        resid = sb("resid", 2 * NP)
        normed = sb("normed", 2 * NP)
        squares = sb("squares", 2 * NP)
        small = sb("small", 512)
        arena = sb("arena", 7936)

        def carve(t, at, *dims):
            n = 1
            for d in dims:
                n *= d
            v = t[:, at:at + n]
            if len(dims) == 1:
                return v
            names = [f"a{i}" for i in range(len(dims))]
            return v.rearrange(f"p ({' '.join(names)}) -> p {' '.join(names)}",
                               **{n: d for n, d in zip(names[1:], dims[1:])})

        resid_v, squares_v, normed_v = (carve(x, 0, 2, NP) for x in (resid, squares, normed))
        ident = const[:, K_ID:K_ID + P]
        lane_of = carve(const, K_IND, 2, 2, 32)

        borrowed6, borrowed7 = 6 * W0_COLS, 7 * W0_COLS
        w_conv3 = carve(ring, borrowed6, 10, D)
        w_conv4 = carve(ring, borrowed6 + 10 * D, 3, 2, P)
        w_conv5 = carve(ring, borrowed6 + 10 * D + 6 * P, 2, D)
        windows = arena[0:TAPS, 0:G1 * B]
        h1 = carve(arena, 1536, G1, B)
        h2 = carve(arena, 3072, M2, B)
        h3 = carve(arena, 3840, 2, N)
        h4 = carve(arena, 4480, 2, N)
        h5 = carve(arena, 5120, 2, N)
        turned = carve(arena, 5760, 2, N)
        crossed = carve(arena, 6400, 2, N)
        sincos = carve(arena, 7040, 2, T)
        angles = carve(arena, 7056, 2, T)
        cos_w = carve(arena, 7072, 2, T)
        sin_w = carve(arena, 7088, 2, T)

        q = carve(arena, 0, 2, SETS, N)
        k = carve(arena, 2560, 2, N)
        values = carve(arena, 3840, 2, N)
        vx = carve(arena, 4480, 2, PAIRS, B)
        score = carve(arena, 6400, 480)
        prob = carve(arena, 6880, 480)
        peak = carve(arena, 7360, 160)
        total = carve(arena, 7520, 160)
        inv = carve(arena, 7680, 160)
        PRODS = 3
        rstd_row = squares[:, 0:N]
        prods = [carve(ring, borrowed7 + i * SETS * N, SETS, N) for i in range(PRODS)]
        lane_to = w_qkv0[:, 0:P * HD]
        weighted = [ring[:, borrowed7:borrowed7 + 3840], arena[:, 0:3840]]

        x_tok = carve(arena, 6720, NT, D)
        place = carve(w_proj0, 0, NT, E0 * SLOT)
        x_slot = carve(arena, 0, 2, E0 * SLOT)
        inner = [carve(arena, 1024 + i * F0, F0) for i in range(2)]
        inner_t = carve(arena, 3072, F0 // P, P)
        y_slot = carve(arena, 4096, 4, D)
        back = carve(arena, 5120, 4, N)
        weight_row = carve(arena, 6400, N)

        share = carve(arena, 0, E1, N)
        NG = 4
        gate_out = [carve(arena, 2560 + i * N, N) for i in range(NG)]
        up_gate = [carve(arena, 3840 + i * N, N) for i in range(NG)]
        act_in = [carve(arena, 5120 + i * N, N) for i in range(NG)]
        final_tok = carve(w_proj0, 0, NT, P, 2)

        ld_first, ld_const, ld_conv, ld_qkv0, ld_proj0, ld_gates, ld_qkv1, ld_proj1 = (
            sem(n) for n in ("ld_first", "ld_const", "ld_conv", "ld_qkv0", "ld_proj0", "ld_gates", "ld_qkv1", "ld_proj1"))
        ld_up = [sem(f"ld_up{i}") for i in range(RING)]
        ld_down = [sem(f"ld_down{i}") for i in range(RING)]
        stored = sem("stored")
        pads_set, iotas, lane_ready = sem("pads_set"), sem("iotas"), sem("lane_ready")
        conv_mm, conv_out = sem("conv_mm"), sem("conv_out")
        angle_ready, sincos_ready, rope_done = sem("angle_ready"), sem("sincos_ready"), sem("rope_done")
        resid_ready = sem("resid_ready")
        normed_ready = sem("normed_ready")
        mean_mm, centred_ready, squares_ready, sums_mm = (sem(n) for n in ("mean_mm", "centred_ready", "squares_ready", "sums_mm"))
        var_ready, std_ready, rstd_ready, row_ready, rms_row_mm, rstd_row_mm = (
            sem(n) for n in ("var_ready", "std_ready", "rstd_ready", "row_ready", "rms_row_mm", "rstd_row_mm"))
        qkv_mm = [sem(f"qkv_mm{l}") for l in range(2)]
        qkv_act = [sem(f"qkv_act{l}") for l in range(2)]
        qkv_dve = [sem(f"qkv_dve{l}") for l in range(2)]
        prod_ready = [sem(f"prod_ready{l}") for l in range(2)]
        score_mm = [sem(f"score_mm{l}") for l in range(2)]
        shifted_ready = [sem(f"shifted_ready{l}") for l in range(2)]
        exp_ready = [sem(f"exp_ready{l}") for l in range(2)]
        prob_ready = [sem(f"prob_ready{l}") for l in range(2)]
        vx_ready = [sem(f"vx_ready{l}") for l in range(2)]
        spread_mm = [sem(f"spread_mm{l}") for l in range(2)]
        weighted_ready = [sem(f"weighted_ready{l}") for l in range(2)]
        mixed_pool = [sem(f"mixed_pool{l}") for l in range(2)]
        mixed_dve = [sem(f"mixed_dve{l}") for l in range(2)]
        proj_mm = [sem(f"proj_mm{l}") for l in range(2)]
        logit_mm = [sem(f"logit_mm{l}") for l in range(2)]
        lsub_ready = [sem(f"lsub_ready{l}") for l in range(2)]
        lexp_ready = [sem(f"lexp_ready{l}") for l in range(2)]
        xtok_mm, xtok_ready, onehot_ready, rank_mm, pos_ready, gatew_ready = (
            sem(n) for n in ("xtok_mm", "xtok_ready", "onehot_ready", "rank_mm", "pos_ready", "gatew_ready"))
        place_ready, xslot_mm, xslot_ready, row_mm, wrow_ready, back_ready = (
            sem(n) for n in ("place_ready", "xslot_mm", "xslot_ready", "row_mm", "wrow_ready", "back_ready"))
        ff1_mm, inner_ready, innert_mm, innert_ready, ff2_mm, yslot_ready, combine_mm = (
            sem(n) for n in ("ff1_mm", "inner_ready", "innert_mm", "innert_ready", "ff2_mm", "yslot_ready", "combine_mm"))
        comb_ready, share_mm, share_ready, gate_mm, silu_ready, upgate_ready, act_ready, down_mm = (
            sem(n) for n in ("comb_ready", "share_mm", "share_ready", "gate_mm", "silu_ready", "upgate_ready", "act_ready", "down_mm"))
        final_ready, final_mm, tok_ready = sem("final_ready"), sem("final_mm"), sem("tok_ready")
        dve_step, pool_step = sem("dve_step"), sem("pool_step")

        QKV_TILES = [12, 6]
        QKV_BANKS = 6
        PE_ORDER = [
            [("t", i) for i in range(8)] + [("s", 0, d) for d in range(3)] + [("t", 8), ("t", 9)] + [("s", 0, 3), ("s", 0, 4)]
            + [("t", 10), ("t", 11)] + [("s", 1, d) for d in range(T)],
            [("t", i) for i in range(6)] + [("s", r, d) for r in range(2) for d in range(T)]]
        DVE_ORDER = [
            [("t", i) for i in range(5)] + [("s", 0, d) for d in range(3)] + [("t", i) for i in (5, 6, 7)] + [("s", 0, 3), ("s", 0, 4)]
            + [("t", 8), ("t", 9)] + [("s", 1, d) for d in range(T)],
            [("t", 0), ("t", 1)] + [("s", 0, d) for d in range(3)] + [("t", 2), ("t", 3)] + [("s", 0, 3), ("s", 0, 4)]
            + [("s", 1, d) for d in range(T)]]

        def qkv_dst(l, i):
            per = 1 + (SETS if l == 0 else 1)
            if i >= 2 * per:
                return values[:, i - 2 * per, :]
            r, j = divmod(i, per)
            return k[:, r, :] if j == 0 else q[:, r, j - 1, :]

        block = ctx.enter_context(nc.Block())

        @block.sync
        def _(sp):
            sp.dma_start(vec[:, :], a["vec"]).then_inc(ld_first, 16)
            sp.dma_start(w_conv12[:, :], a["w_conv12"]).then_inc(ld_first, 16)
            sp.dma_start(windows, a["windows"]).then_inc(ld_first, 16)
            sp.dma_start(const[:, :], a["const"]).then_inc(ld_const, 16)
            sp.dma_start(ring[:, borrowed6:borrowed6 + 10 * D + 6 * P + 2 * D], a["w_conv345"]).then_inc(ld_conv, 16)
            sp.dma_start(w_qkv0[:, :], a["w_qkv0"]).then_inc(ld_qkv0, 16)
            sp.dma_start(w_proj0[:, :], a["w_proj0"]).then_inc(ld_proj0, 16)
            sp.dma_start(w_gates[:, :], a["w_gates"]).then_inc(ld_gates, 16)
            def load_exp0(e, part):
                at, n, done = ((0, 2 * F0, ld_up), (2 * F0, W0_COLS - 2 * F0, ld_down))[part]
                at += (e % RING) * W0_COLS
                sp.dma_start(ring[:, at:at + n], a["w_exp0"][e][:, at % W0_COLS:at % W0_COLS + n]).then_inc(done[e % RING], 16)

            for e4 in range(E0 // 4):
                for part in range(2):
                    if e4 >= 2:
                        if part == 0:
                            sp.wait_ge(ff1_mm, 2 * (e4 - 1))
                        else:
                            sp.wait_ge(ff2_mm, e4 - 1)
                    for e in range(4 * e4, 4 * e4 + 4):
                        if e == 6 and part == 0:
                            sp.wait_ge(conv_mm, 11)
                        if e != 7:
                            load_exp0(e, part)
                if e4 == 1:
                    sp.dma_start(w_qkv1[:, :], a["w_qkv1"]).then_inc(ld_qkv1, 16)
                    sp.dma_start(w_proj1[:, :], a["w_proj1"]).then_inc(ld_proj1, 16)
                    sp.wait_ge(proj_mm[0], 2)
                    load_exp0(7, 0)
                    load_exp0(7, 1)
            for e in range(E1):
                sp.wait_ge(ff2_mm, (e + RING) // 4 + 1)
                if e == 7:
                    sp.wait_ge(proj_mm[1], 2)
                sp.dma_start(ring[:, e * W0_COLS:e * W0_COLS + W1_COLS], a["w_exp1"][e]).then_inc(ld_up[e], 16)
            for t in range(T):
                sp.wait_ge(tok_ready, t // 2 + 1)
                rows = slice(B * (t % 2), B * (t % 2) + B)
                sp.dma_start(out[:, t, :], final_tok[rows, t // 2, :, :].rearrange("b p r -> b (p r)")).then_inc(stored, 16)
            sp.wait_ge(stored, 16 * T)

        @block.gpsimd
        def _(pool):
            g = nc.gpsimd
            g.memset(mean_w[:, :], 1.0 / D).then_inc(pads_set, 1)
            g.memset(h1[:, G1 - 1, :], 0.0).then_inc(pads_set, 1)
            for v in (resid_v, squares_v, normed_v):
                g.memset(v[:, :, N:NP], 0.0).then_inc(pads_set, 1)
            g.iota(slot_id[:, :], [[1, E0 * SLOT]], base=1, channel_multiplier=0,
                   allow_small_or_imprecise_dtypes=True).then_inc(iotas, 1)
            g.iota(key_row[:, 0:N].rearrange("p (t b) -> p t b", b=B), [[1, T], [T, B]], base=0, channel_multiplier=0,
                   allow_small_or_imprecise_dtypes=True).then_inc(iotas, 1)
            g.memset(key_row[:, N:NP], FAR).then_inc(iotas, 1)

            def attention(l, width):
                pool.wait_ge(qkv_act[l], 2)
                for d in range(T):
                    n = (T - d) * B
                    g.tensor_tensor(vx[:, :, OFF[d]:OFF[d] + T - d, :].rearrange("p r s b -> p r (s b)"), values[:, :, 0:n],
                                    rstd_row[:, 0:n].unsqueeze(1).to_broadcast([P, 2, n]), ALU.mult).then_inc(vx_ready[l], 1)
                pool.wait_ge(weighted_ready[l], 8 if l == 0 else 2)
                w = weighted[0].rearrange("p (c s) -> p c s", c=8)[:, :, :] if l == 0 else \
                    weighted[0][:, 0:960].rearrange("p (c s) -> p c s", c=8)
                for d in range(1, T):
                    dst = w[:, :, d * width:T * width]
                    g.tensor_tensor(dst, dst, w[:, :, OFF[d] * width:(OFF[d] + T - d) * width], ALU.add)\
                        .then_inc(mixed_pool[l], 1)
                    pool.wait_ge(mixed_pool[l], d)
            attention(0, 32)
            attention(1, 8)

        @block.scalar
        def _(act):
            s = nc.scalar
            act.wait_ge(ld_first, 48)
            act.wait_ge(angle_ready, 1)
            s.activation(sincos, angles, ACT.Sin).then_inc(sincos_ready, 1)
            act.wait_ge(pads_set, 2)
            for c in range(3):
                act.wait_ge(conv_mm, c + 1)
                if c < 2:
                    s.activation(h1[:, 8 * c:8 * c + 8, :].rearrange("p g b -> p (g b)"), bank[c][:, :], ACT.Gelu,
                                 bias=vec[:, CB1:CB1 + 1]).then_inc(conv_out, 1)
                else:
                    s.activation(h1[:, 16:23, :].rearrange("p g b -> p (g b)"), bank[2][:, 0:7 * B], ACT.Gelu,
                                 bias=vec[:, CB1:CB1 + 1]).then_inc(conv_out, 1)
                    last = (POS1 - 4 * (G1 - 1)) * C1
                    s.activation(h1[0:last, 23, :], bank[2][0:last, 7 * B:8 * B], ACT.Gelu,
                                 bias=vec[0:last, CB1:CB1 + 1]).then_inc(conv_out, 1)
            for c in range(2):
                act.wait_ge(conv_mm, 4 + c)
                s.activation(h2[:, 6 * c:6 * c + 6, :].rearrange("p m b -> p (m b)"), bank[3 + c][:, 0:6 * B], ACT.Gelu,
                             bias=vec[:, CB2:CB2 + 1]).then_inc(conv_out, 1)
            for n, (dst, cb, banks) in enumerate(((h3, CB3, (5, 6)), (h4, CB4, (7, 0)), (h5, CB5, (1, 2)))):
                for r in range(2):
                    act.wait_ge(conv_mm, 6 + 2 * n + r)
                    s.activation(dst[:, r, :], bank[banks[r]][:, 0:N], ACT.Gelu,
                                 bias=vec[:, cb + r:cb + r + 1]).then_inc(conv_out, 1)

            def norm(i, row):
                if i == 0:
                    act.wait_ge(conv_out, 12)
                    act.wait_ge(pads_set, 4)
                    s.activation(resid_v[:, :, 0:N], h5, ACT.Square).then_inc(squares_ready, 1)
                act.wait_ge(centred_ready, i + 1)
                s.activation(squares_v[:, :, 0:N], normed_v[:, :, 0:N], ACT.Square).then_inc(squares_ready, 1)
                act.wait_ge(var_ready, i + 1)
                s.activation(small[:, 8:14], small[:, 0:6], ACT.Sqrt).then_inc(std_ready, 1)
                if row:
                    act.wait_ge(rstd_row_mm, row)
                    s.activation(rstd_row, bank[6][:, 0:N], ACT.Copy).then_inc(row_ready, 1)

            def attention(l):
                tiles = QKV_TILES[l]
                for i in range(tiles - 2, tiles):
                    act.wait_ge(qkv_mm[l], i + 1)
                    s.activation(qkv_dst(l, i), bank[i % QKV_BANKS][:, 0:N], ACT.Copy).then_inc(qkv_act[l], 1)
                if l == 0:
                    s.activation(lane_to.rearrange("p (l d) -> p l d", d=HD), ident.unsqueeze(2).to_broadcast([P, P, HD]),
                                 ACT.Copy).then_inc(lane_ready, 1)
                act.wait_ge(shifted_ready[l], T)
                n = 480 if l == 0 else 120
                s.activation(prob[:, 0:n], score[:, 0:n], ACT.Exp, scale=SCALE).then_inc(exp_ready[l], 1)

            def router(l, n):
                act.wait_ge(lsub_ready[l], 1)
                for j in range(NT):
                    s.activation(small[:, 100 + j * n:100 + j * n + n], small[:, 40 + j * n:40 + j * n + n], ACT.Exp,
                                 scale=small[:, 16 + j:17 + j]).then_inc(lexp_ready[l], 1)

            norm(0, 1)
            attention(0)
            norm(1, 0)
            act.wait_ge(rstd_ready, 2)
            act.wait_ge(xtok_mm, 1)
            for j in range(NT):
                s.activation(x_tok[:, j, :], bank[1 + j // 2][:, (j % 2) * D:(j % 2) * D + D], ACT.Copy,
                             scale=small[:, 16 + j:17 + j]).then_inc(xtok_ready, 1)
            router(0, E0)
            act.wait_ge(xslot_mm, 1)
            s.activation(x_slot[:, 0, :], bank[4][:, :], ACT.Copy).then_inc(xslot_ready, 1)
            act.wait_ge(row_mm, 2)
            s.activation(weight_row, bank[7][:, 0:N], ACT.Copy).then_inc(wrow_ready, 1)
            for e4 in range(E0 // 4):
                if e4 >= 2:
                    act.wait_ge(innert_mm, 2 * (e4 - 1))
                for c in range(2):
                    act.wait_ge(ff1_mm, 2 * e4 + c + 1)
                    s.activation(inner[e4 % 2][:, 512 * c:512 * c + 512], bank[2 * (e4 % 2) + c][:, :],
                                 ACT.Gelu_apprx_tanh).then_inc(inner_ready, 1)
                if e4 >= 1:
                    act.wait_ge(ff2_mm, e4)
                    s.activation(y_slot[:, e4 - 1, :], bank[6 + (e4 - 1) % 2][:, 0:D], ACT.Copy).then_inc(yslot_ready, 1)
            act.wait_ge(ff2_mm, 4)
            s.activation(y_slot[:, 3, :], bank[7][:, 0:D], ACT.Copy).then_inc(yslot_ready, 1)
            norm(2, 2)
            attention(1)
            norm(3, 3)
            router(1, E1)

            def silu(n):
                act.wait_ge(gate_mm, n + 1)
                if n >= NG:
                    act.wait_ge(upgate_ready, n - NG + 1)
                s.activation(gate_out[n % NG], bank[1 + 2 * (n % 2)][:, 0:N], ACT.Silu).then_inc(silu_ready, 1)
            silu(0)
            silu(1)
            for e in range(E1):
                act.wait_ge(share_mm, e + 1)
                s.activation(share[:, e, :], bank[5 * (e % 2)][:, 0:N], ACT.Copy).then_inc(share_ready, 1)
            for n in range(2, 4 * E1):
                silu(n)

        @block.vector
        def _(dve):
            v = nc.vector
            steps = [0]

            def then(ins):
                steps[0] += 1
                ins.then_inc(dve_step, 1)
                dve.wait_ge(dve_step, steps[0])

            dve.wait_ge(ld_first, 48)
            dve.wait_ge(ld_const, 16)
            angle, turns, over = (carve(small, 16 * i, 2, T) for i in range(2, 5))
            PI = 3.1415925
            v.tensor_scalar(angle[:, 0, :], const[:, K_T:K_T + T], vec[:, CFR:CFR + 1], None, ALU.mult)
            then(v.tensor_scalar(angle[:, 1, :], const[:, K_T:K_T + T], vec[:, CFR:CFR + 1], None, ALU.mult))
            then(v.tensor_scalar(turns, angle, 1 / (2 * math.pi), ROUND, ALU.mult, ALU.add))
            then(v.tensor_scalar(turns, turns, -ROUND, None, ALU.add))
            then(v.scalar_tensor_tensor(out=angle, in0=turns, scalar=-TWO_PI_HI, in1=angle, op0=ALU.mult, op1=ALU.add))
            then(v.scalar_tensor_tensor(out=angle, in0=turns, scalar=-TWO_PI_LO, in1=angle, op0=ALU.mult, op1=ALU.add))
            then(v.tensor_scalar(angle[:, 1, :], angle[:, 1, :], math.pi / 2, None, ALU.add))
            then(v.tensor_scalar(over, angle, math.pi, -2 * math.pi, ALU.is_gt, ALU.mult))
            then(v.tensor_tensor(angle, angle, over, ALU.add))
            v.tensor_scalar(angles, angle, PI, -PI, ALU.min, ALU.max).then_inc(angle_ready, 1)
            dve.wait_ge(iotas, 3)
            for j in range(NT):
                then(v.tensor_scalar(before[:, j * NP:(j + 1) * NP], key_row[:, :], const[:, K_KEY + j:K_KEY + j + 1], None,
                                     ALU.is_ge))

            dve.wait_ge(sincos_ready, 1)
            for r in range(2):
                wr = vec[:, CNW + r:CNW + r + 1]
                v.tensor_scalar(cos_w[:, r, :], sincos[:, 1, :], wr, None, ALU.mult)
                last = v.tensor_scalar(sin_w[:, r, :], sincos[:, 0, :], wr, (-1.0, 1.0)[r], ALU.mult, ALU.mult)
            then(last)

            def by_time(x):
                return x.unsqueeze(2).to_broadcast([P, T, B])
            h5t = h5.rearrange("p r (t b) -> p r t b", b=B)
            tt = turned.rearrange("p r (t b) -> p r t b", b=B)
            ct = crossed.rearrange("p r (t b) -> p r t b", b=B)
            for r in range(2):
                dve.wait_ge(conv_out, 11 + r)
                v.tensor_tensor(tt[:, r], h5t[:, r], by_time(cos_w[:, r, :]), ALU.mult)
                last = v.tensor_tensor(ct[:, 1 - r], h5t[:, r], by_time(sin_w[:, 1 - r, :]), ALU.mult)
            then(last)
            v.tensor_tensor(turned, turned, crossed, ALU.add).then_inc(rope_done, 1)

            def centre(i, src):
                dve.wait_ge(mean_mm, i + 1)
                mean = bank[7][:, 0:N].unsqueeze(1).to_broadcast([P, 2, N])
                v.tensor_tensor(normed_v[:, :, 0:N], src, mean, ALU.subtract).then_inc(centred_ready, 1)

            def stats(i):
                dve.wait_ge(sums_mm, i + 1)
                if i == 0:
                    then(v.tensor_scalar(small[:, 3:6], bank[7][:, 3:6], RMS_EPS, None, ALU.add))
                    v.scalar_tensor_tensor(out=small[:, 0:3], in0=small[:, 3:6], scalar=LN_EPS, in1=bank[7][:, 0:3],
                                           op0=ALU.mult, op1=ALU.add).then_inc(var_ready, 1)
                else:
                    v.tensor_scalar(small[:, 0:3], bank[7][:, 0:3], LN_EPS, None, ALU.add).then_inc(var_ready, 1)
                dve.wait_ge(std_ready, i + 1)
                v.reciprocal(small[:, 16:22], small[:, 8:14]).then_inc(rstd_ready, 1)

            centre(0, turned)
            stats(0)
            dve.wait_ge(rms_row_mm, 1)
            then(v.tensor_tensor(resid_v[:, :, 0:N], turned, bank[7][:, 0:N].unsqueeze(1).to_broadcast([P, 2, N]), ALU.mult))

            def attention(l):
                sets = SETS if l == 0 else 1
                w = 32 if l == 0 else 8
                n = PAIRS * w
                dve.wait_ge(row_ready, l + 1)
                for kind, *at in DVE_ORDER[l]:
                    if kind == "t":
                        i = at[0]
                        dve.wait_ge(qkv_mm[l], i + 1)
                        v.tensor_tensor(qkv_dst(l, i), bank[i % QKV_BANKS][:, 0:N], rstd_row, ALU.mult).then_inc(qkv_dve[l], 1)
                    else:
                        r, d = at
                        m = r * T + d
                        cols = (T - d) * B
                        dve.wait_ge(qkv_dve[l], (r + 1) * (1 + sets))
                        if m >= PRODS:
                            dve.wait_ge(score_mm[l], m - PRODS + 1)
                        v.tensor_tensor(prods[m % PRODS][:, 0:sets, 0:cols], q[:, r, 0:sets, d * B:N],
                                        k[:, r, 0:cols].unsqueeze(1).to_broadcast([P, sets, cols]), ALU.mult)\
                            .then_inc(prod_ready[l], 1)
                dve.wait_ge(score_mm[l], 2 * T)
                s_ps = bank[6]
                blk = [slice(OFF[d] * w, (OFF[d] + T - d) * w) for d in range(T)]
                late = [slice(d * w, T * w) for d in range(T)]
                then(v.tensor_copy(peak[:, late[0]], s_ps[:, blk[0]]))
                for d in range(1, T):
                    then(v.tensor_tensor(peak[:, late[d]], s_ps[:, blk[d]], peak[:, late[d]], ALU.max))
                for d in range(T):
                    v.tensor_tensor(score[:, blk[d]], s_ps[:, blk[d]], peak[:, late[d]], ALU.subtract)\
                        .then_inc(shifted_ready[l], 1)
                dve.wait_ge(exp_ready[l], 1)
                then(v.tensor_copy(total[:, late[0]], prob[:, blk[0]]))
                for d in range(1, T):
                    then(v.tensor_tensor(total[:, late[d]], total[:, late[d]], prob[:, blk[d]], ALU.add))
                then(v.reciprocal(inv[:, 0:T * w], total[:, 0:T * w]))
                for d in range(T):
                    v.tensor_tensor(prob[:, blk[d]], prob[:, blk[d]], inv[:, late[d]], ALU.mult).then_inc(prob_ready[l], 1)
                dve.wait_ge(vx_ready[l], T)
                dve.wait_ge(score_mm[l], 2 * T)
                for c in range(16 if l == 0 else 4):
                    dve.wait_ge(spread_mm[l], c + 1)
                    if l == 0:
                        r, (st, half_b) = c // 8, divmod(c % 8, 2)
                        dst = weighted[r][:, (c % 8) * n:(c % 8 + 1) * n].rearrange("p (s b) -> p s b", b=w)
                        src = bank[c % 4][:, 0:n].rearrange("p (s b) -> p s b", b=w)
                        val = vx[:, r, :, half_b * w:(half_b + 1) * w]
                    else:
                        r, quad = divmod(c, 2)
                        dst = weighted[r][:, quad * 4 * n:(quad + 1) * 4 * n].rearrange("p (o s b) -> p o s b", o=4, b=w)
                        src = bank[c % 4][:, 0:4 * n].rearrange("p (o s b) -> p o s b", o=4, b=w)
                        val = vx[:, r, :, quad * 32:(quad + 1) * 32].rearrange("p s (o b) -> p o s b", b=w)
                    v.tensor_tensor(dst, src, val, ALU.mult).then_inc(weighted_ready[l], 1)
                dve.wait_ge(weighted_ready[l], 16 if l == 0 else 4)
                wt = weighted[1][:, 0:8 * n].rearrange("p (c s) -> p c s", c=8)
                for d in range(1, T):
                    v.tensor_tensor(wt[:, :, late[d]], wt[:, :, late[d]], wt[:, :, blk[d]], ALU.add).then_inc(mixed_dve[l], 1)
                    dve.wait_ge(mixed_dve[l], d)
                for r in range(2):
                    dve.wait_ge(proj_mm[l], r + 1)
                    v.tensor_tensor(resid_v[:, r, 0:N], bank[4 + r][:, 0:N], resid_v[:, r, 0:N], ALU.add)\
                        .then_inc(resid_ready, 1)

            attention(0)
            centre(1, resid_v[:, :, 0:N])

            def over_experts(x, n):
                return x.unsqueeze(2).to_broadcast([P, NT, n])

            def first_max(src, top, hit, which, rev, n):
                then(v.tensor_reduce(out=top, in_=src, axis=AX.X, op=ALU.max))
                then(v.tensor_tensor(hit, src, over_experts(top, n), ALU.is_ge))
                then(v.tensor_tensor(hit, hit, rev.unsqueeze(1).to_broadcast([P, NT, n]), ALU.mult))
                then(v.tensor_reduce(out=which, in_=hit, axis=AX.X, op=ALU.max))
                then(v.tensor_tensor(hit, hit, over_experts(which, n), ALU.is_equal))

            top, which = carve(small, 24, NT), carve(small, 27, NT)
            lsub, hit, lexp = carve(small, 40, NT, E0), carve(small, 160, NT, E0), carve(small, 100, NT, E0)
            slotval, kept = carve(small, 220, NT, E0), carve(small, 280, NT, E0)
            hit16 = carve(small, 340, NT, E0)
            pos, gate_w, expsum = carve(small, 30, NT), carve(small, 33, NT), carve(small, 36, NT)
            onehot = hit16.bitcast(bf16)[:, :, 0:E0]
            logits = bank[0][:, 0:NT * E0].rearrange("p (k e) -> p k e", e=E0)
            dve.wait_ge(logit_mm[0], 1)
            then(v.tensor_reduce(out=top, in_=logits, axis=AX.X, op=ALU.max))
            v.tensor_tensor(lsub, logits, over_experts(top, E0), ALU.subtract).then_inc(lsub_ready[0], 1)
            dve.wait_ge(lsub_ready[0], 1)
            then(v.tensor_scalar(hit, lsub, 0.0, None, ALU.is_ge))
            then(v.tensor_tensor(hit, hit, const[:, K_REV16:K_REV16 + E0].unsqueeze(1).to_broadcast([P, NT, E0]), ALU.mult))
            then(v.tensor_reduce(out=which, in_=hit, axis=AX.X, op=ALU.max))
            then(v.tensor_tensor(hit, hit, over_experts(which, E0), ALU.is_equal))
            v.tensor_copy(onehot, hit).then_inc(onehot_ready, 1)
            stats(1)
            rank = bank[3][:, 0:NT * E0].rearrange("p (k e) -> p k e", e=E0)
            dve.wait_ge(rank_mm, 1)
            then(v.scalar_tensor_tensor(out=kept, in0=rank, scalar=float(CAP), in1=hit, op0=ALU.is_le, op1=ALU.mult))
            then(v.tensor_tensor(slotval, rank, const[:, K_E32:K_E32 + E0].unsqueeze(1).to_broadcast([P, NT, E0]), ALU.add))
            then(v.tensor_tensor(slotval, slotval, kept, ALU.mult))
            v.tensor_reduce(out=pos, in_=slotval, axis=AX.X, op=ALU.add).then_inc(pos_ready, 1)
            dve.wait_ge(pos_ready, 1)
            for j in range(NT):
                v.tensor_scalar(place[:, j, :], slot_id[:, :], pos[:, j:j + 1], None, ALU.is_equal).then_inc(place_ready, 1)
            dve.wait_ge(lexp_ready[0], NT)
            then(v.tensor_reduce(out=expsum, in_=lexp, axis=AX.X, op=ALU.add))
            v.reciprocal(gate_w, expsum).then_inc(gatew_ready, 1)
            dve.wait_ge(xslot_mm, 2)
            v.tensor_copy(x_slot[:, 1, :], bank[5][:, :]).then_inc(xslot_ready, 1)
            dve.wait_ge(wrow_ready, 1)
            for j in range(4):
                v.scalar_tensor_tensor(out=back[:, j, :], in0=bank[6][:, 0:N], scalar=const[:, K_SLOT + j:K_SLOT + j + 1],
                                       in1=weight_row, op0=ALU.is_equal, op1=ALU.mult).then_inc(back_ready, 1)
            for e4 in range(E0 // 4):
                for c in range(2):
                    dve.wait_ge(innert_mm, 2 * e4 + c + 1)
                    if e4 >= 1:
                        dve.wait_ge(ff2_mm, e4)
                    v.tensor_copy(inner_t[:, 4 * c:4 * c + 4, :].rearrange("p k s -> p (k s)"), bank[4 + c][:, :])\
                        .then_inc(innert_ready, 1)
            for r in range(2):
                dve.wait_ge(combine_mm, r + 1)
                v.tensor_tensor(resid_v[:, r, 0:N], bank[r][:, 0:N], resid_v[:, r, 0:N], ALU.add).then_inc(resid_ready, 1)
            centre(2, resid_v[:, :, 0:N])
            stats(2)
            attention(1)
            centre(3, resid_v[:, :, 0:N])

            lsub, lexp = carve(small, 40, NT, E1), carve(small, 100, NT, E1)
            probs, masked, masked2 = carve(small, 160, NT, E1), carve(small, 200, NT, E1), carve(small, 240, NT, E1)
            hit_a, hit_b = carve(small, 280, NT, E1), carve(small, 320, NT, E1)
            gscore, gscore2 = carve(small, 360, NT, 4), carve(small, 380, NT, 4)
            ghit_a, ghit_b = carve(small, 400, NT, 4), carve(small, 420, NT, 4)
            top2, comb = carve(small, 480, NT), carve(small, 440, NT, E1)
            rev8, rev4 = const[:, K_REV8:K_REV8 + E1], const[:, K_REV4:K_REV4 + 4]
            logits = bank[0][:, 0:NT * E1].rearrange("p (k e) -> p k e", e=E1)
            dve.wait_ge(logit_mm[1], 1)
            then(v.tensor_reduce(out=top, in_=logits, axis=AX.X, op=ALU.max))
            v.tensor_tensor(lsub, logits, over_experts(top, E1), ALU.subtract).then_inc(lsub_ready[1], 1)
            stats(3)
            dve.wait_ge(row_ready, 3)
            v.tensor_tensor(normed_v[:, :, 0:N], normed_v[:, :, 0:N], rstd_row.unsqueeze(1).to_broadcast([P, 2, N]), ALU.mult)\
                .then_inc(normed_ready, 1)
            dve.wait_ge(lexp_ready[1], NT)
            then(v.tensor_reduce(out=expsum, in_=lexp, axis=AX.X, op=ALU.add))
            then(v.reciprocal(gate_w, expsum))
            then(v.tensor_tensor(probs, lexp, over_experts(gate_w, E1), ALU.mult))
            pair = probs.rearrange("p k (g j) -> p k g j", j=2)
            then(v.tensor_tensor(gscore, pair[:, :, :, 0], pair[:, :, :, 1], ALU.max))
            first_max(gscore, top, ghit_a, which, rev4, 4)
            then(v.scalar_tensor_tensor(out=gscore2, in0=ghit_a, scalar=-2.0, in1=gscore, op0=ALU.mult, op1=ALU.add))
            first_max(gscore2, top, ghit_b, which, rev4, 4)
            then(v.tensor_tensor(ghit_a, ghit_a, ghit_b, ALU.add))
            mp = masked.rearrange("p k (g j) -> p k g j", j=2)
            v.tensor_tensor(mp[:, :, :, 0], pair[:, :, :, 0], ghit_a, ALU.mult)
            then(v.tensor_tensor(mp[:, :, :, 1], pair[:, :, :, 1], ghit_a, ALU.mult))
            first_max(masked, top, hit_a, which, rev8, E1)
            then(v.scalar_tensor_tensor(out=masked2, in0=hit_a, scalar=-2.0, in1=masked, op0=ALU.mult, op1=ALU.add))
            first_max(masked2, top2, hit_b, which, rev8, E1)
            v.tensor_tensor(top, top, top2, ALU.add)
            then(v.tensor_tensor(hit_a, hit_a, hit_b, ALU.add))
            v.reciprocal(gate_w, top)
            then(v.tensor_tensor(masked, masked, hit_a, ALU.mult))
            v.tensor_tensor(comb, masked, over_experts(gate_w, E1), ALU.mult).then_inc(comb_ready, 1)
            for n in range(4 * E1):
                if n % 4 == 0:
                    dve.wait_ge(share_ready, n // 4 + 1)
                dve.wait_ge(silu_ready, n + 1)
                v.tensor_tensor(up_gate[n % NG], bank[2 + 2 * (n % 2)][:, 0:N], gate_out[n % NG], ALU.mult).then_inc(upgate_ready, 1)
                dve.wait_ge(upgate_ready, n + 1)
                if n >= NG:
                    dve.wait_ge(down_mm, n - NG + 1)
                v.tensor_tensor(act_in[n % NG], up_gate[n % NG], share[:, n // 4, :], ALU.mult).then_inc(act_ready, 1)
            dve.wait_ge(down_mm, 4 * E1)
            for r in range(2):
                v.tensor_tensor(normed_v[:, r, 0:N], bank[6 + r][:, 0:N], resid_v[:, r, 0:N], ALU.add).then_inc(final_ready, 1)
            for j in range(NT):
                dve.wait_ge(final_mm, j + 1)
                v.tensor_copy(final_tok[:, j, :, :].rearrange("t p r -> t r p"),
                              bank[j][:, 0:D].rearrange("t (r p) -> t r p", r=2)).then_inc(tok_ready, 1)

        @block.tensor
        def _(pe):
            def mm(o, w, x, start, stop, **kw):
                return nc.tensor.matmul(o, w, x, start=start, stop=stop, **kw)

            idle = mean_w[:, :].bitcast(bf16)

            def keep_warm(n, into):
                for _ in range(n):
                    mm(bank[into].rearrange("p (j c) -> p j c", j=2), idle[:, 0:P],
                       idle.unsqueeze(1).to_broadcast([P, 2, 2 * P]), True, True)

            pe.wait_ge(pads_set, 1)
            keep_warm(WARM[0], 7)
            pe.wait_ge(ld_first, 48)
            for c in range(3):
                mm(bank[c][:, :], w_conv12[0:TAPS, 0:P], windows[:, 512 * c:512 * c + 512], True, True).then_inc(conv_mm, 1)
            keep_warm(WARM[1], 7)
            pe.wait_ge(pads_set, 2)
            w2 = carve(w_conv12, P, 3, P)
            odd = h1.rearrange("p (m j) b -> p m j b", j=2)
            for c in range(2):
                pe.wait_ge(conv_out, 2 + 2 * c)
                o = bank[3 + c][:, 0:6 * B].rearrange("p (m b) -> p m b", b=B)
                m0 = 6 * c
                mm(o, w2[:, 1, :], odd[:, m0:m0 + 6, 0, :], True, False)
                if c == 0:
                    mm(o[:, 1:6, :], w2[:, 0, :], odd[:, 0:5, 1, :], False, False)
                else:
                    mm(o, w2[:, 0, :], odd[:, m0 - 1:m0 + 5, 1, :], False, False)
                mm(o, w2[:, 2, :], odd[:, m0:m0 + 6, 1, :], False, True).then_inc(conv_mm, 1)
            keep_warm(WARM[2], 7)
            pe.wait_ge(ld_conv, 16)
            pe.wait_ge(conv_out, 6)
            for r in range(2):
                o = bank[5 + r][:, 0:N].rearrange("p (t b) -> p t b", b=B)
                jobs = []
                for odd_t in range(2):
                    for dd in (2, 3, 0, 1, 4) if not odd_t else range(5):
                        ts = [t for t in range(odd_t, T, 2) if 0 <= first_pair(t) + dd < M2]
                        jobs.append((odd_t, dd, ts))
                for n, (odd_t, dd, ts) in enumerate(jobs):
                    m0 = first_pair(ts[0]) + dd
                    last = m0 + T * (len(ts) - 1)
                    x = h2[:, m0:last + 1:T, :]
                    i = mm(o[:, ts[0]:ts[-1] + 1:2, :], w_conv3[:, 5 * odd_t + dd, r * P:(r + 1) * P], x,
                           n == 0, n == len(jobs) - 1, skip_group_check=True)
                i.then_inc(conv_mm, 1)
            for r in range(2):
                pe.wait_ge(conv_out, 7 + r)
                o = bank[(7, 0)[r]]
                mm(o[:, 0:N], w_conv4[:, 1, r, :], h3[:, r, :], True, False)
                mm(o[:, B:N], w_conv4[:, 0, r, :], h3[:, r, 0:N - B], False, False)
                mm(o[:, 0:N - B], w_conv4[:, 2, r, :], h3[:, r, B:N], False, True).then_inc(conv_mm, 1)
            for kk in range(2):
                pe.wait_ge(conv_out, 9 + kk)
                for r in range(2):
                    i = mm(bank[1 + r][:, 0:N], w_conv5[:, kk, r * P:(r + 1) * P], h4[:, kk, :], kk == 0, kk == 1)
                    if kk == 1:
                        i.then_inc(conv_mm, 1)

            def mean(i, src):
                for kk in range(2):
                    x = mm(bank[7][:, 0:N], mean_w[:, :], src[:, kk, 0:N], kk == 0, kk == 1)
                x.then_inc(mean_mm, 1)

            def sums(i):
                srcs = (squares_v,) if i else (squares_v, resid_v)
                pe.wait_ge(squares_ready, i + 2)
                for n, src in enumerate(srcs):
                    for j in range(NT):
                        for kk in range(2):
                            x = mm(bank[7][:, 3 * n + j:3 * n + j + 1], src[:, kk, j * P:(j + 1) * P], mean_w[:, 0:1], kk == 0, kk == 1)
                x.then_inc(sums_mm, 1)

            def spread_rows(dst, cols):
                for j in range(NT):
                    n = min(P, N - j * P)
                    x = mm(dst[:, j * P:j * P + n], cols[:, j:j + 1].to_broadcast([P, P]), ident[:, 0:n], True, True)
                return x

            def attention(l, w_qkv, ld_qkv, w_proj, ld_proj):
                sets = SETS if l == 0 else 1
                tiles = QKV_TILES[l]
                pe.wait_ge(centred_ready, 1 if l == 0 else 3)
                pe.wait_ge(ld_qkv, 16)
                s_bank = bank[6]
                w = 32 if l == 0 else 8

                def qkv_tile(i):
                    if i >= QKV_BANKS:
                        pe.wait_ge(qkv_dve[l], i - QKV_BANKS + 1)
                    for kk in range(2):
                        x = mm(bank[i % QKV_BANKS][:, 0:N], w_qkv[:, kk, i, :], normed_v[:, kk, 0:N], kk == 0, kk == 1)
                    x.then_inc(qkv_mm[l], 1)
                    if i == 1:
                        sums(0 if l == 0 else 2)
                    if i == 3:
                        pe.wait_ge(rstd_ready, 1 if l == 0 else 3)
                        spread_rows(bank[6], small[:, 16:19]).then_inc(rstd_row_mm, 1)
                        if l == 0:
                            spread_rows(bank[7], small[:, 19:22]).then_inc(rms_row_mm, 1)

                def scores(r, d):
                    m = r * T + d
                    pe.wait_ge(row_ready, l + 1)
                    pe.wait_ge(prod_ready[l], m + 1)
                    p = prods[m % PRODS].rearrange("p s (t b) -> p s t b", b=B)
                    for kap in range(2):
                        for gg in range(4):
                            if l == 0:
                                src = p[:, 2 * (gg // 2) + kap, 0:T - d, (gg % 2) * 32:(gg % 2) * 32 + 32]
                            else:
                                src = p[:, 0, 0:T - d, (2 * gg + kap) * 8:(2 * gg + kap) * 8 + 8]
                            o = s_bank[32 * gg:32 * gg + 32, OFF[d] * w:(OFF[d] + T - d) * w]
                            x = mm(o.rearrange("p (s b) -> p s b", b=w), lane_of[:, r, kap, :], src,
                                   m == 0 and kap == 0, r == 1 and kap == 1, skip_group_check=True,
                                   tile_position=(0, 32 * gg))
                    x.then_inc(score_mm[l], 1)

                for kind, *at in PE_ORDER[l]:
                    (qkv_tile if kind == "t" else scores)(*at)
                keep_warm(WARM[5 + l], 7)
                pe.wait_ge(prob_ready[l], T)
                pe.wait_ge(lane_ready, 1)
                n = PAIRS * w
                pe.wait_ge(qkv_act[l], 2)
                for c in range(16 if l == 0 else 4):
                    if c >= 4:
                        pe.wait_ge(weighted_ready[l], c - 3)
                    for o8 in range(1 if l == 0 else 4):
                        if l == 0:
                            r, (st, half_b) = c // 8, divmod(c % 8, 2)
                            gg, kap = 2 * (st // 2) + half_b, st % 2
                        else:
                            r, quad = divmod(c, 2)
                            gg, kap = divmod(4 * quad + o8, 2)
                        base = 32 * gg + 16 * kap + 8 * r
                        x = mm(bank[c % 4][:, o8 * n:(o8 + 1) * n], lane_to[:, HD * base:HD * base + P],
                               prob[:, 0:n], True, True)
                    x.then_inc(spread_mm[l], 1)
                pe.wait_ge(ld_proj, 16)
                for r in range(2):
                    pe.wait_ge(*((mixed_pool[l], T - 1), (mixed_dve[l], T - 1))[r])
                    for mo in range(2):
                        dst = bank[4 + mo]
                        for st in range(sets):
                            if l == 0:
                                y = weighted[r].rearrange("p (s h c) -> p s h c", s=SETS, h=2)[:, st, :, 0:T * w]
                                y = y.rearrange("p h (t b) -> p t h b", b=w)
                                o = dst[:, 0:N].rearrange("p (t h b) -> p t h b", h=2, b=w)
                            else:
                                y = weighted[r][:, 0:8 * n].rearrange("p (h c) -> p h c", h=8)[:, :, 0:T * w]
                                y = y.rearrange("p h (t b) -> p t h b", b=w)
                                o = dst[:, 0:N].rearrange("p (t h b) -> p t h b", h=8, b=w)
                            x = mm(o, w_proj[:, r, st, mo * P:(mo + 1) * P], y, r == 0 and st == 0, r == 1 and st == sets - 1)
                        if r == 1:
                            x.then_inc(proj_mm[l], 1)

            def logits(l, n, w):
                for j in range(NT):
                    for kk in range(2):
                        x = mm(bank[0][:, j * n:(j + 1) * n], normed_v[:, kk, j * P:(j + 1) * P], w[:, kk, :], kk == 0, kk == 1)
                x.then_inc(logit_mm[l], 1)

            pe.wait_ge(pads_set, 4)
            pe.wait_ge(ld_const, 16)
            keep_warm(WARM[3], 3)
            pe.wait_ge(rope_done, 1)
            mean(0, turned)
            keep_warm(WARM[4], 3)
            attention(0, carve(w_qkv0, 0, 2, 12, P), ld_qkv0, carve(w_proj0, 0, 2, SETS, D), ld_proj0)
            keep_warm(WARM[7], 3)
            pe.wait_ge(resid_ready, 2)
            mean(1, resid_v)
            keep_warm(WARM[8], 3)
            pe.wait_ge(centred_ready, 2)
            pe.wait_ge(ld_gates, 16)
            logits(0, E0, carve(w_gates, 0, 2, E0))
            for j in range(NT):
                for r in range(2):
                    x = nc.tensor.transpose(bank[1 + j // 2][:, (j % 2) * D + r * P:(j % 2) * D + (r + 1) * P],
                                            normed_v[:, r, j * P:(j + 1) * P], ident)
            x.then_inc(xtok_mm, 1)
            sums(1)
            keep_warm(WARM[9], 6)
            pe.wait_ge(onehot_ready, 1)
            onehot = carve(small, 340, NT, E0).bitcast(bf16)[:, :, 0:E0]
            for j in range(NT):
                for jj in range(NT):
                    x = mm(bank[3][:, j * E0:(j + 1) * E0], before[:, jj * NP + j * P:jj * NP + (j + 1) * P], onehot[:, jj, :],
                           jj == 0, jj == NT - 1)
            x.then_inc(rank_mm, 1)
            keep_warm(WARM[10], 6)
            pe.wait_ge(xtok_ready, NT)
            pe.wait_ge(place_ready, NT)
            for r in range(2):
                for j in range(NT):
                    x = mm(bank[4 + r][:, :], x_tok[:, j, r * P:(r + 1) * P], place[:, j, :], j == 0, j == NT - 1)
                x.then_inc(xslot_mm, 1)
            pe.wait_ge(gatew_ready, 1)
            spread_rows(bank[6], small[:, 30:33]).then_inc(row_mm, 1)
            spread_rows(bank[7], small[:, 33:36]).then_inc(row_mm, 1)
            pe.wait_ge(xslot_ready, 2)

            def expert(e):
                s = (e % RING) * W0_COLS
                return carve(ring, s, 2, F0), carve(ring, s + 2 * F0, F0 // P, D)

            def up(e4):
                for j in range(4):
                    e = 4 * e4 + j
                    pe.wait_ge(ld_up[e % RING], 16 * (e // RING + 1))
                if e4 >= 2:
                    pe.wait_ge(inner_ready, 2 * (e4 - 1))
                for c in range(2):
                    for kk in range(2):
                        for j in range(4):
                            e = 4 * e4 + j
                            x = mm(bank[2 * (e4 % 2) + c][32 * j:32 * j + 32, :], x_slot[:, kk, SLOT * e:SLOT * e + SLOT],
                                   expert(e)[0][:, kk, 512 * c:512 * c + 512], kk == 0, kk == 1, tile_position=(0, 32 * j))
                    x.then_inc(ff1_mm, 1)

            def down(e4):
                if e4 == 0:
                    pe.wait_ge(back_ready, 4)
                for c in range(2):
                    pe.wait_ge(inner_ready, 2 * e4 + c + 1)
                    if e4 >= 1:
                        pe.wait_ge(innert_ready, 2 * (e4 - 1) + c + 1)
                    for kk in range(4):
                        at = 512 * c + P * kk
                        x = nc.tensor.transpose(bank[4 + c][:, P * kk:P * kk + P], inner[e4 % 2][:, at:at + P], ident)
                    x.then_inc(innert_mm, 1)
                if e4 >= 2:
                    pe.wait_ge(yslot_ready, e4 - 1)
                for j in range(4):
                    e = 4 * e4 + j
                    pe.wait_ge(ld_down[e % RING], 16 * (e // RING + 1))
                for kk in range(F0 // P):
                    if kk % 4 == 0:
                        pe.wait_ge(innert_ready, 2 * e4 + kk // 4 + 1)
                    for j in range(4):
                        x = mm(bank[6 + e4 % 2][32 * j:32 * j + 32, 0:D], inner_t[:, kk, 32 * j:32 * j + 32],
                               expert(4 * e4 + j)[1][:, kk, :], kk == 0, kk == F0 // P - 1, tile_position=(0, 32 * j))
                x.then_inc(ff2_mm, 1)

            up(0)
            for e4 in range(E0 // 4):
                if e4 < E0 // 4 - 1:
                    up(e4 + 1)
                down(e4)
            pe.wait_ge(yslot_ready, 4)
            for r in range(2):
                for j in range(4):
                    x = mm(bank[r][:, 0:N], y_slot[:, j, r * P:(r + 1) * P], back[:, j, :], j == 0, j == 3)
                x.then_inc(combine_mm, 1)
            keep_warm(WARM[11], 3)
            pe.wait_ge(resid_ready, 4)
            mean(2, resid_v)
            keep_warm(WARM[12], 3)
            attention(1, carve(w_qkv1, 0, 2, 6, P), ld_qkv1, carve(w_proj1, 0, 2, 1, D), ld_proj1)
            keep_warm(WARM[13], 3)
            pe.wait_ge(resid_ready, 6)
            mean(3, resid_v)
            keep_warm(WARM[14], 3)
            pe.wait_ge(centred_ready, 4)
            logits(1, E1, carve(w_gates, 2 * E0, 2, E1))
            sums(3)
            pe.wait_ge(rstd_ready, 4)
            spread_rows(bank[6], small[:, 16:19]).then_inc(rstd_row_mm, 1)
            pe.wait_ge(normed_ready, 1)

            def gate_up(n):
                e, it = divmod(n, 4)
                if it == 0:
                    pe.wait_ge(ld_up[e], 48)
                if n >= 2:
                    pe.wait_ge(upgate_ready, n - 1)
                w = carve(ring, e * W0_COLS, 2, 2 * (F1 // P), P)
                for kind in range(2):
                    for kk in range(2):
                        x = mm(bank[1 + 2 * (n % 2) + kind][:, 0:N], w[:, kk, kind * (F1 // P) + it, :], normed_v[:, kk, 0:N],
                               kk == 0, kk == 1)
                x.then_inc(gate_mm, 1)

            def down1(n):
                e, it = divmod(n, 4)
                w = carve(ring, e * W0_COLS + 4 * F1, F1 // P, D)
                pe.wait_ge(act_ready, n + 1)
                for r in range(2):
                    x = mm(bank[6 + r][:, 0:N], w[:, it, r * P:(r + 1) * P], act_in[n % NG], n == 0, n == 4 * E1 - 1)
                x.then_inc(down_mm, 1)

            gate_up(0)
            gate_up(1)
            pe.wait_ge(comb_ready, 1)
            comb = carve(small, 440, NT, E1)
            for e in range(E1):
                if e >= 2:
                    pe.wait_ge(share_ready, e - 1)
                for j in range(NT):
                    n = min(P, N - j * P)
                    x = mm(bank[5 * (e % 2)][:, j * P:j * P + n], comb[:, j, e:e + 1].to_broadcast([P, P]), ident[:, 0:n], True, True)
                x.then_inc(share_mm, 1)
            for n in range(4 * E1):
                if n + 2 < 4 * E1 and n >= 0:
                    pass
                if n >= 1 and n + 1 < 4 * E1:
                    gate_up(n + 1)
                down1(n)
            pe.wait_ge(final_ready, 2)
            for j in range(NT):
                for r in range(2):
                    x = nc.tensor.transpose(bank[j][:, r * P:(r + 1) * P], normed_v[:, r, j * P:(j + 1) * P], ident)
                x.then_inc(final_mm, 1)


def first_pair(t):
    return (5 * t - 4) // 2


def layouts(x, w1, b1, w2, b2, w3, b3, w4, b4, w5, b5, freqs, norm_w, attn0, proj0, gate0, up0, down0, attn1, proj1, gate1, w13, down1):
    f = np.float32
    perm = np.arange(D).reshape(P, 2).T
    arr = {}
    vec = np.zeros((P, NVEC), f)
    vec[:, CB1] = np.tile(b1, 4)
    vec[:, CB2] = np.tile(b2, 2)
    vec[:, CB3:CB3 + 2] = b3.reshape(2, P).T
    vec[:, CB4:CB4 + 2] = b4.reshape(2, P).T
    vec[:, CB5:CB5 + 2] = b5[perm].T
    vec[:, CNW:CNW + 2] = norm_w[perm].T
    vec[:, CFR] = np.tile(freqs, P // (HD // 2))
    arr["vec"] = vec
    pad = np.zeros((B, 32 * (G1 - 1) + TAPS), f)
    pad[:, 7:7 + x.shape[2]] = x[:, 0, :]
    arr["windows"] = np.stack([pad[:, i:i + 32 * (G1 - 1) + 1:32].T for i in range(TAPS)]).reshape(TAPS, G1 * B)
    c12 = np.zeros((P, 4 * P), f)
    for j in range(4):
        c12[8 * j:8 * j + 15, 32 * j:32 * j + 32] = w1[:, 0, :].T
    c2 = c12[:, P:].reshape(4, C1, 3, 2, C2)
    for j in range(4):
        if j >= 1:
            c2[j, :, 0, 0, :] = w2[:, :, j - 1].T
            c2[j, :, 1, 1, :] = w2[:, :, j - 1].T
        c2[j, :, 1, 0, :] = w2[:, :, j + 3].T
        c2[j, :, 2, 1, :] = w2[:, :, j + 3].T
    arr["w_conv12"] = c12
    c3 = np.zeros((2, C2, 2, 5, D), f)
    for par in range(2):
        for d in range(5):
            if 2 * d + par <= 8:
                c3[par, :, 0, d, :] = w3[:, :, 2 * d + par].T
            if 2 * d + par >= 1:
                c3[par, :, 1, d, :] = w3[:, :, 2 * d + par - 1].T
    c4 = np.zeros((P, 3, 2, P), f)
    for o in range(D):
        r, oc = divmod(o, P)
        c4[oc // 8 * 8:oc // 8 * 8 + 8, :, r, oc] = w4[o]
    c5 = w5[:, :, 0][perm].transpose(2, 0, 1).reshape(2, P, D).transpose(1, 0, 2)
    arr["w_conv345"] = np.concatenate([c3.reshape(P, -1), c4.reshape(P, -1), c5.reshape(P, -1)], axis=1)
    a0 = attn0.reshape(SETS + 2, 2, P, D)
    tiles = [a0[j, r] for r in range(2) for j in [SETS] + list(range(SETS))] + [a0[SETS + 1, r] for r in range(2)]
    arr["w_qkv0"] = np.stack(tiles)[:, :, perm].transpose(3, 2, 0, 1).reshape(P, -1)
    arr["w_proj0"] = proj0[perm].reshape(2, P, SETS, 2, P).transpose(4, 3, 2, 0, 1).reshape(P, -1)
    a1 = attn1.T.reshape(3, 2, P, D)
    tiles = [a1[j, r] for r in range(2) for j in (1, 0)] + [a1[2, r] for r in range(2)]
    arr["w_qkv1"] = np.stack(tiles)[:, :, perm].transpose(3, 2, 0, 1).reshape(P, -1)
    arr["w_proj1"] = proj1[:, perm].reshape(2, P, 2, P).transpose(1, 0, 2, 3).reshape(P, -1)
    arr["w_gates"] = np.concatenate([gate0[:, perm].transpose(2, 1, 0).reshape(P, -1), gate1[:, perm].transpose(2, 1, 0).reshape(P, -1)], axis=1)
    ups = up0[:, perm, :].transpose(0, 2, 1, 3).reshape(E0, P, -1)
    downs = down0[:, :, perm].reshape(E0, F0 // P, P, D).transpose(0, 2, 1, 3).reshape(E0, P, -1)
    arr["w_exp0"] = np.concatenate([ups, downs], axis=2)
    ups = w13[:, :, perm].transpose(0, 3, 2, 1).reshape(E1, P, -1)
    downs = down1[:, perm, :].transpose(0, 3, 1, 2).reshape(E1, F1 // P, P, D).transpose(0, 2, 1, 3).reshape(E1, P, -1)
    arr["w_exp1"] = np.concatenate([ups, downs], axis=2)
    const = np.zeros((P, NCONST), f)
    const[:, K_ID:K_ID + P] = np.eye(P)
    lanes = const[:, K_IND:K_IND + P].reshape(P, 2, 2, 32)
    for p in range(P):
        for r in range(2):
            for kap in range(2):
                lanes[p, r, kap, 16 * kap + 8 * r + p // HD] = 1
    const[:, K_REV16:K_REV16 + E0] = E0 - np.arange(E0)
    const[:, K_E32:K_E32 + E0] = SLOT * np.arange(E0)
    const[:, K_REV8:K_REV8 + E1] = E1 - np.arange(E1)
    const[:, K_REV4:K_REV4 + 4] = 4 - np.arange(4)
    const[:, K_SLOT:K_SLOT + 4] = 1 + np.arange(4 * P).reshape(4, P).T
    key = np.full(NP, 2 * FAR)
    key[:N] = (np.arange(B)[None, :] * T + np.arange(T)[:, None]).ravel()
    const[:, K_KEY:K_KEY + NT] = key.reshape(NT, P).T
    const[:, K_T:K_T + T] = np.arange(T)
    arr["const"] = const
    return {n: np.ascontiguousarray(v, dtype=f) for n, v in arr.items()}


def kernel(x, L0_tok_w1, L0_tok_b1, L0_tok_w2, L0_tok_b2, L0_tok_w3, L0_tok_b3, L0_tok_w4, L0_tok_b4, L0_tok_w5, L0_tok_b5,
           L0_tok_rope_freqs, L0_tok_norm_w, L0_attn_W_attn, L0_attn_W_proj, L0_ffn_gate_w, L0_ffn_w1, L0_ffn_w2,
           L1_attn_W_attn, L1_attn_W_proj, L1_ffn_gate_w, L1_ffn_w13_weight, L1_ffn_w2_weight):
    import concourse.bacc as bacc
    from concourse.bass_utils import run_bass_kernel_spmd

    arrays = layouts(*(np.asarray(v) for v in (
        x, L0_tok_w1, L0_tok_b1, L0_tok_w2, L0_tok_b2, L0_tok_w3, L0_tok_b3, L0_tok_w4, L0_tok_b4, L0_tok_w5, L0_tok_b5,
        L0_tok_rope_freqs, L0_tok_norm_w, L0_attn_W_attn, L0_attn_W_proj, L0_ffn_gate_w, L0_ffn_w1, L0_ffn_w2,
        L1_attn_W_attn, L1_attn_W_proj, L1_ffn_gate_w, L1_ffn_w13_weight, L1_ffn_w2_weight)))
    nc = bacc.Bacc("TRN2", target_bir_lowering=False, num_devices=1)
    aps = {n: nc.dram_tensor(f"in_{n}", v.shape, mybir.dt.from_np(v.dtype), kind="ExternalInput").ap() for n, v in arrays.items()}
    out = nc.dram_tensor("tokens_out", (B, T, D), mybir.dt.float32, kind="ExternalOutput").ap()
    audio_tower(nc, aps, out)
    r = run_bass_kernel_spmd(nc, [{f"in_{n}": v for n, v in arrays.items()}], core_ids=[0])
    return r.results[0]["tokens_out"]
```

```python
import math
from contextlib import ExitStack

import numpy as np

import concourse.bass as bass
from concourse import mybir

P = 128
B, T = 64, 5
N = B * T
NP = 384
NT = NP // P
D = 256
C1, C2 = 32, 64
G1 = 24
TAPS = 39
POS1 = 94
M2 = 12
HEADS, HD = 16, 16
SETS = 4
E0, F0, CAP = 16, 1024, 26
SLOT = 32
E1, F1 = 8, 512
PAIRS = T * (T + 1) // 2
OFF = [sum(T - i for i in range(d)) for d in range(T)]
LN_EPS, RMS_EPS = 1e-5, 1e-8
SCALE = 1.0 / math.sqrt(HD)
TWO_PI_HI, TWO_PI_LO = 6.28125, 2 * math.pi - 6.28125
ROUND = 1.5 * 2.0 ** 23
BIG = 3.0e38
FAR = 4096.0

W0_COLS = 2 * F0 + (F0 // P) * D
W1_COLS = 2 * 2 * F1 + (F1 // P) * D
PIECE = W1_COLS // (F1 // P)
GATE_UP = ((1, 2), (3, 4), (5, 0))
SHARE_BANK = (6, 7, 5, 0)
FIRST, REST = slice(0, 4 * SLOT), slice(4 * SLOT, E0 * SLOT)
RING = 8
WARM = [9, 6, 4, 13, 5, 30, 18, 3, 5, 0, 2, 3, 5, 3, 5, 6, 0, 0, 0, 0, 0, 2]

CB1, CB2, CB3, CB4, CB5, CNW, CFR, NVEC = 0, 1, 2, 4, 6, 8, 10, 11
K_ID, K_IND, K_REV16, K_E32, K_REV8, K_REV4, K_SLOT, K_KEY, K_T = 0, 128, 256, 272, 288, 296, 300, 304, 307
NCONST = 312


def audio_tower(nc: bass.Bass, a: dict, out: bass.AP):
    f32, bf16 = mybir.dt.float32, mybir.dt.bfloat16
    ALU, ACT, AX = mybir.AluOpType, mybir.ActivationFunctionType, mybir.AxisListType

    with ExitStack() as ctx:
        def sb(name, cols, dt=f32):
            return ctx.enter_context(nc.sbuf_tensor(name, [P, cols], dt))

        def sem(name):
            return ctx.enter_context(nc.semaphore(name))

        bank = [ctx.enter_context(nc.psum_tensor(f"bank{i}", [P, 512], f32)) for i in range(8)]

        ring_a = sb("ring_a", RING // 2 * W0_COLS)
        vec = sb("vec", NVEC)
        const = sb("const", NCONST)
        with ExitStack() as first:
            w_conv12, w_qkv0 = (first.enter_context(nc.sbuf_tensor(name, [P, cols], f32))
                                for name, cols in (("w_conv12", P + 3 * P), ("w_qkv0", 2 * 12 * P)))
        f32r = mybir.dt.float32r
        with ExitStack() as first:
            lane_to = first.enter_context(nc.sbuf_tensor("lane_to", [P, P * HD], f32r))
        extra_up = sb("extra_up", 2 * F0)
        extra = sb("extra", W0_COLS)
        w_proj0 = sb("w_proj0", 2 * SETS * D)
        w_qkv1, w_proj1 = extra[:, 0:2 * 6 * P], extra[:, 2 * 6 * P:2 * 6 * P + 2 * D]
        w_gates = sb("w_gates", 2 * (E0 + E1))
        mean_w = sb("mean_w", P)
        key_row = sb("key_row", NP)
        before = sb("before", NT * NP, bf16)
        resid = sb("resid", 2 * NP)
        normed = sb("normed", 2 * NP)
        squares = sb("squares", 2 * NP)
        small = sb("small", 512)
        prob_hi, prob_lo = (sb(f"prob_{part}", 480, f32r) for part in ("hi", "lo"))
        arena = sb("arena", 6880)

        def carve(t, at, *dims):
            n = 1
            for d in dims:
                n *= d
            v = t[:, at:at + n]
            if len(dims) == 1:
                return v
            names = [f"a{i}" for i in range(len(dims))]
            return v.rearrange(f"p ({' '.join(names)}) -> p {' '.join(names)}",
                               **{n: d for n, d in zip(names[1:], dims[1:])})

        with ExitStack() as first:
            ring_b = first.enter_context(nc.sbuf_tensor("ring_b", [P, RING // 2 * W0_COLS], f32))
        PIECES, AHEAD = 8, 4
        w_hi, w_lo = (sb(f"w_{part}", PIECES * PIECE, f32r) for part in ("hi", "lo"))
        NG = 3
        x_hi, x_lo = (sb(f"x_{part}", 2 * N, f32r) for part in ("hi", "lo"))
        act_hi, act_lo = (sb(f"act_{part}", NG * N, f32r) for part in ("hi", "lo"))

        def slot(s):
            if s == RING:
                return extra[:, :]
            ring = (ring_a, ring_b)[s // (RING // 2)]
            return ring[:, s % (RING // 2) * W0_COLS:(s % (RING // 2) + 1) * W0_COLS]

        PREFETCHED = RING + 2

        def home(e):
            return (e, 1) if e < PREFETCHED else (e - PREFETCHED, 2)

        def expert_cols(e, part, at=0, n=2 * F0):
            if home(e)[0] == RING + 1:
                return (extra_up, w_proj0)[part][:, at:at + n]
            return slot(home(e)[0])[:, 2 * F0 * part + at:2 * F0 * part + at + n]

        def piece(parts, k):
            return carve(parts, k % PIECES * PIECE, PIECE)

        def raw_piece(k):
            return carve(ring_a, k // 4 % 4 * W0_COLS + k % 4 * PIECE, PIECE)

        resid_v, squares_v, normed_v = (carve(x, 0, 2, NP) for x in (resid, squares, normed))
        ident = const[:, K_ID:K_ID + P]
        lane_of = carve(const, K_IND, 2, 2, 32)

        w_conv3 = carve(slot(6), 0, 10, D)
        w_conv4 = carve(slot(6), 10 * D, 3, 2, P)
        w_conv5 = carve(slot(6), 10 * D + 6 * P, 2, D)
        windows = arena[:, 0:G1 * B]
        h1 = carve(arena, 1536, G1, B)
        h2 = carve(arena, 3072, M2, B)
        h3 = carve(arena, 3840, 2, N)
        h4 = carve(arena, 4480, 2, N)
        h5 = carve(arena, 5120, 2, N)
        turned = carve(arena, 5760, 2, N)
        crossed = carve(arena, 0, 2, N)
        sincos = carve(arena, 6400, 2, T)
        angles = carve(arena, 6416, 2, T)
        cos_w = carve(arena, 6432, 2, T)
        sin_w = carve(arena, 6448, 2, T)

        rstd_row = squares[:, 0:N]
        PRODS = 3
        PARTS = (2, 1)
        q = [carve(arena, 0, 2, SETS, N), carve(arena, 0, 2, 1, N)]
        k = [carve(arena, 2560, 2, N), carve(arena, 640, 2, N)]
        values = [carve(arena, 3840, 2, N), carve(arena, 1280, 2, N)]
        vx = [carve(arena, 4480, 2, PAIRS, B), carve(arena, 1920, 2, PAIRS, B)]
        score = [arena[:, 6400:6880], arena[:, 6720:6840]]
        lane_rstd = [arena[:, 3680:3840], arena[:, 4880:4920]]
        peak, total, inv = ([arena[:, at:at + 160], arena[:, at1:at1 + 40]] for at, at1 in ((3200, 6840), (3360, 4800), (3520, 4840)))
        prods = [[carve(slot(7), i * SETS * N, SETS, N) for i in range(PRODS)],
                 [carve(arena, 3840 + i * N, 1, N) for i in range(PRODS)]]
        weighted = [[slot(7)[:, 0:3840], arena[:, 0:3840]], [arena[:, 4800:5760], arena[:, 5760:6720]]]

        x_tok = carve(arena, 4608, NT, D)
        slot_id = arena[:, 2048:2048 + E0 * SLOT]
        place = carve(arena, 3072, NT, E0 * SLOT)
        x_slot = carve(arena, 0, 2, E0 * SLOT)
        inner = [carve(arena, 1024 + i * F0, F0) for i in range(2)]
        inner_t = carve(arena, 3072, F0 // P, P)
        y_slot = carve(arena, 4096, 4, D)
        back = carve(arena, 5120, 4, N)
        weight_row = carve(arena, 6400, N)

        share = carve(arena, 0, E1, N)
        gate_out = [carve(arena, 2560 + i * N, N) for i in range(NG)]
        gate_share = [carve(arena, 3520 + i * N, N) for i in range(NG)]
        act_in = [carve(arena, 4480 + i * N, N) for i in range(NG)]
        final_tok = carve(w_proj0, 0, NT, P, 2)

        ld_first, ld_const, ld_conv, ld_qkv0, ld_proj0, ld_gates, ld_qkv1, ld_proj1 = (
            sem(n) for n in ("ld_first", "ld_const", "ld_conv", "ld_qkv0", "ld_proj0", "ld_gates", "ld_qkv1", "ld_proj1"))
        ld_up = [sem(f"ld_up{i}") for i in range(RING + 2)]
        ld_down = [sem(f"ld_down{i}") for i in range(RING + 2)]
        ld_down_b = [sem(f"ld_down_b{i}") for i in range(4)]
        ld_exp1 = [sem(f"ld_exp1_{i}") for i in range(RING // 2)]
        stored = sem("stored")
        rows_cleared, last_rows_cleared = sem("rows_cleared"), sem("last_rows_cleared")
        lane_rstd_mm = [sem(f"lane_rstd_mm{l}") for l in range(2)]
        lane_rstd_ready = [sem(f"lane_rstd_ready{l}") for l in range(2)]
        factor_ready = [sem(f"factor_ready{l}") for l in range(2)]
        hi_ready, lo_ready, xfull_ready, xhi_ready, xlo_ready, acthi_ready, actlo_ready, gshare_ready = (
            sem(n) for n in ("hi_ready", "lo_ready", "xfull_ready", "xhi_ready", "xlo_ready", "acthi_ready", "actlo_ready", "gshare_ready"))
        combt_mm, comb_hi_ready, comb_lo_ready = sem("combt_mm"), sem("comb_hi_ready"), sem("comb_lo_ready")
        pads_set, iotas, lane_ready, slot_ids = sem("pads_set"), sem("iotas"), sem("lane_ready"), sem("slot_ids")
        prob_hi_ready, prob_lo_ready = ([sem(f"prob_{part}_ready{l}") for l in range(2)] for part in ("hi", "lo"))
        conv_mm, conv_out = sem("conv_mm"), sem("conv_out")
        angle_ready, sincos_ready, rope_done = sem("angle_ready"), sem("sincos_ready"), sem("rope_done")
        resid_ready = sem("resid_ready")
        normed_ready = sem("normed_ready")
        mean_mm, centred_ready, squares_ready, sums_mm = (sem(n) for n in ("mean_mm", "centred_ready", "squares_ready", "sums_mm"))
        var_ready, std_ready, rstd_ready, row_ready, rms_row_mm, rstd_row_mm = (
            sem(n) for n in ("var_ready", "std_ready", "rstd_ready", "row_ready", "rms_row_mm", "rstd_row_mm"))
        qkv_mm = [sem(f"qkv_mm{l}") for l in range(2)]
        qkv_out = [sem(f"qkv_out{l}") for l in range(2)]
        prod_ready = [sem(f"prod_ready{l}") for l in range(2)]
        score_mm = [sem(f"score_mm{l}") for l in range(2)]
        shifted_ready = [sem(f"shifted_ready{l}") for l in range(2)]
        exp_ready = [sem(f"exp_ready{l}") for l in range(2)]
        prob_ready = [sem(f"prob_ready{l}") for l in range(2)]
        vx_ready = [sem(f"vx_ready{l}") for l in range(2)]
        spread_mm = [sem(f"spread_mm{l}") for l in range(2)]
        weighted_ready = [sem(f"weighted_ready{l}") for l in range(2)]
        mixed_pool = [sem(f"mixed_pool{l}") for l in range(2)]
        mixed_dve = [sem(f"mixed_dve{l}") for l in range(2)]
        proj_mm = [sem(f"proj_mm{l}") for l in range(2)]
        logit_mm = [sem(f"logit_mm{l}") for l in range(2)]
        lsub_ready = [sem(f"lsub_ready{l}") for l in range(2)]
        lexp_ready = [sem(f"lexp_ready{l}") for l in range(2)]
        xtok_mm, xtok_ready, onehot_ready, rank_mm, pos_ready, gatew_ready = (
            sem(n) for n in ("xtok_mm", "xtok_ready", "onehot_ready", "rank_mm", "pos_ready", "gatew_ready"))
        place_ready, xslot_mm, xslot_ready, row_mm, wrow_ready, back_ready = (
            sem(n) for n in ("place_ready", "xslot_mm", "xslot_ready", "row_mm", "wrow_ready", "back_ready"))
        ff1_mm, inner_ready, innert_mm, innert_ready, ff2_mm, yslot_ready, combine_mm = (
            sem(n) for n in ("ff1_mm", "inner_ready", "innert_mm", "innert_ready", "ff2_mm", "yslot_ready", "combine_mm"))
        comb_ready, share_mm, gate_mm, silu_ready, act_ready, down_mm = (
            sem(n) for n in ("comb_ready", "share_mm", "gate_mm", "silu_ready", "act_ready", "down_mm"))
        share_ready = [sem(f"share_ready_{bank_of}") for bank_of in (6, 7)]
        final_ready, final_mm, tok_ready = sem("final_ready"), sem("final_mm"), sem("tok_ready")
        dve_step, pool_step = sem("dve_step"), sem("pool_step")

        QKV_TILES = [12, 6]
        QKV_BANKS = 5
        PE_ORDER = [
            [("t", 0), ("t", 1), ("sums",), ("warm", WARM[20]), ("t", 2), ("spread",), ("t", 3), ("lanes",), ("t", 4), ("t", 5), ("t", 6),
             ("s", 0, 0), ("t", 7), ("s", 0, 1), ("t", 8), ("s", 0, 2), ("t", 9), ("s", 0, 3), ("s", 0, 4), ("t", 10), ("t", 11)]
            + [("warm", WARM[18])] + [x for d in range(T) for x in (("s", 1, d), ("warm", WARM[19]))],
            [("t", 0), ("t", 1), ("sums",), ("t", 2), ("spread",), ("t", 3), ("lanes",), ("s", 0, 0), ("s", 0, 1), ("s", 0, 2), ("t", 4),
             ("s", 0, 3), ("s", 0, 4), ("s", 1, 0), ("s", 1, 1), ("t", 5), ("s", 1, 2), ("s", 1, 3), ("s", 1, 4)]]

        def qkv_dst(l, i):
            per = 1 + (SETS if l == 0 else 1)
            if i >= 2 * per:
                return values[l][:, i - 2 * per, :]
            r, j = divmod(i, per)
            return k[l][:, r, :] if j == 0 else q[l][:, r, j - 1, :]

        block = ctx.enter_context(nc.Block())

        @block.sync
        def _(sp):
            sp.dma_start(vec[:, :], a["vec"]).then_inc(ld_first, 16)
            sp.dma_start(w_conv12[:, :], a["w_conv12"]).then_inc(ld_first, 16)
            sp.wait_ge(rows_cleared, 1)
            sp.dma_start(windows[0:TAPS, :], a["windows"]).then_inc(ld_first, 16)
            sp.dma_start(const[:, :], a["const"]).then_inc(ld_const, 16)
            sp.dma_start(slot(6)[:, 0:10 * D + 6 * P + 2 * D], a["w_conv345"]).then_inc(ld_conv, 16)
            sp.dma_start(w_qkv0[:, :], a["w_qkv0"]).then_inc(ld_qkv0, 16)
            sp.dma_start(w_proj0[:, :], a["w_proj0"]).then_inc(ld_proj0, 16)
            sp.dma_start(w_gates[:, :], a["w_gates"]).then_inc(ld_gates, 16)
            def load_exp0(e, part):
                sp.dma_start(expert_cols(e, part), a["w_exp0"][e][:, 2 * F0 * part:2 * F0 * (part + 1)])\
                    .then_inc((ld_up, ld_down)[part][home(e)[0]], 16)

            for es in ((0, 1, 2, 3), (4, 5)):
                for part in range(2):
                    for e in es:
                        load_exp0(e, part)
            sp.wait_ge(conv_mm, 11)
            load_exp0(6, 0)
            load_exp0(6, 1)
            sp.wait_ge(qkv_mm[0], 12)
            load_exp0(8, 0)
            load_exp0(8, 1)
            sp.wait_ge(spread_mm[0], 16)
            load_exp0(9, 0)
            sp.wait_ge(proj_mm[0], 2)
            load_exp0(7, 0)
            load_exp0(7, 1)
            load_exp0(9, 1)
            sp.wait_ge(ff1_mm, 2)
            for e in range(10, 14):
                load_exp0(e, 0)
            sp.wait_ge(ff2_mm, 1)
            for e in range(10, 12):
                load_exp0(e, 1)
            sp.wait_ge(ff1_mm, 4)
            for e in range(14, 16):
                load_exp0(e, 0)
            sp.wait_ge(ff2_mm, 2)
            for half in range(2):
                for e in range(12, 16):
                    sp.dma_start(expert_cols(e, 1, half * F0, F0), a["w_exp0"][e][:, (2 + half) * F0:(3 + half) * F0])\
                        .then_inc(ld_down_b[e - 12] if half else ld_down[home(e)[0]], 16)
            sp.wait_ge(ff2_mm, 3)
            sp.dma_start(w_qkv1, a["w_qkv1"]).then_inc(ld_qkv1, 16)
            sp.dma_start(w_proj1, a["w_proj1"]).then_inc(ld_proj1, 16)
            for e in range(E1):
                if e == 2:
                    sp.wait_ge(ff2_mm, 4)
                if e >= RING // 2:
                    sp.wait_ge(hi_ready, 4 * (e - RING // 2 + 1))
                    sp.wait_ge(lo_ready, 4 * (e - RING // 2 + 1))
                sp.dma_start(slot(e % (RING // 2))[:, 0:W1_COLS], a["w_exp1"][e]).then_inc(ld_exp1[e % (RING // 2)], 16)
            for t in range(T):
                sp.wait_ge(tok_ready, t // 2 + 1)
                rows = slice(B * (t % 2), B * (t % 2) + B)
                sp.dma_start(out[:, t, :], final_tok[rows, t // 2, :, :].rearrange("b p r -> b (p r)")).then_inc(stored, 16)
            sp.wait_ge(stored, 16 * T)

        @block.gpsimd
        def _(pool):
            g = nc.gpsimd
            g.memset(mean_w[:, :], 1.0 / D).then_inc(pads_set, 1)
            pool.wait_ge(pads_set, 1)
            g.memset(windows[64:P, :], 0.0).then_inc(last_rows_cleared, 1)
            pool.wait_ge(last_rows_cleared, 1)
            g.memset(h1[:, G1 - 1, :], 0.0).then_inc(pads_set, 1)
            for v in (resid_v, squares_v, normed_v):
                g.memset(v[:, :, N:NP], 0.0).then_inc(pads_set, 1)
            g.iota(key_row[:, 0:N].rearrange("p (t b) -> p t b", b=B), [[1, T], [T, B]], base=0, channel_multiplier=0,
                   allow_small_or_imprecise_dtypes=True).then_inc(iotas, 1)
            g.memset(key_row[:, N:NP], FAR).then_inc(iotas, 1)

            def attention(l, width):
                pool.wait_ge(lane_rstd_ready[l], 1)
                for d in range(T):
                    g.tensor_tensor(score[l][:, OFF[d] * width:(OFF[d] + T - d) * width], lane_rstd[l][:, d * width:T * width],
                                    lane_rstd[l][:, 0:(T - d) * width], ALU.mult).then_inc(factor_ready[l], 1)
                pool.wait_ge(qkv_out[l], QKV_TILES[l])
                for d in range(T):
                    n = (T - d) * B
                    g.tensor_tensor(vx[l][:, :, OFF[d]:OFF[d] + T - d, :].rearrange("p r s b -> p r (s b)"), values[l][:, :, 0:n],
                                    rstd_row[:, 0:n].unsqueeze(1).to_broadcast([P, 2, n]), ALU.mult).then_inc(vx_ready[l], 1)
                w = weighted[l][0].rearrange("p (c s) -> p c s", c=8)
                for part in range(PARTS[l]):
                    n = 8 // PARTS[l]
                    pool.wait_ge(weighted_ready[l], (4, 2)[l] * (part + 1))
                    for d in range(1, T):
                        dst = w[:, part * n:(part + 1) * n, d * width:T * width]
                        g.tensor_tensor(dst, dst, w[:, part * n:(part + 1) * n, OFF[d] * width:(OFF[d] + T - d) * width], ALU.add)\
                            .then_inc(mixed_pool[l], 1)
                        pool.wait_ge(mixed_pool[l], (T - 1) * part + d)
            attention(0, 32)
            pool.wait_ge(proj_mm[0], 2)
            g.iota(slot_id, [[1, E0 * SLOT]], base=1, channel_multiplier=0,
                   allow_small_or_imprecise_dtypes=True).then_inc(slot_ids, 1)
            attention(1, 8)
            for k in range(AHEAD):
                pool.wait_ge(hi_ready, k + 1)
                g.tensor_tensor(piece(w_lo, k), raw_piece(k), piece(w_hi, k).bitcast(f32), ALU.subtract).then_inc(lo_ready, 1)
            for n in range(4 * E1):
                if n % 4 == 0:
                    pool.wait_ge(share_ready[n // 4 % 2], n // 8 + 1)
                pool.wait_ge(silu_ready, n + 1)
                if n >= NG:
                    pool.wait_ge(act_ready, n - NG + 1)
                g.tensor_tensor(gate_share[n % NG], gate_out[n % NG], share[:, n // 4, :], ALU.mult).then_inc(gshare_ready, 1)

        @block.scalar
        def _(act):
            s = nc.scalar
            act.wait_ge(ld_first, 48)
            act.wait_ge(angle_ready, 1)
            s.activation(sincos, angles, ACT.Sin).then_inc(sincos_ready, 1)
            act.wait_ge(pads_set, 2)
            for c in range(3):
                act.wait_ge(conv_mm, c + 1)
                if c < 2:
                    s.activation(h1[:, 8 * c:8 * c + 8, :].rearrange("p g b -> p (g b)"), bank[c][:, :], ACT.Gelu,
                                 bias=vec[:, CB1:CB1 + 1]).then_inc(conv_out, 1)
                else:
                    s.activation(h1[:, 16:23, :].rearrange("p g b -> p (g b)"), bank[2][:, 0:7 * B], ACT.Gelu,
                                 bias=vec[:, CB1:CB1 + 1]).then_inc(conv_out, 1)
                    last = (POS1 - 4 * (G1 - 1)) * C1
                    s.activation(h1[0:last, 23, :], bank[2][0:last, 7 * B:8 * B], ACT.Gelu,
                                 bias=vec[0:last, CB1:CB1 + 1]).then_inc(conv_out, 1)
            for c in range(2):
                act.wait_ge(conv_mm, 4 + c)
                s.activation(h2[:, 6 * c:6 * c + 6, :].rearrange("p m b -> p (m b)"), bank[3 + c][:, 0:6 * B], ACT.Gelu,
                             bias=vec[:, CB2:CB2 + 1]).then_inc(conv_out, 1)
            for n, (dst, cb, banks) in enumerate(((h3, CB3, (5, 6)), (h4, CB4, (7, 0)), (h5, CB5, (1, 2)))):
                for r in range(2):
                    act.wait_ge(conv_mm, 6 + 2 * n + r)
                    s.activation(dst[:, r, :], bank[banks[r]][:, 0:N], ACT.Gelu,
                                 bias=vec[:, cb + r:cb + r + 1]).then_inc(conv_out, 1)

            def squares_of(i):
                if i == 0:
                    act.wait_ge(conv_out, 12)
                    act.wait_ge(pads_set, 4)
                    s.activation(resid_v[:, :, 0:N], h5, ACT.Square).then_inc(squares_ready, 1)
                act.wait_ge(centred_ready, i + 1)
                s.activation(squares_v[:, :, 0:N], normed_v[:, :, 0:N], ACT.Square).then_inc(squares_ready, 1)

            def root(i):
                act.wait_ge(var_ready, i + 1)
                s.activation(small[:, 8:14], small[:, 0:6], ACT.Sqrt).then_inc(std_ready, 1)

            def row_out(row):
                act.wait_ge(rstd_row_mm, row)
                s.activation(rstd_row, bank[6][:, 0:N], ACT.Copy).then_inc(row_ready, 1)

            def attention(l):
                squares_of((0, 2)[l])
                w = 32 if l == 0 else 8
                for i in range(QKV_TILES[l]):
                    act.wait_ge(qkv_mm[l], i + 1)
                    s.activation(qkv_dst(l, i), bank[i % QKV_BANKS][:, 0:N], ACT.Copy).then_inc(qkv_out[l], 1)
                    if i == 1:
                        root((0, 2)[l])
                    if i == 2:
                        row_out(l + 1)
                    if i == 3:
                        act.wait_ge(lane_rstd_mm[l], 1)
                        s.activation(lane_rstd[l], bank[5][:, 0:T * w], ACT.Copy).then_inc(lane_rstd_ready[l], 1)
                act.wait_ge(shifted_ready[l], T)
                n = 480 if l == 0 else 120
                s.activation(score[l][:, 0:n], score[l][:, 0:n], ACT.Exp, scale=SCALE / 256).then_inc(exp_ready[l], 1)
                if l == 1:
                    act.wait_ge(ff1_mm, 6)
                s.activation(lane_to[:, :].rearrange("p (l d) -> p l d", d=HD), ident.unsqueeze(2).to_broadcast([P, P, HD]),
                             ACT.Copy).then_inc(lane_ready, 1)
                for d in range(T):
                    act.wait_ge(prob_ready[l], d + 1)
                    at = slice(OFF[d] * w, (OFF[d] + T - d) * w)
                    s.activation(prob_hi[:, at], score[l][:, at], ACT.Copy).then_inc(prob_hi_ready[l], 1)

            def router(l, n):
                act.wait_ge(lsub_ready[l], 1)
                for j in range(NT):
                    s.activation(small[:, 100 + j * n:100 + j * n + n], small[:, 40 + j * n:40 + j * n + n], ACT.Exp,
                                 scale=small[:, 16 + j:17 + j]).then_inc(lexp_ready[l], 1)

            attention(0)
            squares_of(1)
            root(1)
            act.wait_ge(rstd_ready, 2)
            act.wait_ge(xtok_mm, 1)
            for j in range(NT):
                s.activation(x_tok[:, j, :], bank[1 + j // 2][:, (j % 2) * D:(j % 2) * D + D], ACT.Copy,
                             scale=small[:, 16 + j:17 + j]).then_inc(xtok_ready, 1)
            router(0, E0)
            act.wait_ge(xslot_mm, 1)
            s.activation(x_slot[:, 0, FIRST], bank[4][:, FIRST], ACT.Copy).then_inc(xslot_ready, 1)
            for e4 in range(E0 // 4):
                if e4 >= 2:
                    act.wait_ge(innert_mm, 2 * (e4 - 1))
                for c in range(2):
                    act.wait_ge(ff1_mm, 2 * e4 + c + 1)
                    s.activation(inner[e4 % 2][:, 512 * c:512 * c + 512], bank[2 * (e4 % 2) + c][:, :],
                                 ACT.Gelu_apprx_tanh).then_inc(inner_ready, 1)
                if e4 == 0:
                    act.wait_ge(xslot_mm, 3)
                    s.activation(x_slot[:, 0, REST], bank[6][:, REST], ACT.Copy).then_inc(xslot_ready, 1)
                    act.wait_ge(row_mm, 2)
                    s.activation(weight_row, bank[5][:, 0:N], ACT.Copy).then_inc(wrow_ready, 1)
                if e4 >= 1:
                    act.wait_ge(ff2_mm, e4)
                    s.activation(y_slot[:, e4 - 1, :], bank[6 + (e4 - 1) % 2][:, 0:D], ACT.Copy).then_inc(yslot_ready, 1)
            act.wait_ge(ff2_mm, 4)
            s.activation(y_slot[:, 3, :], bank[7][:, 0:D], ACT.Copy).then_inc(yslot_ready, 1)
            attention(1)

            def high_part(k):
                if k % 4 == 0:
                    act.wait_ge(ld_exp1[k // 4 % 4], 16 * (k // 16 + 1))
                if k >= PIECES:
                    act.wait_ge(down_mm, k - PIECES + 1)
                s.activation(piece(w_hi, k), raw_piece(k), ACT.Copy).then_inc(hi_ready, 1)

            act.wait_ge(ff2_mm, 4)
            for k in range(AHEAD):
                high_part(k)
            squares_of(3)
            root(3)
            row_out(3)
            for r in range(2):
                act.wait_ge(xfull_ready, r + 1)
                s.activation(x_hi[:, r * N:(r + 1) * N], normed_v[:, r, 0:N], ACT.Copy).then_inc(xhi_ready, 1)
            router(1, E1)

            def silu(n):
                act.wait_ge(gate_mm, n + 1)
                if n >= NG:
                    act.wait_ge(gshare_ready, n - NG + 1)
                s.activation(gate_out[n % NG], bank[GATE_UP[n % 3][0]][:, 0:N], ACT.Silu).then_inc(silu_ready, 1)

            def high_act(n):
                act.wait_ge(act_ready, n + 1)
                if n >= NG:
                    act.wait_ge(down_mm, n - NG + 1)
                s.activation(act_hi[:, n % NG * N:(n % NG + 1) * N], act_in[n % NG], ACT.Copy).then_inc(acthi_ready, 1)
            silu(0)
            act.wait_ge(combt_mm, 1)
            s.activation(prob_hi[0:E1, 0:N], bank[7][0:E1, 0:N], ACT.Copy).then_inc(comb_hi_ready, 1)
            for e in range(0, E1, 2):
                act.wait_ge(share_mm, e + 1)
                s.activation(share[:, e, :], bank[SHARE_BANK[e % 4]][:, 0:N], ACT.Copy).then_inc(share_ready[0], 1)
            for n in range(4 * E1):
                if n + 1 < 4 * E1:
                    silu(n + 1)
                if n + AHEAD < 4 * E1:
                    high_part(n + AHEAD)
                high_act(n)

        @block.vector
        def _(dve):
            v = nc.vector
            steps = [0]

            def then(ins):
                steps[0] += 1
                ins.then_inc(dve_step, 1)
                dve.wait_ge(dve_step, steps[0])

            v.memset(windows[32:64, :], 0.0).then_inc(rows_cleared, 1)
            dve.wait_ge(ld_first, 48)
            dve.wait_ge(ld_const, 16)
            angle, turns, over = (carve(small, 16 * i, 2, T) for i in range(2, 5))
            PI = 3.1415925
            v.tensor_scalar(angle[:, 0, :], const[:, K_T:K_T + T], vec[:, CFR:CFR + 1], None, ALU.mult)
            then(v.tensor_scalar(angle[:, 1, :], const[:, K_T:K_T + T], vec[:, CFR:CFR + 1], None, ALU.mult))
            then(v.tensor_scalar(turns, angle, 1 / (2 * math.pi), ROUND, ALU.mult, ALU.add))
            then(v.tensor_scalar(turns, turns, -ROUND, None, ALU.add))
            then(v.scalar_tensor_tensor(out=angle, in0=turns, scalar=-TWO_PI_HI, in1=angle, op0=ALU.mult, op1=ALU.add))
            then(v.scalar_tensor_tensor(out=angle, in0=turns, scalar=-TWO_PI_LO, in1=angle, op0=ALU.mult, op1=ALU.add))
            then(v.tensor_scalar(angle[:, 1, :], angle[:, 1, :], math.pi / 2, None, ALU.add))
            then(v.tensor_scalar(over, angle, math.pi, -2 * math.pi, ALU.is_gt, ALU.mult))
            then(v.tensor_tensor(angle, angle, over, ALU.add))
            v.tensor_scalar(angles, angle, PI, -PI, ALU.min, ALU.max).then_inc(angle_ready, 1)
            dve.wait_ge(iotas, 2)
            for j in range(NT):
                then(v.tensor_scalar(before[:, j * NP:(j + 1) * NP], key_row[:, :], const[:, K_KEY + j:K_KEY + j + 1], None,
                                     ALU.is_ge))

            dve.wait_ge(sincos_ready, 1)
            for r in range(2):
                wr = vec[:, CNW + r:CNW + r + 1]
                v.tensor_scalar(cos_w[:, r, :], sincos[:, 1, :], wr, None, ALU.mult)
                last = v.tensor_scalar(sin_w[:, r, :], sincos[:, 0, :], wr, (-1.0, 1.0)[r], ALU.mult, ALU.mult)
            then(last)

            def by_time(x):
                return x.unsqueeze(2).to_broadcast([P, T, B])
            h5t = h5.rearrange("p r (t b) -> p r t b", b=B)
            tt = turned.rearrange("p r (t b) -> p r t b", b=B)
            ct = crossed.rearrange("p r (t b) -> p r t b", b=B)
            for r in range(2):
                dve.wait_ge(conv_out, 11 + r)
                v.tensor_tensor(tt[:, r], h5t[:, r], by_time(cos_w[:, r, :]), ALU.mult)
                last = v.tensor_tensor(ct[:, 1 - r], h5t[:, r], by_time(sin_w[:, 1 - r, :]), ALU.mult)
            then(last)
            v.tensor_tensor(turned, turned, crossed, ALU.add).then_inc(rope_done, 1)

            def centre(i, src):
                dve.wait_ge(mean_mm, i + 1)
                mean = bank[7][:, 0:N].unsqueeze(1).to_broadcast([P, 2, N])
                v.tensor_tensor(normed_v[:, :, 0:N], src, mean, ALU.subtract).then_inc(centred_ready, 1)

            def stats(i):
                dve.wait_ge(sums_mm, i + 1)
                if i == 0:
                    then(v.tensor_scalar(small[:, 3:6], bank[7][:, 3:6], RMS_EPS, None, ALU.add))
                    v.scalar_tensor_tensor(out=small[:, 0:3], in0=small[:, 3:6], scalar=LN_EPS, in1=bank[7][:, 0:3],
                                           op0=ALU.mult, op1=ALU.add).then_inc(var_ready, 1)
                else:
                    v.tensor_scalar(small[:, 0:3], bank[7][:, 0:3], LN_EPS, None, ALU.add).then_inc(var_ready, 1)

            def inverse_root(i):
                dve.wait_ge(std_ready, i + 1)
                v.reciprocal(small[:, 16:22], small[:, 8:14]).then_inc(rstd_ready, 1)

            centre(0, turned)
            stats(0)
            inverse_root(0)
            dve.wait_ge(rms_row_mm, 1)
            then(v.tensor_tensor(resid_v[:, :, 0:N], turned, bank[7][:, 0:N].unsqueeze(1).to_broadcast([P, 2, N]), ALU.mult))

            def attention(l):
                sets = SETS if l == 0 else 1
                w = 32 if l == 0 else 8
                n = PAIRS * w
                for r in range(2):
                    dve.wait_ge(qkv_out[l], (r + 1) * (1 + sets))
                    for d in range(T):
                        m = r * T + d
                        cols = (T - d) * B
                        if m >= PRODS:
                            dve.wait_ge(score_mm[l], m - PRODS + 1)
                        v.tensor_tensor(prods[l][m % PRODS][:, 0:sets, 0:cols], q[l][:, r, 0:sets, d * B:N],
                                        k[l][:, r, 0:cols].unsqueeze(1).to_broadcast([P, sets, cols]), ALU.mult)\
                            .then_inc(prod_ready[l], 1)
                s_ps = bank[6]
                blk = [slice(OFF[d] * w, (OFF[d] + T - d) * w) for d in range(T)]
                late = [slice(d * w, T * w) for d in range(T)]
                dve.wait_ge(factor_ready[l], T)
                dve.wait_ge(score_mm[l], 2 * T)
                then(v.tensor_tensor(score[l][:, 0:n], s_ps[:, 0:n], score[l][:, 0:n], ALU.mult))
                then(v.tensor_copy(peak[l][:, late[0]], score[l][:, blk[0]]))
                for d in range(1, T):
                    then(v.tensor_tensor(peak[l][:, late[d]], score[l][:, blk[d]], peak[l][:, late[d]], ALU.max))
                for d in range(T):
                    v.tensor_tensor(score[l][:, blk[d]], score[l][:, blk[d]], peak[l][:, late[d]], ALU.subtract)\
                        .then_inc(shifted_ready[l], 1)
                dve.wait_ge(exp_ready[l], 1)
                then(v.tensor_copy(total[l][:, late[0]], score[l][:, blk[0]]))
                for d in range(1, T):
                    then(v.tensor_tensor(total[l][:, late[d]], total[l][:, late[d]], score[l][:, blk[d]], ALU.add))
                then(v.reciprocal(inv[l][:, 0:T * w], total[l][:, 0:T * w]))
                for d in range(T):
                    v.tensor_tensor(score[l][:, blk[d]], score[l][:, blk[d]], inv[l][:, late[d]], ALU.mult).then_inc(prob_ready[l], 1)
                dve.wait_ge(prob_hi_ready[l], T)
                v.tensor_tensor(prob_lo[:, 0:n], score[l][:, 0:n], prob_hi[:, 0:n].bitcast(f32), ALU.subtract).then_inc(prob_lo_ready[l], 1)
                dve.wait_ge(vx_ready[l], T)
                dve.wait_ge(score_mm[l], 2 * T)
                def weigh(c):
                    dve.wait_ge(spread_mm[l], c + 1)
                    if l == 0:
                        r, (st, half_b) = c // 8, divmod(c % 8, 2)
                        dst = weighted[l][r][:, (c % 8) * n:(c % 8 + 1) * n].rearrange("p (s b) -> p s b", b=w)
                        src = bank[c % 4][:, 0:n].rearrange("p (s b) -> p s b", b=w)
                        val = vx[l][:, r, :, half_b * w:(half_b + 1) * w]
                    else:
                        r, quad = divmod(c, 2)
                        dst = weighted[l][r][:, quad * 4 * n:(quad + 1) * 4 * n].rearrange("p (o s b) -> p o s b", o=4, b=w)
                        src = bank[c % 4][:, 0:4 * n].rearrange("p (o s b) -> p o s b", o=4, b=w)
                        val = vx[l][:, r, :, quad * 32:(quad + 1) * 32].rearrange("p s (o b) -> p o s b", b=w)
                    v.tensor_tensor(dst, src, val, ALU.mult).then_inc(weighted_ready[l], 1)

                steps_of_part = (4, 2)[l]
                for c in range(steps_of_part * PARTS[l]):
                    weigh(c)
                wt = weighted[l][1][:, 0:8 * n].rearrange("p (c s) -> p c s", c=8)
                for part in range(PARTS[l]):
                    first = steps_of_part * (PARTS[l] + part)
                    for c in range(first, first + steps_of_part):
                        weigh(c)
                    dve.wait_ge(weighted_ready[l], first + steps_of_part)
                    m = 8 // PARTS[l]
                    wp = wt[:, part * m:(part + 1) * m, :]
                    for d in range(1, T):
                        v.tensor_tensor(wp[:, :, late[d]], wp[:, :, late[d]], wp[:, :, blk[d]], ALU.add).then_inc(mixed_dve[l], 1)
                        dve.wait_ge(mixed_dve[l], (T - 1) * part + d)
                for r in range(2):
                    dve.wait_ge(proj_mm[l], r + 1)
                    v.tensor_tensor(resid_v[:, r, 0:N], bank[4 + r][:, 0:N], resid_v[:, r, 0:N], ALU.add)\
                        .then_inc(resid_ready, 1)

            attention(0)
            centre(1, resid_v[:, :, 0:N])

            def over_experts(x, n):
                return x.unsqueeze(2).to_broadcast([P, NT, n])

            def first_max(src, top, hit, which, rev, n):
                then(v.tensor_reduce(out=top, in_=src, axis=AX.X, op=ALU.max))
                then(v.tensor_tensor(hit, src, over_experts(top, n), ALU.is_ge))
                then(v.tensor_tensor(hit, hit, rev.unsqueeze(1).to_broadcast([P, NT, n]), ALU.mult))
                then(v.tensor_reduce(out=which, in_=hit, axis=AX.X, op=ALU.max))
                then(v.tensor_tensor(hit, hit, over_experts(which, n), ALU.is_equal))

            top, which = carve(small, 24, NT), carve(small, 27, NT)
            lsub, hit, lexp = carve(small, 40, NT, E0), carve(small, 160, NT, E0), carve(small, 100, NT, E0)
            slotval, kept = carve(small, 220, NT, E0), carve(small, 280, NT, E0)
            hit16 = carve(small, 340, NT, E0)
            pos, gate_w, expsum = carve(small, 30, NT), carve(small, 33, NT), carve(small, 36, NT)
            onehot = hit16.bitcast(bf16)[:, :, 0:E0]
            logits = bank[0][:, 0:NT * E0].rearrange("p (k e) -> p k e", e=E0)
            dve.wait_ge(logit_mm[0], 1)
            then(v.tensor_reduce(out=top, in_=logits, axis=AX.X, op=ALU.max))
            v.tensor_tensor(lsub, logits, over_experts(top, E0), ALU.subtract).then_inc(lsub_ready[0], 1)
            dve.wait_ge(lsub_ready[0], 1)
            then(v.scalar_tensor_tensor(out=hit, in0=lsub, scalar=0.0, in1=const[:, K_REV16:K_REV16 + E0].unsqueeze(1)
                                        .to_broadcast([P, NT, E0]), op0=ALU.is_ge, op1=ALU.mult))
            then(v.tensor_reduce(out=which, in_=hit, axis=AX.X, op=ALU.max))
            then(v.tensor_tensor(hit, hit, over_experts(which, E0), ALU.is_equal))
            v.tensor_copy(onehot, hit).then_inc(onehot_ready, 1)
            stats(1)
            inverse_root(1)
            rank = bank[3][:, 0:NT * E0].rearrange("p (k e) -> p k e", e=E0)
            dve.wait_ge(rank_mm, 1)
            then(v.scalar_tensor_tensor(out=kept, in0=rank, scalar=float(CAP), in1=hit, op0=ALU.is_le, op1=ALU.mult))
            then(v.tensor_tensor(slotval, rank, const[:, K_E32:K_E32 + E0].unsqueeze(1).to_broadcast([P, NT, E0]), ALU.add))
            then(v.tensor_tensor(slotval, slotval, kept, ALU.mult))
            v.tensor_reduce(out=pos, in_=slotval, axis=AX.X, op=ALU.add).then_inc(pos_ready, 1)
            dve.wait_ge(pos_ready, 1)
            dve.wait_ge(slot_ids, 1)
            for cols in (FIRST, REST):
                for j in range(NT):
                    v.tensor_scalar(place[:, j, cols], slot_id[:, cols], pos[:, j:j + 1], None, ALU.is_equal).then_inc(place_ready, 1)
            dve.wait_ge(xslot_mm, 2)
            v.tensor_copy(x_slot[:, 1, FIRST], bank[5][:, FIRST]).then_inc(xslot_ready, 1)
            dve.wait_ge(lexp_ready[0], NT)
            then(v.tensor_reduce(out=expsum, in_=lexp, axis=AX.X, op=ALU.add))
            v.reciprocal(gate_w, expsum).then_inc(gatew_ready, 1)
            dve.wait_ge(xslot_mm, 4)
            v.tensor_copy(x_slot[:, 1, REST], bank[7][:, REST]).then_inc(xslot_ready, 1)
            dve.wait_ge(wrow_ready, 1)
            for j in range(4):
                v.scalar_tensor_tensor(out=back[:, j, :], in0=bank[4][:, 0:N], scalar=const[:, K_SLOT + j:K_SLOT + j + 1],
                                       in1=weight_row, op0=ALU.is_equal, op1=ALU.mult).then_inc(back_ready, 1)
            for e4 in range(E0 // 4):
                for c in range(2):
                    dve.wait_ge(innert_mm, 2 * e4 + c + 1)
                    if e4 >= 1:
                        dve.wait_ge(ff2_mm, e4)
                    v.tensor_copy(inner_t[:, 4 * c:4 * c + 4, :].rearrange("p k s -> p (k s)"), bank[4 + c][:, :])\
                        .then_inc(innert_ready, 1)
            for r in range(2):
                dve.wait_ge(combine_mm, r + 1)
                v.tensor_tensor(resid_v[:, r, 0:N], bank[r][:, 0:N], resid_v[:, r, 0:N], ALU.add).then_inc(resid_ready, 1)
            centre(2, resid_v[:, :, 0:N])
            stats(2)
            inverse_root(2)
            attention(1)
            centre(3, resid_v[:, :, 0:N])

            lsub, lexp = carve(small, 40, NT, E1), carve(small, 100, NT, E1)
            probs, masked = carve(small, 160, NT, E1), carve(small, 200, NT, E1)
            hit_a, hit_b = carve(small, 280, NT, E1), carve(small, 320, NT, E1)
            gscore, gscore2 = carve(small, 360, NT, 4), carve(small, 380, NT, 4)
            ghit_a, ghit_b = carve(small, 400, NT, 4), carve(small, 420, NT, 4)
            comb = carve(small, 440, NT, E1)
            rev8, rev4 = const[:, K_REV8:K_REV8 + E1], const[:, K_REV4:K_REV4 + 4]
            logits = bank[0][:, 0:NT * E1].rearrange("p (k e) -> p k e", e=E1)
            dve.wait_ge(logit_mm[1], 1)
            then(v.tensor_reduce(out=top, in_=logits, axis=AX.X, op=ALU.max))
            v.tensor_tensor(lsub, logits, over_experts(top, E1), ALU.subtract).then_inc(lsub_ready[1], 1)
            dve.wait_ge(lsub_ready[1], 1)
            then(v.scalar_tensor_tensor(out=hit_a, in0=lsub, scalar=0.0, in1=rev8.unsqueeze(1).to_broadcast([P, NT, E1]),
                                        op0=ALU.is_ge, op1=ALU.mult))
            stats(3)
            then(v.tensor_reduce(out=which, in_=hit_a, axis=AX.X, op=ALU.max))
            then(v.tensor_tensor(hit_a, hit_a, over_experts(which, E1), ALU.is_equal))
            inverse_root(3)
            pairs_of = hit_a.rearrange("p k (g j) -> p k g j", j=2)
            pair = lsub.rearrange("p k (g j) -> p k g j", j=2)
            v.tensor_tensor(ghit_a, pairs_of[:, :, :, 0], pairs_of[:, :, :, 1], ALU.max)
            then(v.tensor_tensor(gscore, pair[:, :, :, 0], pair[:, :, :, 1], ALU.max))
            then(v.scalar_tensor_tensor(out=gscore2, in0=ghit_a, scalar=-BIG, in1=gscore, op0=ALU.mult, op1=ALU.add))
            first_max(gscore2, top, ghit_b, which, rev4, 4)
            dve.wait_ge(row_ready, 3)
            for r in range(2):
                v.tensor_tensor(normed_v[:, r, 0:N], normed_v[:, r, 0:N], rstd_row, ALU.mult).then_inc(xfull_ready, 1)
            then(v.tensor_tensor(ghit_a, ghit_a, ghit_b, ALU.add))
            for r in range(2):
                dve.wait_ge(xhi_ready, r + 1)
                v.tensor_tensor(x_lo[:, r * N:(r + 1) * N], normed_v[:, r, 0:N], x_hi[:, r * N:(r + 1) * N].bitcast(f32), ALU.subtract)\
                    .then_inc(xlo_ready, 1)
            v.tensor_scalar(gscore, ghit_a, BIG, -BIG, ALU.mult, ALU.add)
            then(v.scalar_tensor_tensor(out=masked, in0=hit_a, scalar=-BIG, in1=lsub, op0=ALU.mult, op1=ALU.add))
            mp = masked.rearrange("p k (g j) -> p k g j", j=2)
            v.tensor_tensor(mp[:, :, :, 0], mp[:, :, :, 0], gscore, ALU.add)
            then(v.tensor_tensor(mp[:, :, :, 1], mp[:, :, :, 1], gscore, ALU.add))
            first_max(masked, top, hit_b, which, rev8, E1)
            then(v.tensor_tensor(hit_a, hit_a, hit_b, ALU.add))
            dve.wait_ge(lexp_ready[1], NT)
            then(v.tensor_tensor(probs, lexp, hit_a, ALU.mult))
            then(v.tensor_reduce(out=expsum, in_=probs, axis=AX.X, op=ALU.add))
            then(v.reciprocal(gate_w, expsum))
            v.tensor_tensor(comb, probs, over_experts(gate_w, E1), ALU.mult).then_inc(comb_ready, 1)

            dve.wait_ge(comb_hi_ready, 1)
            v.tensor_tensor(prob_lo[0:E1, 0:N], bank[7][0:E1, 0:N], prob_hi[0:E1, 0:N].bitcast(f32), ALU.subtract).then_inc(comb_lo_ready, 1)

            for e in range(1, E1, 2):
                dve.wait_ge(share_mm, e + 1)
                v.tensor_copy(share[:, e, :], bank[SHARE_BANK[e % 4]][:, 0:N]).then_inc(share_ready[1], 1)

            def low_act(n):
                dve.wait_ge(acthi_ready, n + 1)
                part = slice(n % NG * N, (n % NG + 1) * N)
                v.tensor_tensor(act_lo[:, part], act_in[n % NG], act_hi[:, part].bitcast(f32), ALU.subtract).then_inc(actlo_ready, 1)

            for n in range(4 * E1):
                dve.wait_ge(gshare_ready, n + 1)
                if n >= NG:
                    dve.wait_ge(actlo_ready, n - NG + 1)
                v.tensor_tensor(act_in[n % NG], bank[GATE_UP[n % 3][1]][:, 0:N], gate_share[n % NG], ALU.mult).then_inc(act_ready, 1)
                low_act(n)
                if 1 <= n <= 4 * E1 - AHEAD:
                    nxt = n + AHEAD - 1
                    dve.wait_ge(hi_ready, nxt + 1)
                    v.tensor_tensor(piece(w_lo, nxt), raw_piece(nxt), piece(w_hi, nxt).bitcast(f32), ALU.subtract).then_inc(lo_ready, 1)
            dve.wait_ge(down_mm, 4 * E1)
            for r in range(2):
                v.tensor_tensor(normed_v[:, r, 0:N], bank[6 + r][:, 0:N], resid_v[:, r, 0:N], ALU.add).then_inc(final_ready, 1)
            for j in range(NT):
                dve.wait_ge(final_mm, j + 1)
                v.tensor_copy(final_tok[:, j, :, :].rearrange("t p r -> t r p"),
                              bank[j][:, 0:D].rearrange("t (r p) -> t r p", r=2)).then_inc(tok_ready, 1)

        @block.tensor
        def _(pe):
            def mm(o, w, x, start, stop, **kw):
                return nc.tensor.matmul(o, w, x, start=start, stop=stop, **kw)

            idle = mean_w[:, :].bitcast(bf16)

            def keep_warm(n, into):
                for _ in range(n):
                    mm(bank[into].rearrange("p (j c) -> p j c", j=2), idle[:, 0:P],
                       idle.unsqueeze(1).to_broadcast([P, 2, 2 * P]), True, True)

            pe.wait_ge(pads_set, 1)
            keep_warm(WARM[0], 7)
            pe.wait_ge(ld_first, 48)
            pe.wait_ge(last_rows_cleared, 1)
            for c in range(3):
                mm(bank[c][:, :], w_conv12[:, 0:P], windows[:, 512 * c:512 * c + 512], True, True).then_inc(conv_mm, 1)
            keep_warm(WARM[1], 7)
            pe.wait_ge(pads_set, 2)
            w2 = carve(w_conv12, P, 3, P)
            odd = h1.rearrange("p (m j) b -> p m j b", j=2)
            for c in range(2):
                pe.wait_ge(conv_out, 2 + 2 * c)
                o = bank[3 + c][:, 0:6 * B].rearrange("p (m b) -> p m b", b=B)
                m0 = 6 * c
                mm(o, w2[:, 1, :], odd[:, m0:m0 + 6, 0, :], True, False)
                if c == 0:
                    mm(o[:, 1:6, :], w2[:, 0, :], odd[:, 0:5, 1, :], False, False)
                else:
                    mm(o, w2[:, 0, :], odd[:, m0 - 1:m0 + 5, 1, :], False, False)
                mm(o, w2[:, 2, :], odd[:, m0:m0 + 6, 1, :], False, True).then_inc(conv_mm, 1)
            keep_warm(WARM[2], 7)
            pe.wait_ge(ld_conv, 16)
            pe.wait_ge(conv_out, 6)
            for r in range(2):
                o = bank[5 + r][:, 0:N].rearrange("p (t b) -> p t b", b=B)
                jobs = []
                for odd_t in range(2):
                    for dd in (2, 3, 0, 1, 4) if not odd_t else range(5):
                        ts = [t for t in range(odd_t, T, 2) if 0 <= first_pair(t) + dd < M2]
                        jobs.append((odd_t, dd, ts))
                for n, (odd_t, dd, ts) in enumerate(jobs):
                    m0 = first_pair(ts[0]) + dd
                    last = m0 + T * (len(ts) - 1)
                    x = h2[:, m0:last + 1:T, :]
                    i = mm(o[:, ts[0]:ts[-1] + 1:2, :], w_conv3[:, 5 * odd_t + dd, r * P:(r + 1) * P], x,
                           n == 0, n == len(jobs) - 1, skip_group_check=True)
                i.then_inc(conv_mm, 1)
            for r in range(2):
                pe.wait_ge(conv_out, 7 + r)
                o = bank[(7, 0)[r]]
                mm(o[:, 0:N], w_conv4[:, 1, r, :], h3[:, r, :], True, False)
                mm(o[:, B:N], w_conv4[:, 0, r, :], h3[:, r, 0:N - B], False, False)
                mm(o[:, 0:N - B], w_conv4[:, 2, r, :], h3[:, r, B:N], False, True).then_inc(conv_mm, 1)
            for kk in range(2):
                pe.wait_ge(conv_out, 9 + kk)
                for r in range(2):
                    i = mm(bank[1 + r][:, 0:N], w_conv5[:, kk, r * P:(r + 1) * P], h4[:, kk, :], kk == 0, kk == 1)
                    if kk == 1:
                        i.then_inc(conv_mm, 1)

            def mean(i, src):
                for kk in range(2):
                    x = mm(bank[7][:, 0:N], mean_w[:, :], src[:, kk, 0:N], kk == 0, kk == 1)
                x.then_inc(mean_mm, 1)

            def sums(i):
                srcs = (squares_v,) if i else (squares_v, resid_v)
                pe.wait_ge(squares_ready, i + 2)
                for n, src in enumerate(srcs):
                    for j in range(NT):
                        for kk in range(2):
                            x = mm(bank[7][:, 3 * n + j:3 * n + j + 1], src[:, kk, j * P:(j + 1) * P], mean_w[:, 0:1], kk == 0, kk == 1)
                x.then_inc(sums_mm, 1)

            def spread_rows(dst, cols):
                for j in range(NT):
                    n = min(P, N - j * P)
                    x = mm(dst[:, j * P:j * P + n], cols[:, j:j + 1].to_broadcast([P, P]), ident[:, 0:n], True, True)
                return x

            def attention(l, w_qkv, ld_qkv, w_proj, ld_proj):
                sets = SETS if l == 0 else 1
                tiles = QKV_TILES[l]
                pe.wait_ge(centred_ready, 1 if l == 0 else 3)
                pe.wait_ge(ld_qkv, 16)
                s_bank = bank[6]
                w = 32 if l == 0 else 8

                def qkv_tile(i):
                    if i >= QKV_BANKS:
                        pe.wait_ge(qkv_out[l], i - QKV_BANKS + 1)
                    for kk in range(2):
                        x = mm(bank[i % QKV_BANKS][:, 0:N], w_qkv[:, kk, i, :], normed_v[:, kk, 0:N], kk == 0, kk == 1)
                    x.then_inc(qkv_mm[l], 1)

                def spread():
                    pe.wait_ge(rstd_ready, 1 if l == 0 else 3)
                    spread_rows(bank[6], small[:, 16:19]).then_inc(rstd_row_mm, 1)
                    if l == 0:
                        spread_rows(bank[7], small[:, 19:22]).then_inc(rms_row_mm, 1)

                def clips(gg, kap):
                    return slice((gg % 2) * 32, (gg % 2) * 32 + 32) if l == 0 else slice((2 * gg + kap) * 8, (2 * gg + kap) * 8 + 8)

                def lanes():
                    pe.wait_ge(row_ready, l + 1)
                    row = rstd_row.rearrange("p (t b) -> p t b", b=B)
                    for r in range(2):
                        for kap in range(2):
                            for gg in range(4):
                                x = mm(bank[5][32 * gg:32 * gg + 32, 0:T * w].rearrange("p (t b) -> p t b", b=w),
                                       lane_of[:, r, kap, :], row[:, :, clips(gg, kap)],
                                       r == 0 and kap == 0, r == 1 and kap == 1, tile_position=(0, 32 * gg))
                    x.then_inc(lane_rstd_mm[l], 1)

                def scores(r, d):
                    m = r * T + d
                    pe.wait_ge(row_ready, l + 1)
                    pe.wait_ge(prod_ready[l], m + 1)
                    p = prods[l][m % PRODS].rearrange("p s (t b) -> p s t b", b=B)
                    for kap in range(2):
                        for gg in range(4):
                            src = p[:, 2 * (gg // 2) + kap if l == 0 else 0, 0:T - d, clips(gg, kap)]
                            o = s_bank[32 * gg:32 * gg + 32, OFF[d] * w:(OFF[d] + T - d) * w]
                            x = mm(o.rearrange("p (s b) -> p s b", b=w), lane_of[:, r, kap, :], src,
                                   m == 0 and kap == 0, r == 1 and kap == 1, skip_group_check=True,
                                   tile_position=(0, 32 * gg))
                    x.then_inc(score_mm[l], 1)

                for kind, *at in PE_ORDER[l]:
                    {"warm": lambda n: keep_warm(n, 7), "t": qkv_tile, "s": scores, "spread": spread, "lanes": lanes, "sums": lambda: sums((0, 2)[l])}[kind](*at)
                keep_warm(WARM[5 + l], 7)
                pe.wait_ge(prob_hi_ready[l], T)
                pe.wait_ge(lane_ready, l + 1)
                n = PAIRS * w

                pe.wait_ge(qkv_out[l], tiles)

                def spread(c, part):
                    for o8 in range(1 if l == 0 else 4):
                        if l == 0:
                            r, (st, half_b) = c // 8, divmod(c % 8, 2)
                            gg, kap = 2 * (st // 2) + half_b, st % 2
                        else:
                            r, quad = divmod(c, 2)
                            gg, kap = divmod(4 * quad + o8, 2)
                        base = 32 * gg + 16 * kap + 8 * r
                        x = mm(bank[c % 4][:, o8 * n:(o8 + 1) * n], lane_to[:, HD * base:HD * base + P],
                               (prob_hi, prob_lo)[part][:, 0:n], part == 0 and o8 == 0, part == 1, skip_group_check=True)
                    return x
                early = (4, 1)[l]
                for c in range(early):
                    spread(c, 0)
                pe.wait_ge(prob_lo_ready[l], 1)
                for c in range(16 if l == 0 else 4):
                    if c >= 4:
                        pe.wait_ge(weighted_ready[l], c - 3)
                    if c >= early:
                        spread(c, 0)
                    spread(c, 1).then_inc(spread_mm[l], 1)
                pe.wait_ge(ld_proj, 16)
                for r in range(2):
                    for st in range(sets):
                        if st % (sets // PARTS[l]) == 0:
                            pe.wait_ge((mixed_pool, mixed_dve)[r][l], (T - 1) * (st * PARTS[l] // sets + 1))
                        for mo in range(2):
                            dst = bank[4 + mo]
                            if l == 0:
                                y = weighted[l][r].rearrange("p (s h c) -> p s h c", s=SETS, h=2)[:, st, :, 0:T * w]
                                y = y.rearrange("p h (t b) -> p t h b", b=w)
                                o = dst[:, 0:N].rearrange("p (t h b) -> p t h b", h=2, b=w)
                            else:
                                y = weighted[l][r].rearrange("p (h c) -> p h c", h=8)[:, :, 0:T * w]
                                y = y.rearrange("p h (t b) -> p t h b", b=w)
                                o = dst[:, 0:N].rearrange("p (t h b) -> p t h b", h=8, b=w)
                            x = mm(o, w_proj[:, r, st, mo * P:(mo + 1) * P], y, r == 0 and st == 0, r == 1 and st == sets - 1)
                            if r == 1 and st == sets - 1:
                                x.then_inc(proj_mm[l], 1)

            def logits(l, n, w):
                for j in range(NT):
                    for kk in range(2):
                        x = mm(bank[0][:, j * n:(j + 1) * n], normed_v[:, kk, j * P:(j + 1) * P], w[:, kk, :], kk == 0, kk == 1)
                x.then_inc(logit_mm[l], 1)

            pe.wait_ge(pads_set, 4)
            pe.wait_ge(ld_const, 16)
            keep_warm(WARM[3], 3)
            pe.wait_ge(rope_done, 1)
            mean(0, turned)
            keep_warm(WARM[4], 3)
            attention(0, carve(w_qkv0, 0, 2, 12, P), ld_qkv0, carve(w_proj0, 0, 2, SETS, D), ld_proj0)
            keep_warm(WARM[7], 3)
            pe.wait_ge(resid_ready, 2)
            mean(1, resid_v)
            keep_warm(WARM[8], 3)
            pe.wait_ge(centred_ready, 2)
            pe.wait_ge(ld_gates, 16)
            logits(0, E0, carve(w_gates, 0, 2, E0))
            for j in range(NT):
                for r in range(2):
                    x = nc.tensor.transpose(bank[1 + j // 2][:, (j % 2) * D + r * P:(j % 2) * D + (r + 1) * P],
                                            normed_v[:, r, j * P:(j + 1) * P], ident)
            x.then_inc(xtok_mm, 1)
            sums(1)
            keep_warm(WARM[9], 6)
            pe.wait_ge(onehot_ready, 1)
            onehot = carve(small, 340, NT, E0).bitcast(bf16)[:, :, 0:E0]
            for j in range(NT):
                for jj in range(NT):
                    x = mm(bank[3][:, j * E0:(j + 1) * E0], before[:, jj * NP + j * P:jj * NP + (j + 1) * P], onehot[:, jj, :],
                           jj == 0, jj == NT - 1)
            x.then_inc(rank_mm, 1)
            keep_warm(WARM[10], 6)
            pe.wait_ge(xtok_ready, NT)

            def dispatch(part):
                cols = (FIRST, REST)[part]
                pe.wait_ge(place_ready, NT * (part + 1))
                for r in range(2):
                    for j in range(NT):
                        x = mm(bank[4 + 2 * part + r][:, cols], x_tok[:, j, r * P:(r + 1) * P], place[:, j, cols], j == 0, j == NT - 1)
                    x.then_inc(xslot_mm, 1)
            dispatch(0)
            keep_warm(WARM[21], 7)

            def expert(e):
                return carve(expert_cols(e, 0), 0, 2, F0), carve(expert_cols(e, 1), 0, F0 // P, D)

            def up(e4):
                for j in range(4):
                    e = 4 * e4 + j
                    pe.wait_ge(ld_up[home(e)[0]], 16 * home(e)[1])
                if e4 >= 2:
                    pe.wait_ge(inner_ready, 2 * (e4 - 1))
                for c in range(2):
                    for kk in range(2):
                        for j in range(4):
                            e = 4 * e4 + j
                            x = mm(bank[2 * (e4 % 2) + c][32 * j:32 * j + 32, :], x_slot[:, kk, SLOT * e:SLOT * e + SLOT],
                                   expert(e)[0][:, kk, 512 * c:512 * c + 512], kk == 0, kk == 1, tile_position=(0, 32 * j))
                    x.then_inc(ff1_mm, 1)

            def down(e4):
                if e4 == 0:
                    pe.wait_ge(back_ready, 4)
                for c in range(2):
                    pe.wait_ge(inner_ready, 2 * e4 + c + 1)
                    if e4 >= 1:
                        pe.wait_ge(innert_ready, 2 * (e4 - 1) + c + 1)
                    for kk in range(4):
                        at = 512 * c + P * kk
                        x = nc.tensor.transpose(bank[4 + c][:, P * kk:P * kk + P], inner[e4 % 2][:, at:at + P], ident)
                    x.then_inc(innert_mm, 1)
                if e4 >= 2:
                    pe.wait_ge(yslot_ready, e4 - 1)
                for j in range(4):
                    e = 4 * e4 + j
                    pe.wait_ge(ld_down[home(e)[0]], 16 * home(e)[1])
                for kk in range(F0 // P):
                    if kk % 4 == 0:
                        pe.wait_ge(innert_ready, 2 * e4 + kk // 4 + 1)
                    if kk == 4 and e4 == 3:
                        for j in range(4):
                            pe.wait_ge(ld_down_b[j], 16)
                    for j in range(4):
                        x = mm(bank[6 + e4 % 2][32 * j:32 * j + 32, 0:D], inner_t[:, kk, 32 * j:32 * j + 32],
                               expert(4 * e4 + j)[1][:, kk, :], kk == 0, kk == F0 // P - 1, tile_position=(0, 32 * j))
                x.then_inc(ff2_mm, 1)

            pe.wait_ge(xslot_ready, 2)
            up(0)
            dispatch(1)
            pe.wait_ge(gatew_ready, 1)
            spread_rows(bank[4], small[:, 30:33]).then_inc(row_mm, 1)
            spread_rows(bank[5], small[:, 33:36]).then_inc(row_mm, 1)
            pe.wait_ge(xslot_ready, 4)
            up(1)
            down(0)
            up(2)
            down(1)
            down(2)
            up(3)
            pe.wait_ge(inner_ready, 6)
            for j in range(4):
                if j == 3:
                    down(3)
                pe.wait_ge(yslot_ready, j + 1)
                for r in range(2):
                    x = mm(bank[r][:, 0:N], y_slot[:, j, r * P:(r + 1) * P], back[:, j, :], j == 0, j == 3)
                    if j == 3:
                        x.then_inc(combine_mm, 1)
            keep_warm(WARM[11], 3)
            pe.wait_ge(resid_ready, 4)
            mean(2, resid_v)
            keep_warm(WARM[12], 3)
            attention(1, carve(w_qkv1, 0, 2, 6, P), ld_qkv1, carve(w_proj1, 0, 2, 1, D), ld_proj1)
            keep_warm(WARM[13], 3)
            pe.wait_ge(resid_ready, 6)
            mean(3, resid_v)
            keep_warm(WARM[14], 3)
            pe.wait_ge(centred_ready, 4)
            logits(1, E1, carve(w_gates, 2 * E0, 2, E1))
            sums(3)
            pe.wait_ge(rstd_ready, 4)
            spread_rows(bank[6], small[:, 16:19]).then_inc(rstd_row_mm, 1)
            keep_warm(WARM[15], 3)
            pe.wait_ge(xlo_ready, 2)

            def split_mm(o, w, x, start, stop):
                for n, (wp, xp) in enumerate(((w[0], x[0]), (w[0], x[1]), (w[1], x[0]))):
                    i = mm(o, wp, xp, start and n == 0, stop and n == 2)
                return i

            def gate_up(n):
                pe.wait_ge(lo_ready, n + 1)
                if n >= 3:
                    pe.wait_ge(act_ready, n - 2)
                w = [carve(x, n % PIECES * PIECE, 2, 2, P) for x in (w_hi, w_lo)]
                for kind in range(2):
                    for kk in range(2):
                        x = split_mm(bank[GATE_UP[n % 3][kind]][:, 0:N], [y[:, kk, kind, :] for y in w],
                                     [y[:, kk * N:(kk + 1) * N] for y in (x_hi, x_lo)], kk == 0, kk == 1)
                x.then_inc(gate_mm, 1)

            def down1(n):
                w = [carve(x, n % PIECES * PIECE + 4 * P, D) for x in (w_hi, w_lo)]
                pe.wait_ge(actlo_ready, n + 1)
                for r in range(2):
                    x = split_mm(bank[6 + r][:, 0:N], [y[:, r * P:(r + 1) * P] for y in w],
                                 [y[:, n % NG * N:(n % NG + 1) * N] for y in (act_hi, act_lo)], n == 0, n == 4 * E1 - 1)
                x.then_inc(down_mm, 1)

            gate_up(0)
            keep_warm(WARM[16], 6)
            pe.wait_ge(comb_ready, 1)
            comb = carve(small, 440, NT, E1)
            for j in range(NT):
                x = mm(bank[7][0:E1, j * P:(j + 1) * P], comb[:, j, :], ident, True, True)
            x.then_inc(combt_mm, 1)
            gate_up(1)
            keep_warm(WARM[17], 6)
            pe.wait_ge(comb_lo_ready, 1)
            for e in range(E1):
                if e >= 4:
                    pe.wait_ge(share_ready[e % 2], e // 2 - 1)
                for part in range(2):
                    x = mm(bank[SHARE_BANK[e % 4]][:, 0:N], lane_to[0:E1, HD * e:HD * e + 1].to_broadcast([E1, P]),
                           (prob_hi, prob_lo)[part][0:E1, 0:N], part == 0, part == 1)
                x.then_inc(share_mm, 1)
            pe.wait_ge(share_ready[0], E1 // 2)
            pe.wait_ge(share_ready[1], E1 // 2)
            gate_up(2)
            for n in range(4 * E1):
                if 1 <= n < 4 * E1 - 2:
                    gate_up(n + 2)
                down1(n)
            pe.wait_ge(final_ready, 2)
            for j in range(NT):
                for r in range(2):
                    x = nc.tensor.transpose(bank[j][:, r * P:(r + 1) * P], normed_v[:, r, j * P:(j + 1) * P], ident)
                x.then_inc(final_mm, 1)


def first_pair(t):
    return (5 * t - 4) // 2


def layouts(x, w1, b1, w2, b2, w3, b3, w4, b4, w5, b5, freqs, norm_w, attn0, proj0, gate0, up0, down0, attn1, proj1, gate1, w13, down1):
    f = np.float32
    perm = np.arange(D).reshape(P, 2).T
    arr = {}
    vec = np.zeros((P, NVEC), f)
    vec[:, CB1] = np.tile(b1, 4)
    vec[:, CB2] = np.tile(b2, 2)
    vec[:, CB3:CB3 + 2] = b3.reshape(2, P).T
    vec[:, CB4:CB4 + 2] = b4.reshape(2, P).T
    vec[:, CB5:CB5 + 2] = b5[perm].T
    vec[:, CNW:CNW + 2] = norm_w[perm].T
    vec[:, CFR] = np.tile(freqs, P // (HD // 2))
    arr["vec"] = vec
    pad = np.zeros((B, 32 * (G1 - 1) + TAPS), f)
    pad[:, 7:7 + x.shape[2]] = x[:, 0, :]
    arr["windows"] = np.stack([pad[:, i:i + 32 * (G1 - 1) + 1:32].T for i in range(TAPS)]).reshape(TAPS, G1 * B)
    c12 = np.zeros((P, 4 * P), f)
    for j in range(4):
        c12[8 * j:8 * j + 15, 32 * j:32 * j + 32] = w1[:, 0, :].T
    c2 = c12[:, P:].reshape(4, C1, 3, 2, C2)
    for j in range(4):
        if j >= 1:
            c2[j, :, 0, 0, :] = w2[:, :, j - 1].T
            c2[j, :, 1, 1, :] = w2[:, :, j - 1].T
        c2[j, :, 1, 0, :] = w2[:, :, j + 3].T
        c2[j, :, 2, 1, :] = w2[:, :, j + 3].T
    arr["w_conv12"] = c12
    c3 = np.zeros((2, C2, 2, 5, D), f)
    for par in range(2):
        for d in range(5):
            if 2 * d + par <= 8:
                c3[par, :, 0, d, :] = w3[:, :, 2 * d + par].T
            if 2 * d + par >= 1:
                c3[par, :, 1, d, :] = w3[:, :, 2 * d + par - 1].T
    c4 = np.zeros((P, 3, 2, P), f)
    for o in range(D):
        r, oc = divmod(o, P)
        c4[oc // 8 * 8:oc // 8 * 8 + 8, :, r, oc] = w4[o]
    c5 = w5[:, :, 0][perm].transpose(2, 0, 1).reshape(2, P, D).transpose(1, 0, 2)
    arr["w_conv345"] = np.concatenate([c3.reshape(P, -1), c4.reshape(P, -1), c5.reshape(P, -1)], axis=1)
    a0 = attn0.reshape(SETS + 2, 2, P, D)
    tiles = [a0[j, r] for r in range(2) for j in [SETS] + list(range(SETS))] + [a0[SETS + 1, r] for r in range(2)]
    arr["w_qkv0"] = np.stack(tiles)[:, :, perm].transpose(3, 2, 0, 1).reshape(P, -1)
    arr["w_proj0"] = proj0[perm].reshape(2, P, SETS, 2, P).transpose(4, 3, 2, 0, 1).reshape(P, -1)
    a1 = attn1.T.reshape(3, 2, P, D)
    tiles = [a1[j, r] for r in range(2) for j in (1, 0)] + [a1[2, r] for r in range(2)]
    arr["w_qkv1"] = np.stack(tiles)[:, :, perm].transpose(3, 2, 0, 1).reshape(P, -1)
    arr["w_proj1"] = proj1[:, perm].reshape(2, P, 2, P).transpose(1, 0, 2, 3).reshape(P, -1)
    arr["w_gates"] = np.concatenate([gate0[:, perm].transpose(2, 1, 0).reshape(P, -1), gate1[:, perm].transpose(2, 1, 0).reshape(P, -1)], axis=1)
    ups = up0[:, perm, :].transpose(0, 2, 1, 3).reshape(E0, P, -1)
    downs = down0[:, :, perm].reshape(E0, F0 // P, P, D).transpose(0, 2, 1, 3).reshape(E0, P, -1)
    arr["w_exp0"] = np.concatenate([ups, downs], axis=2)
    ups = w13[:, :, perm].transpose(0, 3, 2, 1).reshape(E1, P, -1)
    downs = down1[:, perm, :].transpose(0, 3, 1, 2).reshape(E1, F1 // P, P, D).transpose(0, 2, 1, 3).reshape(E1, P, -1)
    ups = ups.reshape(E1, P, 2, 2, F1 // P, P).transpose(0, 1, 4, 2, 3, 5).reshape(E1, P, F1 // P, -1)
    arr["w_exp1"] = np.concatenate([ups, downs.reshape(E1, P, F1 // P, D)], axis=3).reshape(E1, P, -1)
    const = np.zeros((P, NCONST), f)
    const[:, K_ID:K_ID + P] = np.eye(P)
    lanes = const[:, K_IND:K_IND + P].reshape(P, 2, 2, 32)
    for p in range(P):
        for r in range(2):
            for kap in range(2):
                lanes[p, r, kap, 16 * kap + 8 * r + p // HD] = 1
    const[:, K_REV16:K_REV16 + E0] = E0 - np.arange(E0)
    const[:, K_E32:K_E32 + E0] = SLOT * np.arange(E0)
    const[:, K_REV8:K_REV8 + E1] = E1 - np.arange(E1)
    const[:, K_REV4:K_REV4 + 4] = 4 - np.arange(4)
    const[:, K_SLOT:K_SLOT + 4] = 1 + np.arange(4 * P).reshape(4, P).T
    key = np.full(NP, 2 * FAR)
    key[:N] = (np.arange(B)[None, :] * T + np.arange(T)[:, None]).ravel()
    const[:, K_KEY:K_KEY + NT] = key.reshape(NT, P).T
    const[:, K_T:K_T + T] = np.arange(T)
    arr["const"] = const
    return {n: np.ascontiguousarray(v, dtype=f) for n, v in arr.items()}


def kernel(x, L0_tok_w1, L0_tok_b1, L0_tok_w2, L0_tok_b2, L0_tok_w3, L0_tok_b3, L0_tok_w4, L0_tok_b4, L0_tok_w5, L0_tok_b5,
           L0_tok_rope_freqs, L0_tok_norm_w, L0_attn_W_attn, L0_attn_W_proj, L0_ffn_gate_w, L0_ffn_w1, L0_ffn_w2,
           L1_attn_W_attn, L1_attn_W_proj, L1_ffn_gate_w, L1_ffn_w13_weight, L1_ffn_w2_weight):
    import concourse.bacc as bacc
    from concourse.bass_utils import run_bass_kernel_spmd

    arrays = layouts(*(np.asarray(v) for v in (
        x, L0_tok_w1, L0_tok_b1, L0_tok_w2, L0_tok_b2, L0_tok_w3, L0_tok_b3, L0_tok_w4, L0_tok_b4, L0_tok_w5, L0_tok_b5,
        L0_tok_rope_freqs, L0_tok_norm_w, L0_attn_W_attn, L0_attn_W_proj, L0_ffn_gate_w, L0_ffn_w1, L0_ffn_w2,
        L1_attn_W_attn, L1_attn_W_proj, L1_ffn_gate_w, L1_ffn_w13_weight, L1_ffn_w2_weight)))
    nc = bacc.Bacc("TRN2", target_bir_lowering=False, num_devices=1)
    aps = {n: nc.dram_tensor(f"in_{n}", v.shape, mybir.dt.from_np(v.dtype), kind="ExternalInput").ap() for n, v in arrays.items()}
    out = nc.dram_tensor("tokens_out", (B, T, D), mybir.dt.float32, kind="ExternalOutput").ap()
    audio_tower(nc, aps, out)
    r = run_bass_kernel_spmd(nc, [{f"in_{n}": v for n, v in arrays.items()}], core_ids=[0])
    return r.results[0]["tokens_out"]
```
